# Optimizing a Trainium2 kernel written in Bass

```python
import numpy as np
import jax
import jax.numpy as jnp

def _softmax(x, axis=-1):
    return jax.nn.softmax(x, axis=axis)

def _gelu(x):
    return jax.nn.gelu(x, approximate=True)

def _silu(x):
    return jax.nn.silu(x)

def _sigmoid(x):
    return jax.nn.sigmoid(x)

def _layernorm(x, axis=-1, eps=1e-05):
    m = jnp.mean(x, axis=axis, keepdims=True)
    v = jnp.var(x, axis=axis, keepdims=True)
    return (x - m) / jnp.sqrt(v + eps)

def _scatter_add(tgt, idx, src, axis=0):
    return tgt.at[idx].add(src)

def _segment_sum(src, seg, n):
    return jax.ops.segment_sum(src, seg, n)
kernel_name = 'mk_audio_tower_d1_tok_audfeat768_r4_9b4633'

def setup_inputs(seed: int=0):
    np.random.seed(seed)
    _w = jnp.asarray

    def _rec_inputs():
        import jax
        import jax.numpy as jnp
        _rk = jax.random.key(seed)
        x = 0.000106427 + 1.00001 * jax.random.normal(jax.random.fold_in(_rk, 1), (32, 125, 192), jnp.float32)
        return x
    x = _rec_inputs()

    def _L0_tok_setup():
        import jax, jax.numpy as jnp
        import numpy as np
        D_MODEL = 192
        SEGMENT_SIZE = 128
        DILATION_RATE = 2
        key = jax.random.key(seed)
        x = jax.random.normal(key, (4, 4096, D_MODEL), dtype=jnp.float32)
        return {'x': x}
    _L0_tok_all = _L0_tok_setup()
    _L0_tok_in = {k: v for k, v in _L0_tok_all.items() if k in ()}
    del _L0_tok_all

    def _L0_attn_setup():
        import jax, jax.numpy as jnp
        import numpy as np
        EPS = 1e-06

        def _ln(x, g, b):
            mu = x.mean(-1, keepdims=True)
            var = ((x - mu) ** 2).mean(-1, keepdims=True)
            return (x - mu) * jax.lax.rsqrt(var + EPS) * g + b

        def _ln_l2_grad(z, target, g, b):
            d = z.shape[-1]
            mu = z.mean(-1, keepdims=True)
            var = ((z - mu) ** 2).mean(-1, keepdims=True)
            std = jnp.sqrt(var + EPS)
            zh = (z - mu) / std
            go = zh * g + b - target
            gxh = go * g
            return (d * gxh - gxh.sum(-1, keepdims=True) - zh * (gxh * zh).sum(-1, keepdims=True)) / (d * std)

        def _forward(x, W_down, b_down, Wq, Wk, Wv, Wo, W1, b1, ttt_g, ttt_b, lr_w, lr_b, post_g, post_b, norm_g, norm_b, W_up, b_up):
            B, S, D = x.shape
            A = W_down.shape[1]
            H, hd, _ = W1.shape
            h = jax.nn.silu(x @ W_down + b_down)
            xq = (h @ Wq).reshape(B, S, H, hd)
            xk = (h @ Wk).reshape(B, S, H, hd)
            xv = (h @ Wv).reshape(B, S, H, hd)
            eta = jax.nn.sigmoid(h @ lr_w + lr_b) / hd
            W1_0 = jnp.broadcast_to(W1, (B, H, hd, hd))
            b1_0 = jnp.broadcast_to(b1, (B, H, 1, hd))
            xs = (xq.transpose(1, 0, 2, 3), xk.transpose(1, 0, 2, 3), xv.transpose(1, 0, 2, 3), eta.transpose(1, 0, 2))

            def step(carry, ins):
                W, bb = carry
                q, k, v, e = ins
                Z = jnp.einsum('bhd,bhde->bhe', k, W) + bb[:, :, 0, :]
                g = _ln_l2_grad(Z, v - k, ttt_g, ttt_b)
                e4 = e[:, :, None, None]
                Wn = W - e4 * (k[..., :, None] * g[..., None, :])
                bn = bb - e4 * g[:, :, None, :]
                Zq = jnp.einsum('bhd,bhde->bhe', q, Wn) + bn[:, :, 0, :]
                out = q + _ln(Zq, ttt_g, ttt_b)
                return ((Wn, bn), out)
            _, ys = jax.lax.scan(step, (W1_0, b1_0), xs)
            t = ys.transpose(1, 0, 2, 3).reshape(B, S, A)
            t = _ln(t, post_g, post_b) @ Wo
            out = _ln(t, norm_g, norm_b)
            return out @ W_up + b_up
        key = jax.random.key(seed)
        ks = jax.random.split(key, 12)
        B, S, D, A, H = (4, 256, 192, 192, 3)
        hd = A // H
        s = 0.02
        return {'x': jax.random.normal(ks[0], (B, S, D), jnp.float32), 'W_down': jax.random.normal(ks[1], (D, A), jnp.float32) * s, 'b_down': jnp.zeros((A,), jnp.float32), 'Wq': jax.random.normal(ks[2], (A, A), jnp.float32) * s, 'Wk': jax.random.normal(ks[3], (A, A), jnp.float32) * s, 'Wv': jax.random.normal(ks[4], (A, A), jnp.float32) * s, 'Wo': jax.random.normal(ks[5], (A, A), jnp.float32) * s, 'W1': jax.random.normal(ks[6], (H, hd, hd), jnp.float32) * s, 'b1': jnp.zeros((H, 1, hd), jnp.float32), 'ttt_g': jnp.ones((H, hd), jnp.float32), 'ttt_b': jnp.zeros((H, hd), jnp.float32), 'lr_w': jax.random.normal(ks[7], (A, H), jnp.float32) * s, 'lr_b': jnp.zeros((H,), jnp.float32), 'post_g': jnp.ones((A,), jnp.float32), 'post_b': jnp.zeros((A,), jnp.float32), 'norm_g': jnp.ones((A,), jnp.float32), 'norm_b': jnp.zeros((A,), jnp.float32), 'W_up': jax.random.normal(ks[8], (A, D), jnp.float32) * s, 'b_up': jnp.zeros((D,), jnp.float32)}
    _L0_attn_all = _L0_attn_setup()
    _L0_attn_in = {k: v for k, v in _L0_attn_all.items() if k in ('W_down', 'b_down', 'Wq', 'Wk', 'Wv', 'Wo', 'W1', 'b1', 'ttt_g', 'ttt_b', 'lr_w', 'lr_b', 'post_g', 'post_b', 'norm_g', 'norm_b', 'W_up', 'b_up')}
    del _L0_attn_all

    def _L0_ffn_setup():
        import jax, jax.numpy as jnp
        import numpy as np
        B, T, C, H, E, TOPK, DR = (2, 512, 192, 768, 8, 2, 24)

        def _normalize(v, axis=-1, eps=1e-12):
            return v / jnp.maximum(jnp.linalg.norm(v, axis=axis, keepdims=True), eps)
        key = jax.random.key(seed)
        ks = jax.random.split(key, 16)
        std = 0.02
        n = lambda k, shape, s=std: (s * jax.random.normal(k, shape)).astype(jnp.float32)
        emb = jax.random.normal(ks[3], (E, DR), dtype=jnp.float32)
        emb = emb / (jnp.linalg.norm(emb, axis=-1, keepdims=True) + 1e-08)
        return {'x': jax.random.normal(ks[0], (B, T, C), dtype=jnp.float32), 'router_w': n(ks[1], (E, C)), 'probe_w': n(ks[2], (DR, C)), 'router_emb': emb, 'fatigue': jnp.zeros((E,), jnp.float32), 'energy': jnp.ones((E,), jnp.float32), 'w_fast1': n(ks[4], (E, C, H)), 'w_slow1': n(ks[5], (E, C, H)), 'h_fast1': n(ks[6], (E, C, H), 0.005), 'm_gate1': jax.random.uniform(ks[7], (E,), dtype=jnp.float32), 'b1': jnp.zeros((E, H), jnp.float32), 'w_fast2': n(ks[8], (E, H, C)), 'w_slow2': n(ks[9], (E, H, C)), 'h_fast2': n(ks[10], (E, H, C), 0.005), 'm_gate2': jax.random.uniform(ks[11], (E,), dtype=jnp.float32), 'b2': jnp.zeros((E, C), jnp.float32)}
    _L0_ffn_all = _L0_ffn_setup()
    _L0_ffn_in = {k: v for k, v in _L0_ffn_all.items() if k in ('router_w', 'probe_w', 'router_emb', 'fatigue', 'energy', 'w_fast1', 'w_slow1', 'h_fast1', 'm_gate1', 'b1', 'w_fast2', 'w_slow2', 'h_fast2', 'm_gate2', 'b2')}
    del _L0_ffn_all
    return {'x': x, 'L0_attn_W_down': _L0_attn_in['W_down'], 'L0_attn_b_down': _L0_attn_in['b_down'], 'L0_attn_Wq': _L0_attn_in['Wq'], 'L0_attn_Wk': _L0_attn_in['Wk'], 'L0_attn_Wv': _L0_attn_in['Wv'], 'L0_attn_Wo': _L0_attn_in['Wo'], 'L0_attn_W1': _L0_attn_in['W1'], 'L0_attn_b1': _L0_attn_in['b1'], 'L0_attn_ttt_g': _L0_attn_in['ttt_g'], 'L0_attn_ttt_b': _L0_attn_in['ttt_b'], 'L0_attn_lr_w': _L0_attn_in['lr_w'], 'L0_attn_lr_b': _L0_attn_in['lr_b'], 'L0_attn_post_g': _L0_attn_in['post_g'], 'L0_attn_post_b': _L0_attn_in['post_b'], 'L0_attn_norm_g': _L0_attn_in['norm_g'], 'L0_attn_norm_b': _L0_attn_in['norm_b'], 'L0_attn_W_up': _L0_attn_in['W_up'], 'L0_attn_b_up': _L0_attn_in['b_up'], 'L0_ffn_router_w': _L0_ffn_in['router_w'], 'L0_ffn_probe_w': _L0_ffn_in['probe_w'], 'L0_ffn_router_emb': _L0_ffn_in['router_emb'], 'L0_ffn_fatigue': _L0_ffn_in['fatigue'], 'L0_ffn_energy': _L0_ffn_in['energy'], 'L0_ffn_w_fast1': _L0_ffn_in['w_fast1'], 'L0_ffn_w_slow1': _L0_ffn_in['w_slow1'], 'L0_ffn_h_fast1': _L0_ffn_in['h_fast1'], 'L0_ffn_m_gate1': _L0_ffn_in['m_gate1'], 'L0_ffn_b1': _L0_ffn_in['b1'], 'L0_ffn_w_fast2': _L0_ffn_in['w_fast2'], 'L0_ffn_w_slow2': _L0_ffn_in['w_slow2'], 'L0_ffn_h_fast2': _L0_ffn_in['h_fast2'], 'L0_ffn_m_gate2': _L0_ffn_in['m_gate2'], 'L0_ffn_b2': _L0_ffn_in['b2']}

def reference(x, L0_attn_W_down, L0_attn_b_down, L0_attn_Wq, L0_attn_Wk, L0_attn_Wv, L0_attn_Wo, L0_attn_W1, L0_attn_b1, L0_attn_ttt_g, L0_attn_ttt_b, L0_attn_lr_w, L0_attn_lr_b, L0_attn_post_g, L0_attn_post_b, L0_attn_norm_g, L0_attn_norm_b, L0_attn_W_up, L0_attn_b_up, L0_ffn_router_w, L0_ffn_probe_w, L0_ffn_router_emb, L0_ffn_fatigue, L0_ffn_energy, L0_ffn_w_fast1, L0_ffn_w_slow1, L0_ffn_h_fast1, L0_ffn_m_gate1, L0_ffn_b1, L0_ffn_w_fast2, L0_ffn_w_slow2, L0_ffn_h_fast2, L0_ffn_m_gate2, L0_ffn_b2):
    import jax
    import jax.numpy as jnp

    def _L0_tok_ref(x):
        import jax, jax.numpy as jnp
        import numpy as np
        D_MODEL = 192
        SEGMENT_SIZE = 128
        DILATION_RATE = 2
        B, S, D = x.shape
        pad = -S % SEGMENT_SIZE
        if pad:
            x = jnp.pad(x, ((0, 0), (0, pad), (0, 0)))
        xs = x.reshape(B, -1, SEGMENT_SIZE, D)[:, :, ::DILATION_RATE, :]
        scale = 1.0 / jnp.sqrt(jnp.asarray(D, dtype=x.dtype))
        scores = jnp.einsum('bnqd,bnkd->bnqk', xs, xs) * scale
        attn = jax.nn.softmax(scores, axis=-1)
        out = jnp.einsum('bnqk,bnkd->bnqd', attn, xs)
        return out.reshape(B, -1, D)

    def _L0_attn_ref(x, W_down, b_down, Wq, Wk, Wv, Wo, W1, b1, ttt_g, ttt_b, lr_w, lr_b, post_g, post_b, norm_g, norm_b, W_up, b_up):
        import jax, jax.numpy as jnp
        import numpy as np
        EPS = 1e-06

        def _ln(x, g, b):
            mu = x.mean(-1, keepdims=True)
            var = ((x - mu) ** 2).mean(-1, keepdims=True)
            return (x - mu) * jax.lax.rsqrt(var + EPS) * g + b

        def _ln_l2_grad(z, target, g, b):
            d = z.shape[-1]
            mu = z.mean(-1, keepdims=True)
            var = ((z - mu) ** 2).mean(-1, keepdims=True)
            std = jnp.sqrt(var + EPS)
            zh = (z - mu) / std
            go = zh * g + b - target
            gxh = go * g
            return (d * gxh - gxh.sum(-1, keepdims=True) - zh * (gxh * zh).sum(-1, keepdims=True)) / (d * std)

        def _forward(x, W_down, b_down, Wq, Wk, Wv, Wo, W1, b1, ttt_g, ttt_b, lr_w, lr_b, post_g, post_b, norm_g, norm_b, W_up, b_up):
            B, S, D = x.shape
            A = W_down.shape[1]
            H, hd, _ = W1.shape
            h = jax.nn.silu(x @ W_down + b_down)
            xq = (h @ Wq).reshape(B, S, H, hd)
            xk = (h @ Wk).reshape(B, S, H, hd)
            xv = (h @ Wv).reshape(B, S, H, hd)
            eta = jax.nn.sigmoid(h @ lr_w + lr_b) / hd
            W1_0 = jnp.broadcast_to(W1, (B, H, hd, hd))
            b1_0 = jnp.broadcast_to(b1, (B, H, 1, hd))
            xs = (xq.transpose(1, 0, 2, 3), xk.transpose(1, 0, 2, 3), xv.transpose(1, 0, 2, 3), eta.transpose(1, 0, 2))

            def step(carry, ins):
                W, bb = carry
                q, k, v, e = ins
                Z = jnp.einsum('bhd,bhde->bhe', k, W) + bb[:, :, 0, :]
                g = _ln_l2_grad(Z, v - k, ttt_g, ttt_b)
                e4 = e[:, :, None, None]
                Wn = W - e4 * (k[..., :, None] * g[..., None, :])
                bn = bb - e4 * g[:, :, None, :]
                Zq = jnp.einsum('bhd,bhde->bhe', q, Wn) + bn[:, :, 0, :]
                out = q + _ln(Zq, ttt_g, ttt_b)
                return ((Wn, bn), out)
            _, ys = jax.lax.scan(step, (W1_0, b1_0), xs)
            t = ys.transpose(1, 0, 2, 3).reshape(B, S, A)
            t = _ln(t, post_g, post_b) @ Wo
            out = _ln(t, norm_g, norm_b)
            return out @ W_up + b_up
        return _forward(x, W_down, b_down, Wq, Wk, Wv, Wo, W1, b1, ttt_g, ttt_b, lr_w, lr_b, post_g, post_b, norm_g, norm_b, W_up, b_up)

    def _L0_ffn_ref(x, router_w, probe_w, router_emb, fatigue, energy, w_fast1, w_slow1, h_fast1, m_gate1, b1, w_fast2, w_slow2, h_fast2, m_gate2, b2):
        import jax, jax.numpy as jnp
        import numpy as np
        B, T, C, H, E, TOPK, DR = (2, 512, 192, 768, 8, 2, 24)

        def _normalize(v, axis=-1, eps=1e-12):
            return v / jnp.maximum(jnp.linalg.norm(v, axis=axis, keepdims=True), eps)
        Bd, Td, Cd = x.shape
        logits = jnp.einsum('btc,ec->bte', x, router_w)
        tok_proxy = x.mean(axis=-1, keepdims=True)
        router_gain = jnp.linalg.norm(router_emb, axis=-1)
        base_bias = 0.02 * tok_proxy
        gain_bias = 0.02 * tok_proxy * router_gain
        tok_unit = _normalize(jnp.einsum('btc,dc->btd', x, probe_w))
        align_bias = 0.02 * jnp.einsum('btd,ed->bte', tok_unit, _normalize(router_emb))
        logits = logits + base_bias + gain_bias + align_bias + 0.1 * energy - 0.1 * fatigue
        g, idx = jax.lax.top_k(logits, TOPK)
        gates = jax.nn.softmax(g, axis=-1)
        N = Bd * Td
        gates_full = jnp.zeros((N, E), x.dtype).at[jnp.arange(N)[:, None], idx.reshape(N, TOPK)].set(gates.reshape(N, TOPK))
        flat_x = x.reshape(N, Cd)

        def body(acc, p):
            wf1, ws1, hf1, mg1, bb1, wf2, ws2, hf2, mg2, bb2, ge = p
            W1 = wf1 + mg1 * ws1 + hf1
            h = jnp.square(jnp.maximum(flat_x @ W1 + bb1, 0.0))
            W2 = wf2 + mg2 * ws2 + hf2
            y = h @ W2 + bb2
            return (acc + ge[:, None] * y, None)
        out, _ = jax.lax.scan(body, jnp.zeros((N, Cd), x.dtype), (w_fast1, w_slow1, h_fast1, m_gate1, b1, w_fast2, w_slow2, h_fast2, m_gate2, b2, gates_full.T))
        return out.reshape(Bd, Td, Cd)
    h = _L0_tok_ref(x)
    h = h + _L0_attn_ref(_layernorm(h, axis=-1), L0_attn_W_down, L0_attn_b_down, L0_attn_Wq, L0_attn_Wk, L0_attn_Wv, L0_attn_Wo, L0_attn_W1, L0_attn_b1, L0_attn_ttt_g, L0_attn_ttt_b, L0_attn_lr_w, L0_attn_lr_b, L0_attn_post_g, L0_attn_post_b, L0_attn_norm_g, L0_attn_norm_b, L0_attn_W_up, L0_attn_b_up)
    h = h + _L0_ffn_ref(_layernorm(h, axis=-1), L0_ffn_router_w, L0_ffn_probe_w, L0_ffn_router_emb, L0_ffn_fatigue, L0_ffn_energy, L0_ffn_w_fast1, L0_ffn_w_slow1, L0_ffn_h_fast1, L0_ffn_m_gate1, L0_ffn_b1, L0_ffn_w_fast2, L0_ffn_w_slow2, L0_ffn_h_fast2, L0_ffn_m_gate2, L0_ffn_b2)
    return h

_drawn_inputs = setup_inputs


def setup_inputs(seed=0):
    import zlib

    import numpy as np

    out = dict(_drawn_inputs(seed))
    spreads = {'L0_attn_b_down': (0.0, 0.298),
     'L0_attn_b1': (0.0, 0.1),
     'L0_attn_ttt_g': (1.0, 0.2),
     'L0_attn_ttt_b': (0.0, 0.1),
     'L0_attn_lr_b': (0.0, 0.8),
     'L0_attn_post_g': (1.0, 0.2),
     'L0_attn_post_b': (0.0, 0.299),
     'L0_attn_norm_g': (1.0, 0.2),
     'L0_attn_norm_b': (0.0, 0.1),
     'L0_attn_b_up': (0.0, 0.1),
     'L0_ffn_fatigue': (0.0, 0.484),
     'L0_ffn_energy': (1.0, 0.578),
     'L0_ffn_b1': (0.0, 0.358),
     'L0_ffn_b2': (0.0, 0.1)}
    factors = {'L0_attn_lr_w': 8.0,
     'L0_ffn_probe_w': 5.151,
     'L0_ffn_router_emb': 5.266,
     'L0_ffn_h_fast1': 3.717,
     'L0_ffn_m_gate1': 2.744,
     'L0_ffn_h_fast2': 4.355,
     'L0_ffn_m_gate2': 3.986}
    for name, (base, spread) in spreads.items():
        noise = np.random.default_rng([zlib.crc32(name.encode()), seed]).standard_normal(out[name].shape)
        drawn = base * np.exp(spread * noise) if base else spread * noise
        out[name] = jnp.asarray(drawn.astype(out[name].dtype))
    for name, factor in factors.items():
        out[name] = (out[name] * factor).astype(out[name].dtype)
    return out
```

```python
from contextlib import ExitStack

import concourse.bass as bass
from concourse import mybir
from concourse.bass import IndirectOffsetOnAxis, ds

F32 = mybir.dt.float32
I32 = mybir.dt.int32
ALU = mybir.AluOpType
ACT = mybir.ActivationFunctionType
AX = mybir.AxisListType


def audio_tower_kernel(nc, io, out):
    B, T_IN, D = io["x"].shape
    SEG = 128
    S = SEG // 2
    H, HD = io["L0_attn_ttt_g"].shape
    E, _, HID = io["L0_ffn_w_fast1"].shape
    DR = io["L0_ffn_probe_w"].shape[0]
    P = 128
    NT = B * S // P
    R = B * H
    KB = D - P
    S_IN = (T_IN + 1) // 2
    BLK = 8
    NB = S // BLK
    G4 = 4
    NG = B * S // 512

    with ExitStack() as ctx:
        def sb(name, shape, dt=F32):
            return ctx.enter_context(nc.sbuf_tensor(name, shape, dt))

        def dram(name, shape, dt=F32):
            return nc.dram_tensor(name, shape, dt, kind="Internal").ap()

        sems = {}

        def sem(name):
            sems[name] = ctx.enter_context(nc.semaphore(name))
            return sems[name]

        arena = sb("arena", [P, 48128])
        at = 0

        def cut(n):
            nonlocal at
            at += n
            return arena[:, at - n:at]

        X = cut(NT * D)
        KQM = cut(R * 2 * S)
        GW = cut(R * HD)
        CC = cut(S * HD)
        MN = cut(S * 2 * BLK)
        W1A = cut(E * HID)
        W1B = cut(E * HID)
        W2 = cut(E * HID // P * D)
        xs = X.rearrange("p (i d) -> p i d", d=D)
        hmix = CC[:, 0:NT * D].rearrange("p (i d) -> p i d", d=D)
        xnTs = W2[:, 0:2 * NT * P].rearrange("p (i c t) -> p i c t", c=2, t=P)
        hTa = W2[:, 2 * NT * P:3 * NT * P]
        hTb = W2[0:KB + 1, 3 * NT * P:4 * NT * P]
        vk = W2[:, 0:NT * D].rearrange("p (i d) -> p i d", d=D)
        Wd = [GW[:, 0:D], GW[KB:P, D:2 * D]]
        Wkq = [GW[:, 384:768].rearrange("p (h c e) -> p h c e", h=H, c=2),
               GW[0:KB, 768:1152].rearrange("p (h c e) -> p h c e", h=H, c=2)]
        NQV = 2 * D + H
        Wqv = [GW[:, 1152:1152 + NQV], GW[0:KB + 1, 1152 + NQV:1152 + 2 * NQV]]
        qst = GW[:, 2048:2048 + 4 * D].rearrange("p (i d) -> p i d", d=D)
        xT_sb = [KQM[:, k * 2 * P:(k + 1) * 2 * P] for k in range(2)]
        Sm = [KQM[:, 512 + k * P:512 + (k + 1) * P] for k in range(2)]
        Ex = [KQM[:, 768 + k * P:768 + (k + 1) * P] for k in range(2)]
        ExT = [KQM[:, 1024 + k * P:1024 + (k + 1) * P] for k in range(2)]
        kqm = KQM.rearrange("p (r c t) -> p r c t", c=2, t=S)
        gw = GW.rearrange("p (r e) -> p r e", e=HD)

        far_sb = X[0:R, 0:32 * HD]
        ablk = [X[0:R, 2048 + 512 * k:2048 + 512 * (k + 1)] for k in range(2)]
        mn = MN[0:R, :].rearrange("p (s w) -> p s w", w=2 * BLK)
        cc = CC[0:R, :].rearrange("p (t e) -> p t e", e=HD)

        PRS = sb("PRS", [P, 2 * 14 * HD])
        PR = [PRS[:, 14 * HD * k:14 * HD * (k + 1)].rearrange("p (n e) -> p n e", e=HD) for k in range(2)]
        Gst = sb("Gst", [R, 4, HD])
        U = sb("U", [R, 2, HD])
        JK = sb("JK", [R, HD])
        PG = sb("PG", [R, HD])
        PC = sb("PC", [R, HD])
        Wv_ = sb("Wv_", [R, HD])
        M2 = sb("M2", [R, 2, HD])
        MY = sb("MY", [R, 2, 2 * BLK])
        sc = sb("sc", [R, 8])
        usum = sb("usum", [R, 2])
        UC = sb("UC", [R, HD])
        y1 = sb("y1", [R, 2])
        eta96 = sb("eta96", [R, S])
        b0r = sb("b0r", [R, HD])
        b0m = sb("b0m", [R, 2])
        g2r = sb("g2r", [R, HD])
        ident = sb("ident", [P, P])
        maskbd = KQM[:, 1280:1280 + P]
        negc = sb("negc", [S, S])
        mv = sb("mv", [P, NT, 2])
        st6 = sb("st6", [P, 2, 6])
        rowm = sb("rowm", [P, NT])
        negm = sb("negm", [P, NT])
        esum = sb("esum", [P, NT])
        rinv = sb("rinv", [P, NT])
        std0 = sb("std0", [P, NT])
        rstd0 = sb("rstd0", [P, NT])
        epsc = sb("epsc", [P, 3])
        bdc = sb("bdc", [P, 2])
        etal = sb("etal", [P, H, NT])
        etaT = CC[0:H * NT, NT * D:NT * D + P]
        w0h = sb("w0h", [HD, H, HD])
        w0m = sb("w0m", [HD, H])
        cmean = sb("cmean", [P, 3 * NT])
        gtok = sb("gtok", [P, D])
        btok = sb("btok", [P, D])

        def tiles(region, at, n, w=D):
            return [region[:, at + w * k:at + w * (k + 1)] for k in range(n)]

        ZS = tiles(X, 0, 5)
        TN = tiles(X, 960, 2)
        XN = tiles(X, 1344, 3)
        tT1 = tiles(X, 1920, 2, 2 * P)
        tT2 = tiles(X, 2432, 2, 2 * P)
        tT3 = tiles(MN, 0, 2, 2 * P)
        QR = tiles(MN, 512, 2)
        h2 = hmix
        Wo = [PRS[:, 0:D], PRS[KB:P, D:2 * D]]
        Wu = [PRS[:, 2 * D:3 * D], PRS[KB:P, 3 * D:4 * D]]
        SQ = PRS[:, 768:768 + D]
        bup = PRS[:, 960:960 + D]
        b0t = sb("b0t", [P, D])
        gcol = sb("gcol", [P, 2, 4])
        emb = sb("emb", [E, DR + 4])
        enT = sb("enT", [DR, E])
        rw = sb("rw", [E, D])
        pw = sb("pw", [DR, D])
        ones8 = sb("ones8", [E, P])
        dg8 = sb("dg8", [E, E])
        dgj = sb("dgj", [E, DR])
        Wr = sb("Wr", [P, 2, 2 * E + DR])
        NR = 2 * E + DR
        LG = CC[:, NT * D:NT * (D + NR)].rearrange("p (i n) -> p i n", n=NR)
        rz = sb("rz", [P, 3, 2 * H])
        mvs = sb("mvs", [P, 3, 3, 4])
        s6 = sb("s6", [P, 3, 6])

        w1a = W1A.rearrange("p (e n) -> p e n", n=HID)
        w1b = W1B.rearrange("p (e n) -> p e n", n=HID)
        KH = HID // P
        w2 = W2.rearrange("p (e k d) -> p e k d", k=KH, d=D)
        mg = sb("mg", [P, 2, E])
        ebias = sb("ebias", [P, E])
        TK = 2
        SLOTS = TK * B * S // P + E
        NI = NT * E
        ka = 0

        def kcut(n):
            nonlocal ka
            ka += n
            return KQM[:, ka - n:ka]

        def rv(n=E):
            return kcut(NT * n).rearrange("p (i e) -> p i e", e=n)
        sq24, Lg, al8, eqt, sct, oh1, oh2, oha, L2t, gsel = rv(DR), rv(), rv(), rv(), rv(), rv(), rv(), rv(), rv(), rv()
        P8 = rv()
        nrm = kcut(3 * NT).rearrange("p (k i) -> p k i", k=3)
        mx = kcut(2 * NT).rearrange("p (c i) -> p c i", c=2)
        cs = kcut(2 * NT).rearrange("p (c i) -> p c i", c=2)
        gt = kcut(4 * NT).rearrange("p (c i) -> p c i", c=4)
        pos = kcut(2 * NT)
        slot_ = kcut(2 * NT)
        row_ = kcut(2 * NT)
        ge = kcut(2 * NT * (SLOTS + 1)).rearrange("p (j k) -> p j k", k=SLOTS + 1)
        av = kcut(2 * NT * 2 * SLOTS).rearrange("p (j v k) -> p j v k", v=2, k=SLOTS)
        Bh = kcut(2 * NT * P).rearrange("p (j r) -> p j r", r=P)
        cnt = kcut(E)
        tlm = kcut(E * NT).rearrange("p (e k) -> p e k", k=NT)
        tl = kcut(E)
        bmt = kcut(E * E).rearrange("p (a b) -> p a b", b=E)
        bs = kcut(2 * E)
        exm = kcut(SLOTS * E).rearrange("p (k e) -> p k e", e=E)
        lst = kcut(4 * SLOTS).rearrange("p (v k) -> p v k", v=4)
        ga = 0

        def gcut(n):
            nonlocal ga
            ga += n
            return GW[:, ga - n:ga]
        w8 = gcut(E)
        irow = gcut(P)
        i41 = gcut(SLOTS + 1)
        tokid = gcut(NT)
        tri = gcut(P)
        ones = gcut(P)
        emask = gcut(E * E).rearrange("p (a b) -> p a b", b=E)
        trash = gcut(1)
        XG = [gcut(2 * P) for k in range(4)]
        xgT = gcut(2 * P)
        RL = gcut(HID)
        HT2 = gcut(HID)
        YO = [gcut(D) for k in range(4)]
        b2r = gcut(E * D)[0:1, :]
        idx = sb("idx", [P, SLOTS], I32)
        ex = sb("ex", [P, SLOTS], I32)
        gates = sb("gates", [P, SLOTS])
        fat = sb("fat", [P, E])

        bank = [ctx.enter_context(nc.psum_tensor(f"bank{k}", [P, 512], F32)) for k in range(8)]

        hmix_d = dram("hmix_d", (NT * P, D))
        q_d = dram("q_d", (NT * P, D))
        c_d = dram("c_d", (NT * P, D))
        km_d = dram("km_d", (S, R, S))
        xn_d = dram("xn_d", (NT * P + P, D))
        acc_d = dram("acc_d", (NT * P + P, D))

        consts = sem("consts")
        x_zero = sem("x_zero")
        x_in = [sem(f"x_in{c}") for c in range(4)]
        w_in = sem("w_in")
        xT_done = sem("xT_done")
        xT_out = sem("xT_out")
        s_done = sem("s_done")
        mx_out = sem("mx_out")
        negm_out = sem("negm_out")
        exp_out = sem("exp_out")
        rinv_out = sem("rinv_out")
        eT_done = sem("eT_done")
        eT_out = sem("eT_out")
        o_done = sem("o_done")
        h_out = sem("h_out")
        stat_a = sem("stat_a")
        stat_b = sem("stat_b")
        std_out = sem("std_out")
        rstd_out = sem("rstd_out")
        xn_out = sem("xn_out")
        hmix_st = sem("hmix_st")
        xnT_done = sem("xnT_done")
        xnT_out = sem("xnT_out")
        hd_done = sem("hd_done")
        hT_out = sem("hT_out")
        wprep = sem("wprep")
        kq_done = sem("kq_done")
        k_out = sem("k_out")
        q_out = sem("q_out")
        qv_done = sem("qv_done")
        qt_out = sem("qt_out")
        vk_out = sem("vk_out")
        q_st = [sem(f"q_st{k}") for k in range(4)]
        eta_done = sem("eta_done")
        eta_out = sem("eta_out")
        gram_done = sem("gram_done")
        km_out = sem("km_out")
        qm_out = sem("qm_out")
        c_chain = sem("c_chain")
        c_out = sem("c_out")
        rows_in = sem("rows_in")
        w0_out = sem("w0_out")
        b0_out = sem("b0_out")
        gw_rep = sem("gw_rep")
        km_st = sem("km_st")
        mn_zero = sem("mn_zero")
        mn_in = sem("mn_in")
        mne_out = sem("mne_out")
        eta_in = sem("eta_in")
        c_st = sem("c_st")
        c_in = sem("c_in")
        rt_in = sem("rt_in")
        rt_prep = sem("rt_prep")
        rt_sq = sem("rt_sq")
        rt_mm = sem("rt_mm")
        b0t_out = sem("b0t_out")
        post_w = sem("post_w")
        h_in = sem("h_in")
        hb_out = sem("hb_out")
        qr_in = [sem(f"qr_in{k}") for k in range(2)]
        qb_out = sem("qb_out")
        zq_done = sem("zq_done")
        zs_out = sem("zs_out")
        sq_out = sem("sq_out")
        sqz_out = sem("sqz_out")
        rz_out = sem("rz_out")
        zn_out = sem("zn_out")
        yg_out = sem("yg_out")
        y_out = sem("y_out")
        st_a = sem("st_a")
        st_y = sem("st_y")
        st_t = sem("st_t")
        st_h = sem("st_h")
        sd_y = sem("sd_y")
        sd_t = sem("sd_t")
        sd_h = sem("sd_h")
        ri_out = sem("ri_out")
        yn_out = sem("yn_out")
        tn_out = sem("tn_out")
        xn2_out = sem("xn2_out")
        t1_done = sem("t1_done")
        t2_done = sem("t2_done")
        t3_done = sem("t3_done")
        t1_out = sem("t1_out")
        t2_out = sem("t2_out")
        t3_out = sem("t3_out")
        wo_done = sem("wo_done")
        up_done = sem("up_done")
        h2_out = sem("h2_out")
        rt_done = sem("rt_done")
        lg_out = sem("lg_out")
        xn_st = [sem(f"xn_st{k}") for k in range(3)]
        w1b_zero = sem("w1b_zero")
        w1_in = sem("w1_in")
        w2_in = sem("w2_in")
        w_sc = sem("w_sc")
        w_acc = sem("w_acc")
        eb_out = sem("eb_out")
        rc_out = sem("rc_out")
        z_st = sem("z_st")
        b2_in = sem("b2_in")
        rt_dve = sem("rt_dve")
        rt_act = sem("rt_act")
        rt_pe = sem("rt_pe")
        idx_out = sem("idx_out")
        acc_st = sem("acc_st")
        xg_in = [sem(f"xg_in{k}") for k in range(4)]
        xgT_done = sem("xgT_done")
        xgT_out = sem("xgT_out")
        l1_done = sem("l1_done")
        relu_out = sem("relu_out")
        hid_done = sem("hid_done")
        hid_out = sem("hid_out")
        l2_done = sem("l2_done")
        yo_out = sem("yo_out")
        y_add = sem("y_add")
        out_st = sem("out_st")
        u_out = sem("u_out")
        v_step = sem("v_step")
        uc_out = sem("uc_out")
        rr_out = sem("rr_out")
        r_out = sem("r_out")
        my_out = sem("my_out")
        m2_out = sem("m2_out")
        pr_out = sem("pr_out")
        g_out = sem("g_out")
        g_in = [sem(f"g_in{k}") for k in range(4)]
        grp_done = sem("grp_done")
        far_done = sem("far_done")
        far_out = sem("far_out")
        a_in = [sem(f"a_in{t}") for t in range(BLK)]
        block = ctx.enter_context(nc.Block())

        SC = float(D) ** -0.5
        RD = {"nsq": 2, "cnt": 20, "d": 21, "B": 43}

        @block.gpsimd
        def _(eng):
            eng.memset(ident[:, :], 0.0).then_inc(consts, 1)
            eng.memset(maskbd[:, :], 0.0).then_inc(consts, 1)
            eng.memset(negc[:, :], -1.0).then_inc(consts, 1)
            eng.wait_ge(consts, 3)
            eng.affine_select(out=ident[:, :], in_=ident[:, :], compare_op=ALU.not_equal, fill=1.0,
                              base=0, pattern=[[-1, P]], channel_multiplier=1).then_inc(consts, 1)
            eng.wait_ge(consts, 4)
            eng.memset(maskbd[0:S, S:P], -1e30).then_inc(consts, 1)
            eng.memset(maskbd[S:P, 0:S], -1e30).then_inc(consts, 1)
            eng.wait_ge(consts, 6)
            eng.affine_select(out=negc[:, :], in_=negc[:, :], compare_op=ALU.is_ge, fill=0.0,
                              base=0, pattern=[[1, S]], channel_multiplier=-1).then_inc(consts, 1)
            eng.memset(MN, 0.0).then_inc(mn_zero, 1)
            eng.wait_ge(mn_zero, 1)
            eng.memset(W1B[KB:P, :], 0.0).then_inc(w1b_zero, 1)
            eng.wait_ge(w1b_zero, 1)
            eng.wait_ge(w0_out, 3)
            eng.wait_ge(qv_done, NT)
            eng.wait_ge(kq_done, H * NG)
            for k in range(4):
                eng.wait_ge(q_st[k], 16 * NT // 4)
            for h in range(H):
                eng.tensor_copy(gw[0:HD, 32 * h:32 * h + 32, :],
                                w0h[:, h, :].unsqueeze(1).broadcast_to([HD, 32, HD])).then_inc(gw_rep, 1)

            na = 0
            for c in range(4):
                e2 = slice(2 * c, 2 * c + 2)
                eng.wait_ge(w_sc, 8 * (c + 1))
                for n in ("w_fast1", "h_fast1"):
                    w = io["L0_ffn_" + n]
                    eng.dma_start(w1a[:, e2, :], w[e2, 0:P, :].rearrange("e p n -> p e n"), accum_op=ALU.add).then_inc(w_acc, 16)
                    eng.dma_start(w1b[0:KB, e2, :], w[e2, P:D, :].rearrange("e p n -> p e n"), accum_op=ALU.add).then_inc(w_acc, 16)
                    na += 32
                    eng.wait_ge(w_acc, na)
            for c in range(4):
                e2 = slice(2 * c, 2 * c + 2)
                eng.wait_ge(w_sc, 32 + 6 * (c + 1))
                for n in ("w_fast2", "h_fast2"):
                    for e in (2 * c, 2 * c + 1):
                        eng.dma_start(w2[:, e, :, :], io["L0_ffn_" + n][e].rearrange("(k p) d -> p k d", p=P), accum_op=ALU.add).then_inc(w_acc, 16)
                    na += 32
                    eng.wait_ge(w_acc, na)

            eng.wait_ge(h_in, 32)

            def y_tile(i):
                k = i % 2
                eng.wait_ge(qr_in[k], 16 * (i // 2 + 1))
                eng.tensor_tensor(QR[k], QR[k], btok[:, :], ALU.add).then_inc(qb_out, 1)
                eng.wait_ge(zn_out, i + 1)
                eng.tensor_tensor(ZS[i % 5], ZS[i % 5], gtok[:, :], ALU.mult).then_inc(yg_out, 1)
                eng.wait_ge(yg_out, i + 1)
                eng.wait_ge(qb_out, i + 1)
                eng.tensor_tensor(ZS[i % 5], ZS[i % 5], QR[k], ALU.add).then_inc(y_out, 1)

            for i in range(NT):
                eng.tensor_tensor(h2[:, i, :], h2[:, i, :], bup, ALU.add).then_inc(hb_out, 1)
                y_tile(i)

            eng.wait_ge(zq_done, NT)
            eng.iota(w8, [[-1, E]], base=E, channel_multiplier=0, allow_small_or_imprecise_dtypes=True).then_inc(rc_out, 1)
            eng.iota(irow, [[1, P]], base=0, channel_multiplier=0, allow_small_or_imprecise_dtypes=True).then_inc(rc_out, 1)
            eng.iota(i41, [[P, SLOTS + 1]], base=0, channel_multiplier=0, allow_small_or_imprecise_dtypes=True).then_inc(rc_out, 1)
            eng.iota(tokid, [[P, NT]], base=1, channel_multiplier=1, allow_small_or_imprecise_dtypes=True).then_inc(rc_out, 1)
            eng.iota(trash, [[1, 1]], base=NT * P + 1, channel_multiplier=1, allow_small_or_imprecise_dtypes=True).then_inc(rc_out, 1)
            eng.memset(tri, 1.0).then_inc(rc_out, 1)
            eng.memset(ones, 1.0).then_inc(rc_out, 1)
            eng.memset(emask, 1.0).then_inc(rc_out, 1)
            for k in range(4):
                eng.memset(XG[k], 0.0).then_inc(rc_out, 1)
            eng.wait_ge(rc_out, 12)
            eng.affine_select(out=tri, in_=tri, compare_op=ALU.is_gt, fill=0.0, base=0, pattern=[[1, P]],
                              channel_multiplier=-1).then_inc(rc_out, 1)
            eng.affine_select(out=emask, in_=emask, compare_op=ALU.is_gt, fill=0.0, base=0, pattern=[[1, E], [-1, E]],
                              channel_multiplier=0).then_inc(rc_out, 1)
            for k in range(4):
                eng.memset(XG[k][:, D:D + 1], 1.0).then_inc(rc_out, 1)

            def gather(s):
                if s >= 4:
                    eng.wait_ge(xgT_done, s - 3)
                eng.indirect_dma_start(out=XG[s % 4][:, 0:D], out_offset=None, in_=xn_d,
                                       in_offset=IndirectOffsetOnAxis(ap=idx[:, s:s + 1], axis=0)).then_inc(xg_in[s % 4], 16)

            def add(s):
                eng.wait_ge(yo_out, s + 1)
                if s >= 1:
                    eng.wait_ge(y_add, 16 * s)
                eng.indirect_dma_start(out=acc_d, out_offset=IndirectOffsetOnAxis(ap=idx[:, s:s + 1], axis=0), in_=YO[s % 4],
                                       in_offset=None, compute_op=ALU.add).then_inc(y_add, 16)

            eng.wait_ge(rc_out, 18)
            eng.wait_ge(idx_out, 1)
            eng.wait_ge(z_st, 32)
            for k in range(3):
                eng.wait_ge(xn_st[k], 16 * len(range(k, NT, 3)))
            for s in range(4):
                gather(s)
            eng.wait_ge(acc_st, 16)
            for s in range(SLOTS):
                add(s)
                if s + 4 < SLOTS:
                    gather(s + 4)
        CONSTS = 7

        @block.sync
        def _(eng):
            eng.wait_ge(x_zero, 1)
            for c in range(4):
                for b2 in range(2):
                    src = io["x"].rearrange("(i b) t d -> b t i d", b=2)[b2, 0:T_IN:2, 4 * c:4 * c + 4, :]
                    eng.dma_start(xs[S * b2:S * b2 + S_IN, 4 * c:4 * c + 4, :], src).then_inc(x_in[c], 16)
            for a, r in ((0, slice(0, P)), (1, slice(P, D))):
                eng.dma_start(Wd[a], io["L0_attn_W_down"][r, :]).then_inc(w_in, 16)
                for c, n in ((0, "Wk"), (1, "Wq")):
                    eng.dma_start(Wkq[a][:, :, c, :], io["L0_attn_" + n][r, :].rearrange("k (h e) -> k h e", h=H)).then_inc(w_in, 16)
                n = r.stop - r.start
                eng.dma_start(Wqv[a][0:n, 0:D], io["L0_attn_Wq"][r, :]).then_inc(w_in, 16)
                eng.dma_start(Wqv[a][0:n, D:2 * D], io["L0_attn_Wv"][r, :]).then_inc(w_in, 16)
                eng.dma_start(Wqv[a][0:n, 2 * D:NQV], io["L0_attn_lr_w"][r, :]).then_inc(w_in, 16)
                eng.dma_start(bdc[0:n, a:a + 1], io["L0_attn_b_down"][r].rearrange("(k o) -> k o", o=1)).then_inc(w_in, 16)
            eng.wait_ge(wprep, 3)
            eng.dma_start(Wqv[1][KB:KB + 1, 2 * D:NQV], io["L0_attn_lr_b"].rearrange("(o k) -> o k", o=1)).then_inc(w_in, 16)
            eng.dma_start(gtok[:, :], io["L0_attn_ttt_g"].rearrange("h e -> (h e)").partition_broadcast(P)).then_inc(w_in, 16)
            eng.dma_start(btok[:, :], io["L0_attn_ttt_b"].rearrange("h e -> (h e)").partition_broadcast(P)).then_inc(w_in, 16)
            eng.dma_start(w0h[:, :, :], io["L0_attn_W1"].rearrange("h d e -> d h e")).then_inc(rows_in, 16)
            for h in range(H):
                rows = slice(32 * h, 32 * h + 32)
                eng.dma_start(b0r[rows, :], io["L0_attn_b1"][h, 0, :].partition_broadcast(32)).then_inc(rows_in, 16)
                eng.dma_start(g2r[rows, :], io["L0_attn_ttt_g"][h, :].partition_broadcast(32)).then_inc(rows_in, 16)
            eng.dma_start(b0t[:, :], io["L0_attn_b1"].rearrange("h o e -> (o h e)").partition_broadcast(P)).then_inc(rt_in, 16)
            eng.dma_start(emb[:, 0:DR], io["L0_ffn_router_emb"]).then_inc(rt_in, 16)
            eng.dma_start(rw[:, :], io["L0_ffn_router_w"]).then_inc(rt_in, 16)
            eng.dma_start(pw[:, :], io["L0_ffn_probe_w"]).then_inc(rt_in, 16)
            for c, n in enumerate(("post_g", "post_b", "norm_g", "norm_b")):
                for k in range(2):
                    eng.dma_start(gcol[:, k, c:c + 1], io["L0_attn_" + n][KB * k:KB * k + P].rearrange("(k o) -> k o", o=1)).then_inc(rt_in, 16)
            for k in range(2):
                eng.dma_start(mg[:, k, :], io[f"L0_ffn_m_gate{k + 1}"].partition_broadcast(P)).then_inc(rt_in, 16)
            eng.dma_start(ebias[:, :], io["L0_ffn_energy"].partition_broadcast(P)).then_inc(rt_in, 16)
            eng.dma_start(fat[:, :], io["L0_ffn_fatigue"].partition_broadcast(P)).then_inc(rt_in, 16)
            eng.wait_ge(w1b_zero, 1)
            eng.dma_start(W1B[KB:KB + 1, :], io["L0_ffn_b1"].rearrange("e (o n) -> o (e n)", o=1)).then_inc(rt_in, 16)
            for c in range(4):
                e2 = slice(2 * c, 2 * c + 2)
                eng.dma_start(w1a[:, e2, :], io["L0_ffn_w_slow1"][e2, 0:P, :].rearrange("e p n -> p e n")).then_inc(w1_in, 16)
                eng.dma_start(w1b[0:KB, e2, :], io["L0_ffn_w_slow1"][e2, P:D, :].rearrange("e p n -> p e n")).then_inc(w1_in, 16)
            eng.wait_ge(h_out, NT)
            eng.dma_start(hmix_d.rearrange("(i p) d -> p i d", p=P), hmix).then_inc(hmix_st, 16)
            for i in range(NT):
                eng.wait_ge(qt_out, i + 1)
                eng.dma_start(q_d[i * P:(i + 1) * P, :], qst[:, i % 4, :]).then_inc(q_st[i % 4], 16)
            eng.wait_ge(hmix_st, 16)
            eng.wait_ge(eta_out, 1)
            eng.dma_start(eta96[:, :], etaT).then_inc(eta_in, 16)
            for q in range(6):
                eng.wait_ge(km_out, 4 * (q + 1))
                eng.dma_start(km_d[:, 16 * q:16 * (q + 1), :], kqm[HD:P, 16 * q:16 * (q + 1), 0, :]).then_inc(km_st, 16)
            eng.wait_ge(km_st, 16 * 6)
            eng.wait_ge(mn_zero, 1)
            for J in range(NB):
                n = min(2 * BLK, S - BLK * J)
                eng.dma_start(mn[:, BLK * J:BLK * (J + 1), 0:n],
                              km_d[BLK * J:BLK * (J + 1), :, BLK * J:BLK * J + n].rearrange("s r w -> r s w")).then_inc(mn_in, 16)
            eng.wait_ge(c_out, 2)
            eng.dma_start(c_d.rearrange("(i p) d -> p i d", p=P), vk).then_inc(c_st, 16)
            eng.wait_ge(c_st, 16)
            eng.wait_ge(eta_in, 16)
            for h in range(H):
                eng.dma_start(cc[32 * h:32 * h + 32, :, :],
                              c_d.rearrange("(b t) (h e) -> h b t e", t=S, h=H)[h]).then_inc(c_in, 16)

            for e in range(E):
                eng.dma_start(w2[:, e, :, :], io["L0_ffn_w_slow2"][e].rearrange("(k p) d -> p k d", p=P)).then_inc(w2_in, 16)

            def spread(J):
                eng.wait_ge(far_out, 4 * (J + 1))
                if J >= 2:
                    eng.wait_ge(grp_done, BLK * (J - 1) + 6)
                for t in range(BLK):
                    eng.dma_start(ablk[J % 2][:, HD * t:HD * (t + 1)], far_sb[t:R:32, :]).then_inc(a_in[t], 16)

            spread(0)
            spread(1)
            for t in range(S):
                eng.wait_ge(g_out, t + 1)
                eng.dma_start(GW[HD + t:HD + t + 1, :], Gst[:, t % 4, :]).then_inc(g_in[t % 4], 16)
                J = t // BLK
                if t % BLK == 6 and 1 <= J < NB - 1:
                    spread(J + 1)
            for k in range(4):
                eng.wait_ge(g_in[k], 16 * S // 4)
            eng.wait_ge(m2_out, S)
            eng.wait_ge(grp_done, S - 1)
            for i in range(2):
                eng.dma_start(QR[i], q_d[P * i:P * (i + 1), :]).then_inc(qr_in[i % 2], 16)
            eng.dma_start(bup, io["L0_attn_b_up"].partition_broadcast(P)).then_inc(h_in, 16)
            eng.dma_start(h2, hmix_d.rearrange("(i p) d -> p i d", p=P)).then_inc(h_in, 16)
            for w, n in ((Wo, "Wo"), (Wu, "W_up")):
                eng.dma_start(w[0], io["L0_attn_" + n][0:P, :]).then_inc(post_w, 16)
                eng.dma_start(w[1], io["L0_attn_" + n][P:D, :]).then_inc(post_w, 16)
            for j in range(NT + 7):
                i = j + 2
                if i < NT:
                    eng.wait_ge(y_out, i - 1)
                    eng.dma_start(QR[i % 2], q_d[P * i:P * (i + 1), :]).then_inc(qr_in[i % 2], 16)
                i = j - 7
                if 0 <= i:
                    eng.wait_ge(xn2_out, i + 1)
                    eng.dma_start(xn_d[P * i:P * (i + 1), :], XN[i % 3]).then_inc(xn_st[i % 3], 16)
            eng.dma_start(acc_d[0:NT * P, :].rearrange("(i p) d -> p i d", p=P), h2).then_inc(acc_st, 16)
            eng.wait_ge(zq_done, NT)
            eng.dma_start(b2r, io["L0_ffn_b2"].rearrange("e (o d) -> o (e d)", o=1)).then_inc(b2_in, 16)
            eng.wait_ge(rc_out, 12)
            for d in (xn_d, acc_d):
                eng.dma_start(d[NT * P:, :], XG[0][:, 0:D]).then_inc(z_st, 16)
            eng.wait_ge(y_add, 16 * SLOTS)
            eng.dma_start(out.rearrange("b t d -> (b t) d"), acc_d[0:NT * P, :]).then_inc(out_st, 16)
            eng.wait_ge(out_st, 16)
        NW = 7 * 2 + 1 + 2

        @block.tensor
        def _(eng):
            eng.wait_ge(consts, CONSTS)

            def xT(i):
                eng.wait_ge(x_in[i // 4], 32)
                if i >= 2:
                    eng.wait_ge(xT_out, i - 1)
                eng.transpose(bank[i % 2][:, 0:P], xs[:, i, 0:P], ident[:, :])
                eng.transpose(bank[i % 2][:, P:2 * P], xs[:, i, KB:D], ident[:, :]).then_inc(xT_done, 1)

            def scores(i):
                eng.wait_ge(xT_out, i + 1)
                if i >= 2:
                    eng.wait_ge(mx_out, i - 1)
                ps = bank[2 + i % 2][:, 0:P]
                xa, xb = xT_sb[i % 2][:, 0:P], xT_sb[i % 2][KB:P, P:2 * P]
                eng.matmul(ps, xa, xa, start=True, stop=False)
                eng.matmul(ps, xb, xb, start=False, stop=True).then_inc(s_done, 1)

            def eT(i):
                eng.wait_ge(exp_out, i + 1)
                if i >= 2:
                    eng.wait_ge(eT_out, i - 1)
                eng.transpose(bank[4 + i % 2][:, 0:P], Ex[i % 2], ident[:, :]).then_inc(eT_done, 1)

            def mix(i):
                eng.wait_ge(eT_out, i + 1)
                if i >= 2:
                    eng.wait_ge(h_out, i - 1)
                eng.matmul(bank[6 + i % 2][:, 0:D], ExT[i % 2], xs[:, i, :], start=True, stop=True).then_inc(o_done, 1)

            for j in range(NT + 3):
                if j < NT:
                    xT(j)
                if 0 <= j - 1 < NT:
                    scores(j - 1)
                if 0 <= j - 2 < NT:
                    eT(j - 2)
                if 0 <= j - 3 < NT:
                    mix(j - 3)

            def xnT(i):
                eng.wait_ge(xn_out, i + 1)
                if i >= 2:
                    eng.wait_ge(xnT_out, i - 1)
                eng.transpose(bank[i % 2][:, 0:P], xs[:, i, 0:P], ident[:, :])
                eng.transpose(bank[i % 2][:, P:2 * P], xs[:, i, KB:D], ident[:, :]).then_inc(xnT_done, 1)

            def down(g):
                eng.wait_ge(xnT_out, 4 * (g + 1))
                if g == 0:
                    eng.wait_ge(w_in, 16 * NW)
                if g >= 1:
                    eng.wait_ge(hT_out, 2 * g)
                tiles = slice(4 * g, 4 * g + 4)
                for m, (a, b) in enumerate(((0, P), (P, D))):
                    ps = bank[2 + m][0:b - a, :]
                    eng.matmul(ps, Wd[0][:, a:b], xnTs[:, tiles, 0, :], start=True, stop=False)
                    eng.matmul(ps, Wd[1][:, a:b], xnTs[KB:P, tiles, 1, :], start=False, stop=True).then_inc(hd_done, 1)

            for i in range(NT):
                xnT(i)
                if i % 4 == 3:
                    down(i // 4)

            def kq(n):
                g, h = divmod(n, H)
                eng.wait_ge(hT_out, 2 * (g + 1))
                if n >= 2:
                    eng.wait_ge(k_out, n - 1)
                    eng.wait_ge(q_out, n - 1)
                cols = slice(512 * g, 512 * (g + 1))
                ps = bank[4 + n % 2]
                eng.matmul(ps[:, :], Wkq[0][:, h, :, :].rearrange("p c e -> p (c e)"), hTa[:, cols], start=True, stop=False)
                eng.matmul(ps[:, :], Wkq[1][:, h, :, :].rearrange("p c e -> p (c e)"), hTb[0:KB, cols], start=False, stop=True).then_inc(kq_done, 1)

            def qv(i):
                if i == 0:
                    eng.wait_ge(wprep, 4)
                if i >= 2:
                    eng.wait_ge(qt_out, i - 1)
                    eng.wait_ge(vk_out, i - 1)
                cols = slice(P * i, P * (i + 1))
                ps = bank[6 + i % 2][:, 0:NQV]
                eng.matmul(ps, hTa[:, cols], Wqv[0], start=True, stop=False)
                eng.matmul(ps, hTb[:, cols], Wqv[1], start=False, stop=True).then_inc(qv_done, 1)

            for g in range(NG):
                for h in range(H):
                    kq(H * g + h)
                for i in range(4 * g, 4 * g + 4):
                    qv(i)
            eng.wait_ge(vk_out, NT)
            eng.transpose(bank[0][0:H * NT, 0:P], etal[:, :, :].rearrange("p h i -> p (h i)"), ident[:, :]).then_inc(eta_done, 1)

            def grams(n):
                if n == 0:
                    eng.wait_ge(k_out, H * NG)
                    eng.wait_ge(q_out, H * NG)
                ps = bank[2 + n % 3]
                if n >= 3:
                    eng.wait_ge(qm_out, n - 2)
                for j in range(4):
                    mm = eng.matmul(ps[0:S, P * j:P * (j + 1)], kqm[0:HD, 4 * n + j, 0, :],
                                    kqm[0:HD, 4 * n + j, :, :].rearrange("p c t -> p (c t)"), start=True, stop=True)
                mm.then_inc(gram_done, 1)

            for n in range(R // 4):
                grams(n)

            def far(J, part, span=16):
                K = HD + BLK * max(0, J - 1)
                for j in range(span * part, min(span * (part + 1), R)):
                    b, h = divmod(j, H)
                    row = 32 * h + b
                    if j % 24 == 0 and J >= 1:
                        eng.wait_ge(far_out, 4 * (J - 1) + j // 24 + 1)
                    mm = eng.matmul(bank[4 + b // 8][32 * h:32 * h + 32, HD * (b % 8):HD * (b % 8 + 1)],
                                    kqm[0:K, row, 0:2, :].rearrange("p c t -> p (c t)")[:, BLK * J:BLK * J + 32],
                                    gw[0:K, row, :], start=True, stop=True)
                    if j % 24 == 23:
                        mm.then_inc(far_done, 1)

            idr = ident[0:R, 0:R]

            def open_z(J):
                eng.matmul(bank[J % 2][0:R, :], idr, b0r[:, :].unsqueeze(1).broadcast_to([R, BLK, HD]),
                           start=True, stop=False, skip_group_check=True)

            eng.wait_ge(rt_prep, 5)
            eng.wait_ge(vk_out, NT)
            eng.transpose(bank[6][0:DR, 0:E], emb[:, 0:DR], ident[0:E, 0:E]).then_inc(rt_mm, 1)
            eng.wait_ge(rt_prep, 6)
            for k in range(2):
                ch = slice(KB * k, KB * k + P)
                o = NR * k
                eng.matmul(bank[7][:, o:o + E], rw[:, ch], ident[0:E, 0:E], start=True, stop=False, skip_group_check=True)
                eng.matmul(bank[7][:, o:o + E], ones8[:, :], dg8[:, :], start=False, stop=True, skip_group_check=True)
                eng.matmul(bank[7][:, o + E:o + 2 * E], pw[:, ch], enT[:, :], start=True, stop=True, skip_group_check=True)
                eng.matmul(bank[7][:, o + 2 * E:o + NR], pw[:, ch], ident[0:DR, 0:DR], start=True, stop=True,
                           skip_group_check=True).then_inc(rt_mm, 1)

            eng.wait_ge(gw_rep, 3)
            eng.wait_ge(rt_prep, 7)
            eng.wait_ge(qm_out, R // 4)
            eng.wait_ge(km_out, R // 4)
            for J in range(2):
                for part in range(6):
                    far(J, part)
            eng.wait_ge(b0_out, 3)
            eng.wait_ge(eta_out, 1)
            open_z(0)
            for t in range(BLK):
                eng.wait_ge(a_in[t], 16)
            eng.matmul(bank[0][0:R, :], idr, ablk[0], start=False, stop=False, skip_group_check=True).then_inc(grp_done, 1)
            SPAN = 20
            for t in range(S - 2):
                J, i = divmod(t, BLK)
                eng.wait_ge(pr_out, t + 1)
                if i == 0 and J < NB - 1:
                    open_z(J + 1)
                n = max(0, BLK - (i + 2))
                mm = None
                if n:
                    mm = eng.matmul(bank[J % 2][0:R, HD * (i + 2):], ident[:, 0:R], PR[t % 2][:, 0:n, :],
                                    start=False, stop=False, skip_group_check=True)
                if J < NB - 1:
                    first = max(0, i + 2 - BLK)
                    mm = eng.matmul(bank[(J + 1) % 2][0:R, HD * first:], ident[:, 0:R], PR[t % 2][:, n:n + BLK - first, :],
                                    start=False, stop=False, skip_group_check=True)
                a = t + 2
                if BLK <= a < S:
                    eng.wait_ge(a_in[a % BLK], 16 * (a // BLK + 1))
                    mm = eng.matmul(bank[a // BLK % 2][0:R, HD * (a % BLK):HD * (a % BLK + 1)], idr,
                                    ablk[a // BLK % 2][:, HD * (a % BLK):HD * (a % BLK + 1)],
                                    start=False, stop=False, skip_group_check=True)
                if mm is None:
                    break
                mm.then_inc(grp_done, 1)
                if 1 <= J < NB - 1 and i < -(-R // SPAN):
                    if i == 0:
                        for k in range(4):
                            eng.wait_ge(g_in[k], 16 * (BLK * J // 4))
                    far(J + 1, i, SPAN)

            def zq(i):
                if i == 0:
                    for k in range(4):
                        eng.wait_ge(g_in[k], 16 * S // 4)
                    eng.wait_ge(u_out, S)
                if i >= 2:
                    eng.wait_ge(zs_out, i - 1)
                for b2 in range(2):
                    for h in range(H):
                        row = 32 * h + 2 * i + b2
                        mm = eng.matmul(bank[i % 2][S * b2:S * (b2 + 1), HD * h:HD * (h + 1)], kqm[:, row, 1, :], gw[:, row, :],
                                        start=True, stop=True)
                mm.then_inc(zq_done, 1)

            for j in range(NT + 8):
                if j < NT:
                    zq(j)
                i = j - 4
                if 0 <= i < NT:
                    if i == 0:
                        eng.wait_ge(post_w, 64)
                    eng.wait_ge(t1_out, 2 * i + 2)
                    if i >= 1:
                        eng.wait_ge(tn_out, i)
                    eng.matmul(bank[2][:, 0:D], tT1[i % 2][:, 0:P], Wo[0], start=True, stop=False)
                    eng.matmul(bank[2][:, 0:D], tT1[i % 2][KB:P, P:2 * P], Wo[1], start=False, stop=True).then_inc(wo_done, 1)
                i = j - 6
                if 0 <= i < NT:
                    eng.wait_ge(t2_out, 2 * i + 2)
                    if i >= 1:
                        eng.wait_ge(h2_out, i)
                    eng.matmul(bank[3][:, 0:D], tT2[i % 2][:, 0:P], Wu[0], start=True, stop=False)
                    eng.matmul(bank[3][:, 0:D], tT2[i % 2][KB:P, P:2 * P], Wu[1], start=False, stop=True).then_inc(up_done, 1)
                i = j - 8
                if 0 <= i < NT:
                    eng.wait_ge(t3_out, i + 1)
                    if i >= 1:
                        eng.wait_ge(lg_out, i)
                    eng.matmul(bank[4][:, 0:NR], tT3[i % 2][:, 0:P], Wr[:, 0, :], start=True, stop=False)
                    eng.matmul(bank[4][:, 0:NR], tT3[i % 2][KB:P, P:2 * P], Wr[KB:P, 1, :], start=False, stop=True).then_inc(rt_done, 1)
                if 0 <= j - 3 < NT:
                    i = j - 3
                    eng.wait_ge(yn_out, i + 1)
                    if i >= 1:
                        eng.wait_ge(t1_out, 2 * i)
                    eng.transpose(bank[5][:, 0:P], ZS[i % 5][:, 0:P], ident[:, :])
                    eng.transpose(bank[5][:, P:2 * P], ZS[i % 5][:, KB:D], ident[:, :]).then_inc(t1_done, 1)
                if 0 <= j - 5 < NT:
                    i = j - 5
                    eng.wait_ge(tn_out, i + 1)
                    if i >= 1:
                        eng.wait_ge(t2_out, 2 * i)
                    eng.transpose(bank[6][:, 0:P], TN[i % 2][:, 0:P], ident[:, :])
                    eng.transpose(bank[6][:, P:2 * P], TN[i % 2][:, KB:D], ident[:, :]).then_inc(t2_done, 1)
                if 0 <= j - 7 < NT:
                    i = j - 7
                    eng.wait_ge(xn2_out, i + 1)
                    if i >= 1:
                        eng.wait_ge(t3_out, i)
                    eng.transpose(bank[7][:, 0:P], XN[i % 3][:, 0:P], ident[:, :])
                    eng.transpose(bank[7][:, P:2 * P], XN[i % 3][:, KB:D], ident[:, :]).then_inc(t3_done, 1)

            eng.wait_ge(rc_out, 14)
            eng.wait_ge(rt_dve, RD["cnt"])
            eng.matmul(bank[0][:, 0:E], ones, cnt, start=True, stop=True).then_inc(rt_pe, 1)
            eng.matmul(bank[1][:, 0:NI], tri, oha.rearrange("p i e -> p (i e)"), start=True, stop=False, skip_group_check=True)
            for i in range(NT - 1):
                n = NT - 1 - i
                mm = eng.matmul(bank[1][:, E * (i + 1):NI], ones, oha[:, i, :].unsqueeze(1).broadcast_to([P, n, E]),
                                start=False, stop=i == NT - 2, skip_group_check=True)
            mm.then_inc(rt_pe, 1)
            for j in range(2 * NT):
                if j % 8 == 0:
                    eng.wait_ge(rt_dve, RD["B"] + j // 8)
                mm = eng.matmul(bank[2][:, 0:2 * SLOTS], Bh[:, j, :], av[:, j, :, :], start=j == 0, stop=j == 2 * NT - 1)
            mm.then_inc(rt_pe, 1)

            eng.wait_ge(rc_out, 18)
            eng.wait_ge(idx_out, 1)
            eng.wait_ge(b2_in, 16)
            eng.wait_ge(w_acc, 16 * 32)

            def x_T(s, k, g):
                eng.wait_ge(xg_in[k], 16 * (g + 1))
                eng.transpose(bank[4][:, 0:P], XG[k][:, 0:P], ident[:, :])
                eng.transpose(bank[4][:, P:2 * P], XG[k][:, P:2 * P], ident[:, :]).then_inc(xgT_done, 1)

            def layer1(s):
                e = eng.value_load(ex[0:1, ds(s, 1)], min_val=0, max_val=E - 1)
                eng.wait_ge(xgT_out, s + 1)
                for m in range(2):
                    ps = bank[m][:, 0:HID // 2]
                    o = HID // 2 * m
                    eng.matmul(ps, xgT[:, 0:P], W1A[:, ds(e * HID + o, HID // 2)], start=True, stop=False)
                    eng.matmul(ps, xgT[:, P:2 * P], W1B[:, ds(e * HID + o, HID // 2)], start=False, stop=True).then_inc(l1_done, 1)

            def layer2(s):
                e = eng.value_load(ex[0:1, ds(s, 1)], min_val=0, max_val=E - 1)
                if not (isinstance(s, int) and s == 0):
                    eng.wait_ge(yo_out, s)
                eng.wait_ge(hid_out, 2 * s + 2)
                for c in range(KH):
                    eng.matmul(bank[7][:, 0:D], HT2[:, P * c:P * (c + 1)], W2[:, ds(e * (KH * D) + D * c, D)],
                               start=c == 0, stop=False)
                eng.matmul(bank[7][:, 0:D], ones[0:1, :], b2r[:, ds(e * D, D)], start=False, stop=True).then_inc(l2_done, 1)

            def hid_T(s):
                eng.wait_ge(relu_out, 2 * s + 2)
                for c in range(KH):
                    mm = eng.transpose(bank[5 + c // 3][:, P * (c % 3):P * (c % 3 + 1)], RL[:, P * c:P * (c + 1)], ident[:, :])
                    if c % 3 == 2:
                        mm.then_inc(hid_done, 1)

            def slots(g, first, last):
                for k in range(4):
                    s = 4 * g + k
                    layer1(s)
                    if not (first and k == 0):
                        layer2(s - 1)
                    if not (last and k == 3):
                        x_T(s + 1, (k + 1) % 4, g + (k + 1) // 4)
                    hid_T(s)

            x_T(0, 0, 0)
            slots(0, True, False)
            with eng.Fori(1, SLOTS // 4 - 1) as g:
                slots(g, False, False)
            slots(SLOTS // 4 - 1, False, True)
            layer2(SLOTS - 1)

        @block.scalar
        def _(eng):
            for j in range(NT + 3):
                if j < NT:
                    eng.wait_ge(xT_done, j + 1)
                    if j >= 2:
                        eng.wait_ge(s_done, j - 1)
                    eng.activation(xT_sb[j % 2], bank[j % 2][:, 0:2 * P], ACT.Copy).then_inc(xT_out, 1)
                if 0 <= j - 1 < NT:
                    i = j - 1
                    eng.wait_ge(negm_out, i + 1)
                    if i >= 2:
                        eng.wait_ge(eT_done, i - 1)
                    eng.activation(Ex[i % 2], Sm[i % 2], ACT.Exp, bias=negm[:, i:i + 1], scale=SC,
                                   accum_out=esum[:, i:i + 1]).then_inc(exp_out, 1)
                if 0 <= j - 2 < NT:
                    i = j - 2
                    eng.wait_ge(eT_done, i + 1)
                    if i >= 2:
                        eng.wait_ge(o_done, i - 1)
                    eng.activation(ExT[i % 2], bank[4 + i % 2][:, 0:P], ACT.Copy).then_inc(eT_out, 1)
            eng.wait_ge(stat_b, NT)
            eng.wait_ge(rt_prep, 1)
            eng.activation(emb[:, DR + 1:DR + 2], emb[:, DR:DR + 1], ACT.Sqrt).then_inc(rt_sq, 1)
            eng.activation(std0[:, :], mv[:, :, 1], ACT.Sqrt, bias=epsc[:, 0:1]).then_inc(std_out, 1)
            for i in range(NT):
                eng.wait_ge(xnT_done, i + 1)
                eng.activation(xnTs[:, i, :, :], bank[i % 2][:, 0:2 * P].rearrange("p (c t) -> p c t", c=2), ACT.Copy).then_inc(xnT_out, 1)
                if i % 4 == 3:
                    g = i // 4
                    cols = slice(512 * g, 512 * (g + 1))
                    eng.wait_ge(hd_done, 2 * g + 2)
                    eng.activation(hTa[:, cols], bank[2][:, :], ACT.Silu, bias=bdc[:, 0:1]).then_inc(hT_out, 1)
                    eng.activation(hTb[0:KB, cols], bank[3][0:KB, :], ACT.Silu, bias=bdc[0:KB, 1:2]).then_inc(hT_out, 1)
            for g in range(NG):
                for n in range(H * g, H * g + H):
                    h = n % H
                    eng.wait_ge(kq_done, n + 1)
                    eng.activation(kqm[0:HD, 32 * h + 8 * g:32 * h + 8 * g + 8, 0, :],
                                   bank[4 + n % 2][0:HD, :].rearrange("p (r t) -> p r t", t=S), ACT.Copy).then_inc(k_out, 1)
                for i in range(4 * g, 4 * g + 4):
                    eng.wait_ge(qv_done, i + 1)
                    if i >= 4:
                        eng.wait_ge(q_st[i % 4], 16 * (i // 4))
                    eng.activation(qst[:, i % 4, :], bank[6 + i % 2][:, 0:D], ACT.Copy).then_inc(qt_out, 1)
            eng.wait_ge(eta_done, 1)
            eng.activation(etaT, bank[0][0:H * NT, 0:P], ACT.Sigmoid).then_inc(eta_out, 1)
            for n in range(R // 4):
                eng.wait_ge(gram_done, n + 1)
                eng.activation(kqm[HD:P, 4 * n:4 * n + 4, 0, :],
                               bank[2 + n % 3][0:S, :].rearrange("p (r c t) -> p r c t", c=2, t=S)[:, :, 0, :],
                               ACT.Copy, scale=-1.0, bias=-1.0).then_inc(km_out, 1)

            EV = [3, 4, 5, 6]

            def far_evac(J, k):
                eng.wait_ge(far_done, 4 * J + k + 1)
                if J >= 1:
                    for t in range(BLK):
                        eng.wait_ge(a_in[t], 16 * J)
                eng.activation(far_sb[:, 512 * k:512 * (k + 1)], bank[4 + k][0:R, :], ACT.Copy).then_inc(far_out, 1)

            for J in range(2):
                for k in range(4):
                    far_evac(J, k)
            HH = HID // 2
            pieces = []
            for e in range(E):
                for m in range(2):
                    pieces.append((W1A[:, HID * e + HH * m:HID * e + HH * (m + 1)], mg[:, 0, e:e + 1], w1_in))
                for m in range(2):
                    pieces.append((W1B[0:KB, HID * e + HH * m:HID * e + HH * (m + 1)], mg[0:KB, 0, e:e + 1], w1_in))
            for e in range(E):
                for m in range(3):
                    o = KH * D * e + 2 * D * m
                    pieces.append((W2[:, o:o + 2 * D], mg[:, 1, e:e + 1], w2_in))
            eng.wait_ge(rt_in, 16 * 17)

            for t in range(S):
                J, i = divmod(t, BLK)
                eng.wait_ge(u_out, t + 1)
                if t >= 1:
                    eng.wait_ge(m2_out, t)
                eng.activation(UC[:, :], U[:, t % 2, :], ACT.Identity, scale=-float(HD), bias=usum[:, t % 2:t % 2 + 1]).then_inc(uc_out, 1)
                eng.wait_ge(rr_out, t + 1)
                eng.activation(sc[:, 2 + t % 2:3 + t % 2], sc[:, 1:2], ACT.Sqrt).then_inc(r_out, 1)
                eng.wait_ge(m2_out, t + 1)
                eng.wait_ge(my_out, 2 * (t + 1))
                if t >= 4:
                    eng.wait_ge(g_in[t % 4], 16 * (t // 4))
                eng.activation(Gst[:, t % 4, :], M2[:, t % 2, :], ACT.Copy, scale=y1[:, t % 2:t % 2 + 1]).then_inc(g_out, 1)
                if 1 <= J < NB - 1 and i in EV:
                    far_evac(J + 1, EV.index(i))
                if t < len(pieces):
                    w, m, ready = pieces[t]
                    eng.wait_ge(ready, 16 * E)
                    eng.activation(w, w, ACT.Copy, scale=m).then_inc(w_sc, 1)

            def sd(ready, n, k, i, eps, done):
                eng.wait_ge(ready, i + 1)
                eng.activation(mvs[:, k, i % 3, 2:3], mvs[:, k, i % 3, 1:2], ACT.Sqrt, bias=epsc[:, eps:eps + 1]).then_inc(done, 1)

            for j in range(NT + 8):
                if j < NT:
                    eng.wait_ge(sq_out, 2 * j + 2)
                    eng.activation(rz[:, j % 3, H:2 * H], rz[:, j % 3, 0:H], ACT.Sqrt, bias=epsc[:, 1:2], scale=1.0 / HD).then_inc(sqz_out, 1)
                i = j - 2
                if 0 <= i < NT:
                    sd(st_y, 0, 0, i, 1, sd_y)
                i = j - 4
                if 0 <= i < NT:
                    sd(st_t, 0, 1, i, 1, sd_t)
                i = j - 6
                if 0 <= i < NT:
                    sd(st_h, 0, 2, i, 0, sd_h)
                i = j - 3
                if 0 <= i < NT:
                    eng.wait_ge(t1_done, i + 1)
                    if i >= 2:
                        eng.wait_ge(wo_done, i - 1)
                    for c in range(2):
                        eng.activation(tT1[i % 2][:, P * c:P * (c + 1)], bank[5][:, P * c:P * (c + 1)], ACT.Identity,
                                       scale=gcol[:, c, 0:1], bias=gcol[:, c, 1:2]).then_inc(t1_out, 1)
                i = j - 5
                if 0 <= i < NT:
                    eng.wait_ge(t2_done, i + 1)
                    if i >= 2:
                        eng.wait_ge(up_done, i - 1)
                    for c in range(2):
                        eng.activation(tT2[i % 2][:, P * c:P * (c + 1)], bank[6][:, P * c:P * (c + 1)], ACT.Identity,
                                       scale=gcol[:, c, 2:3], bias=gcol[:, c, 3:4]).then_inc(t2_out, 1)
                i = j - 7
                if 0 <= i < NT:
                    eng.wait_ge(t3_done, i + 1)
                    if i >= 2:
                        eng.wait_ge(rt_done, i - 1)
                    eng.activation(tT3[i % 2], bank[7][:, 0:2 * P], ACT.Copy).then_inc(t3_out, 1)

            eng.wait_ge(rt_dve, RD["nsq"])
            eng.activation(nrm[:, 1, :], nrm[:, 0, :], ACT.Sqrt).then_inc(rt_act, 1)
            eng.wait_ge(rt_dve, RD["d"])
            eng.activation(gt[:, 2, :], gt[:, 3, :], ACT.Exp).then_inc(rt_act, 1)

            def x_out(s):
                eng.wait_ge(xgT_done, s + 1)
                if not (isinstance(s, int) and s == 0):
                    eng.wait_ge(l1_done, 2 * s)
                eng.activation(xgT, bank[4][:, 0:2 * P], ACT.Copy).then_inc(xgT_out, 1)

            def square(s):
                if not (isinstance(s, int) and s == 0):
                    eng.wait_ge(l2_done, s)
                for m in range(2):
                    eng.wait_ge(hid_done, 2 * s + m + 1)
                    eng.activation(HT2[:, HH * m:HH * (m + 1)], bank[5 + m][:, 0:HH], ACT.Square).then_inc(hid_out, 1)

            x_out(0)
            x_out(1)
            square(0)
            with eng.Fori(1, SLOTS - 1) as s:
                x_out(s + 1)
                square(s)
            square(SLOTS - 1)


        @block.vector
        def _(eng):
            eng.memset(X, 0.0).then_inc(x_zero, 1)
            for k in range(2):
                eng.memset(PR[k][:, :, :], 0.0)
            eng.memset(epsc[:, 1:2], 1e-6)
            eng.memset(epsc[:, 0:1], 1e-5).then_inc(wprep, 1)
            eng.memset(hTb[KB:KB + 1, :], 1.0).then_inc(wprep, 1)
            eng.memset(Wqv[1][KB:KB + 1, :], 0.0).then_inc(wprep, 1)
            for j in range(NT + 3):
                if 0 <= j - 1 < NT:
                    i = j - 1
                    eng.wait_ge(s_done, i + 1)
                    if i >= 2:
                        eng.wait_ge(exp_out, i - 1)
                    if i == 0:
                        eng.wait_ge(consts, CONSTS)
                    eng.tensor_tensor_reduce(Sm[i % 2], bank[2 + i % 2][:, 0:P], maskbd[:, :], 1.0, -3e38,
                                             ALU.add, ALU.max, rowm[:, i:i + 1]).then_inc(mx_out, 1)
                    eng.wait_ge(mx_out, i + 1)
                    eng.tensor_scalar(negm[:, i:i + 1], rowm[:, i:i + 1], -SC, None, ALU.mult).then_inc(negm_out, 1)
                if 0 <= j - 2 < NT:
                    i = j - 2
                    eng.wait_ge(exp_out, i + 1)
                    eng.reciprocal(rinv[:, i:i + 1], esum[:, i:i + 1]).then_inc(rinv_out, 1)
                if 0 <= j - 3 < NT:
                    i = j - 3
                    eng.wait_ge(o_done, i + 1)
                    eng.wait_ge(rinv_out, i + 1)
                    eng.tensor_scalar(hmix[:, i, :], bank[6 + i % 2][:, 0:D], rinv[:, i:i + 1], None, ALU.mult).then_inc(h_out, 1)
                    eng.wait_ge(h_out, i + 1)
                    eng.bn_stats(st6[:, i % 2, :], hmix[:, i, :]).then_inc(stat_a, 1)
                    eng.wait_ge(stat_a, i + 1)
                    eng.bn_aggr(mv[:, i, :], st6[:, i % 2, :]).then_inc(stat_b, 1)
            eng.wait_ge(rt_in, 16 * 17)
            eng.tensor_scalar(fat[:, :], fat[:, :], -0.1, None, ALU.mult).then_inc(eb_out, 1)
            eng.wait_ge(eb_out, 1)
            eng.scalar_tensor_tensor(ebias[:, :], ebias[:, :], 0.1, fat[:, :], ALU.mult, ALU.add).then_inc(eb_out, 1)
            eng.tensor_tensor_reduce(dgj[:, :], emb[:, 0:DR], emb[:, 0:DR], 1.0, 0.0, ALU.mult, ALU.add, emb[:, DR:DR + 1]).then_inc(rt_prep, 1)
            eng.wait_ge(rt_sq, 1)
            eng.tensor_scalar(emb[:, DR + 2:DR + 3], emb[:, DR + 1:DR + 2], 0.02 / D, 0.02 / D, ALU.mult, ALU.add).then_inc(rt_prep, 1)
            eng.tensor_scalar(emb[:, DR + 3:DR + 4], emb[:, DR + 1:DR + 2], 1e-12, None, ALU.max).then_inc(rt_prep, 1)
            eng.memset(ones8[:, :], 1.0)
            eng.wait_ge(rt_prep, 3)
            eng.reciprocal(emb[:, DR + 3:DR + 4], emb[:, DR + 3:DR + 4]).then_inc(rt_prep, 1)
            eng.tensor_scalar(dg8[:, :], ident[0:E, 0:E], emb[:, DR + 2:DR + 3], None, ALU.mult)
            eng.wait_ge(rt_prep, 4)
            eng.tensor_scalar(emb[:, 0:DR], emb[:, 0:DR], emb[:, DR + 3:DR + 4], None, ALU.mult).then_inc(rt_prep, 1)
            eng.wait_ge(std_out, 1)
            eng.reciprocal(rstd0[:, :], std0[:, :]).then_inc(rstd_out, 1)
            eng.wait_ge(rstd_out, 1)
            for i in range(NT):
                eng.tensor_scalar(xs[:, i, :], hmix[:, i, :], mv[:, i, 0:1], rstd0[:, i:i + 1],
                                  ALU.subtract, ALU.mult).then_inc(xn_out, 1)
            eng.wait_ge(rows_in, 16 * 7)
            eng.tensor_reduce(w0m[:, :], w0h[:, :, :], AX.X, ALU.add).then_inc(w0_out, 1)
            eng.tensor_reduce(b0m[:, 0:1], b0r[:, :], AX.X, ALU.add).then_inc(b0_out, 1)
            eng.tensor_tensor(g2r[:, :], g2r[:, :], g2r[:, :], ALU.mult)
            eng.wait_ge(w0_out, 1)
            eng.tensor_scalar(w0m[:, :], w0m[:, :], -1.0 / HD, None, ALU.mult).then_inc(w0_out, 1)
            eng.wait_ge(b0_out, 1)
            eng.tensor_scalar(b0m[:, 1:2], b0m[:, 0:1], -1.0 / HD, None, ALU.mult).then_inc(b0_out, 1)
            eng.wait_ge(w0_out, 2)
            eng.tensor_tensor(w0h[:, :, :], w0h[:, :, :], w0m[:, :].unsqueeze(2).broadcast_to([HD, H, HD]), ALU.add).then_inc(w0_out, 1)
            eng.wait_ge(b0_out, 2)
            eng.tensor_scalar(b0r[:, :], b0r[:, :], b0m[:, 1:2], None, ALU.add).then_inc(b0_out, 1)
            eng.wait_ge(w_in, 16 * NW)
            for a, n in ((0, P), (1, KB)):
                w = Wqv[a][0:n, D:2 * D].rearrange("p (h e) -> p h e", h=H)
                ins = eng.tensor_tensor(w, w, Wkq[a][:, :, 0, :], ALU.subtract)
            ins.then_inc(wprep, 1)
            for g in range(NG):
                for n in range(H * g, H * g + H):
                    h = n % H
                    eng.wait_ge(kq_done, n + 1)
                    eng.tensor_copy(kqm[0:HD, 32 * h + 8 * g:32 * h + 8 * g + 8, 1, :],
                                    bank[4 + n % 2][HD:P, :].rearrange("p (r t) -> p r t", t=S)).then_inc(q_out, 1)
                for i in range(4 * g, 4 * g + 4):
                    eng.wait_ge(qv_done, i + 1)
                    if i == 0:
                        eng.wait_ge(hd_done, 2 * NG)
                    eng.wait_ge(qt_out, i + 1)
                    eng.tensor_copy(etal[:, :, i], bank[6 + i % 2][:, 2 * D:NQV])
                    eng.tensor_tensor(vk[:, i, :], btok[:, :], bank[6 + i % 2][:, D:2 * D], ALU.subtract).then_inc(vk_out, 1)

            def c_scale():
                eng.wait_ge(vk_out, NT)
                for q in range(4):
                    v = vk[:, 4 * q:4 * q + 4, :]
                    eng.tensor_tensor(v, v, gtok[:, :].unsqueeze(1).broadcast_to([P, 4, D]), ALU.mult).then_inc(c_chain, 1)
                eng.wait_ge(c_chain, 4)
                for q in range(4):
                    v = vk[:, 4 * q:4 * q + 4, :].rearrange("p i (h e) -> p (i h) e", h=H)
                    eng.tensor_reduce(cmean[:, 12 * q:12 * q + 12], v, AX.X, ALU.add).then_inc(c_chain, 1)
                eng.wait_ge(c_chain, 8)
                eng.tensor_scalar(cmean[:, :], cmean[:, :], 1.0 / HD, None, ALU.mult).then_inc(c_chain, 1)
                eng.wait_ge(c_chain, 9)
                for q in range(2):
                    v = vk[:, 8 * q:8 * q + 8, :].rearrange("p i (h e) -> p (i h) e", h=H)
                    eng.tensor_tensor(v, v, cmean[:, 24 * q:24 * q + 24].unsqueeze(2).broadcast_to([P, 24, HD]),
                                      ALU.subtract).then_inc(c_out, 1)

            for n in range(R // 4):
                eng.wait_ge(gram_done, n + 1)
                if n == 0:
                    eng.wait_ge(consts, CONSTS)
                eng.wait_ge(km_out, n + 1)
                eng.scalar_tensor_tensor(kqm[HD:P, 4 * n:4 * n + 4, 1, :],
                                         bank[2 + n % 3][0:S, :].rearrange("p (r c t) -> p r c t", c=2, t=S)[:, :, 1, :],
                                         1.0, negc[:, :].unsqueeze(1).broadcast_to([S, 4, S]),
                                         ALU.add, ALU.mult).then_inc(qm_out, 1)
            c_scale()
            eng.wait_ge(rt_mm, 1)
            eng.tensor_copy(enT[:, :], bank[6][0:DR, 0:E]).then_inc(rt_prep, 1)
            b0v = b0t[:, :].rearrange("p (h e) -> p h e", h=H)
            eng.wait_ge(c_out, 2)
            eng.tensor_reduce(cmean[:, 0:H], b0v, AX.X, ALU.add).then_inc(b0t_out, 1)
            eng.wait_ge(b0t_out, 1)
            eng.tensor_scalar(cmean[:, 0:H], cmean[:, 0:H], 1.0 / HD, None, ALU.mult).then_inc(b0t_out, 1)
            eng.wait_ge(b0t_out, 2)
            eng.tensor_tensor(b0v, b0v, cmean[:, 0:H].unsqueeze(2).broadcast_to([P, H, HD]), ALU.subtract).then_inc(b0t_out, 1)
            eng.wait_ge(rt_mm, 3)
            eng.tensor_copy(Wr[:, :, :].rearrange("p c n -> p (c n)"), bank[7][:, 0:2 * NR]).then_inc(rt_prep, 1)
            eng.wait_ge(eta_in, 16)
            eng.tensor_scalar(eta96[:, :], eta96[:, :], 1.0 / HD, None, ALU.mult).then_inc(mne_out, 1)
            eng.wait_ge(mne_out, 1)
            eng.wait_ge(mn_in, 16 * NB)
            eng.tensor_tensor(mn, mn, eta96[:, :].unsqueeze(2).broadcast_to([R, S, 2 * BLK]), ALU.mult).then_inc(mne_out, 1)
            eng.wait_ge(mne_out, 2)
            eng.wait_ge(c_in, 16 * H)

            def z_next(t):
                J, i = divmod(t, BLK)
                z = bank[J % 2][0:R, HD * i:HD * (i + 1)]
                eng.wait_ge(grp_done, max(1, t))
                if t == 0:
                    eng.tensor_scalar(U[:, 0, :], z, 1.0, None, ALU.mult, ALU.add, accum_out=usum[:, 0:1]).then_inc(u_out, 1)
                    return
                ip = (t - 1) % BLK
                eng.wait_ge(m2_out, t)
                eng.scalar_tensor_tensor(U[:, t % 2, :], M2[:, (t - 1) % 2, :], MY[:, (t - 1) % 2, ip + 1:ip + 2], z,
                                         ALU.mult, ALU.add, accum_out=usum[:, t % 2:t % 2 + 1]).then_inc(u_out, 1)

            z_next(0)
            for t in range(S):
                J, i = divmod(t, BLK)
                u = U[:, t % 2, :]
                if t >= 1:
                    n = min(2 * BLK, S - BLK * ((t - 1) // BLK)) - ((t - 1) % BLK + 2)
                    if n > 0:
                        if t >= 3:
                            eng.wait_ge(grp_done, t - 2 + 1)
                        j0 = (t - 1) % BLK + 2
                        eng.tensor_tensor(PR[(t - 1) % 2][0:R, 0:n, :],
                                          M2[:, (t - 1) % 2, :].unsqueeze(1).broadcast_to([R, n, HD]),
                                          MY[:, (t - 1) % 2, j0:j0 + n].unsqueeze(2).broadcast_to([R, n, HD]),
                                          ALU.mult).then_inc(pr_out, 1)
                eng.wait_ge(u_out, t + 1)
                eng.tensor_tensor_reduce(JK[:, :], u, u, 1.0 / HD, 1e-6, ALU.mult, ALU.add, sc[:, 0:1]).then_inc(v_step, 1)
                eng.wait_ge(v_step, 6 * t + 1)
                eng.reciprocal(sc[:, 1:2], sc[:, 0:1]).then_inc(rr_out, 1)
                eng.tensor_tensor_reduce(PG[:, :], u, g2r[:, :], 1.0, 0.0, ALU.mult, ALU.add, sc[:, 4:5]).then_inc(v_step, 1)
                eng.wait_ge(v_step, 6 * t + 2)
                eng.scalar_tensor_tensor(PC[:, :], sc[:, 4:5].broadcast_to([R, HD]), -1.0 / HD, PG[:, :],
                                         ALU.mult, ALU.add).then_inc(v_step, 1)
                eng.wait_ge(v_step, 6 * t + 3)
                eng.wait_ge(r_out, t + 1)
                r = sc[:, 2 + t % 2:3 + t % 2]
                eng.scalar_tensor_tensor(Wv_[:, :], PC[:, :], r, cc[:, t, :], ALU.mult, ALU.add).then_inc(v_step, 1)
                if t >= 2:
                    eng.wait_ge(g_out, t - 1)
                eng.tensor_tensor(MY[:, t % 2, :], mn[:, t, :], r.broadcast_to([R, 2 * BLK]), ALU.mult).then_inc(my_out, 1)
                eng.wait_ge(v_step, 6 * t + 4)
                eng.tensor_tensor_reduce(JK[:, :], Wv_[:, :], u, 1.0 / HD ** 2, 0.0, ALU.mult, ALU.add, sc[:, 5:6]).then_inc(v_step, 1)
                eng.tensor_tensor(y1[:, t % 2:t % 2 + 1], eta96[:, t:t + 1], r, ALU.mult).then_inc(my_out, 1)
                eng.wait_ge(v_step, 6 * t + 5)
                eng.tensor_tensor(sc[:, 6:7], sc[:, 5:6], sc[:, 1:2], ALU.mult).then_inc(v_step, 1)
                eng.wait_ge(v_step, 6 * t + 6)
                eng.wait_ge(uc_out, t + 1)
                eng.scalar_tensor_tensor(M2[:, t % 2, :], UC[:, :], sc[:, 6:7], Wv_[:, :], ALU.mult, ALU.add).then_inc(m2_out, 1)
                if t + 1 < S:
                    z_next(t + 1)

            nri = [0]

            def inv(k, i):
                nri[0] += 1
                eng.reciprocal(mvs[:, k, i % 3, 3:4], mvs[:, k, i % 3, 2:3]).then_inc(ri_out, 1)
                eng.wait_ge(ri_out, nri[0])
                return mvs[:, k, i % 3, 0:1], mvs[:, k, i % 3, 3:4]

            nst = [0]

            def stat(k, i, src, done):
                nst[0] += 1
                eng.bn_stats(s6[:, k, :], src).then_inc(st_a, 1)
                eng.wait_ge(st_a, nst[0])
                eng.bn_aggr(mvs[:, k, i % 3, 0:2], s6[:, k, :]).then_inc(done, 1)

            for j in range(NT + 9):
                if j < NT:
                    i = j
                    eng.wait_ge(zq_done, i + 1)
                    if i == 0:
                        eng.wait_ge(b0t_out, 3)
                    if i >= 5:
                        eng.wait_ge(t1_done, i - 4)
                    eng.tensor_tensor(ZS[i % 5], bank[i % 2][:, 0:D], b0t[:, :], ALU.add).then_inc(zs_out, 1)
                    eng.wait_ge(zs_out, i + 1)
                    eng.tensor_tensor(SQ, ZS[i % 5], ZS[i % 5], ALU.mult).then_inc(sq_out, 1)
                    eng.wait_ge(sq_out, 2 * i + 1)
                    eng.tensor_reduce(rz[:, i % 3, 0:H], SQ.rearrange("p (h e) -> p h e", h=H), AX.X, ALU.add).then_inc(sq_out, 1)
                i = j - 1
                if 0 <= i < NT:
                    eng.wait_ge(sqz_out, i + 1)
                    eng.reciprocal(rz[:, i % 3, 0:H], rz[:, i % 3, H:2 * H]).then_inc(rz_out, 1)
                    eng.wait_ge(rz_out, i + 1)
                    z3 = ZS[i % 5].rearrange("p (h e) -> p h e", h=H)
                    eng.tensor_tensor(z3, z3, rz[:, i % 3, 0:H].unsqueeze(2).broadcast_to([P, H, HD]), ALU.mult).then_inc(zn_out, 1)
                i = j - 2
                if 0 <= i < NT:
                    eng.wait_ge(y_out, i + 1)
                    stat(0, i, ZS[i % 5], st_y)
                i = j - 3
                if 0 <= i < NT:
                    eng.wait_ge(sd_y, i + 1)
                    m, r = inv(0, i)
                    eng.tensor_scalar(ZS[i % 5], ZS[i % 5], m, r, ALU.subtract, ALU.mult).then_inc(yn_out, 1)
                i = j - 4
                if 0 <= i < NT:
                    eng.wait_ge(wo_done, i + 1)
                    stat(1, i, bank[2][:, 0:D], st_t)
                    eng.wait_ge(sd_t, i + 1)
                    m, r = inv(1, i)
                    if i >= 2:
                        eng.wait_ge(t2_done, i - 1)
                    eng.tensor_scalar(TN[i % 2], bank[2][:, 0:D], m, r, ALU.subtract, ALU.mult).then_inc(tn_out, 1)
                i = j - 6
                if 0 <= i < NT:
                    eng.wait_ge(up_done, i + 1)
                    eng.wait_ge(hb_out, i + 1)
                    eng.tensor_tensor(h2[:, i, :], bank[3][:, 0:D], h2[:, i, :], ALU.add).then_inc(h2_out, 1)
                    eng.wait_ge(h2_out, i + 1)
                    stat(2, i, h2[:, i, :], st_h)
                i = j - 7
                if 0 <= i < NT:
                    eng.wait_ge(sd_h, i + 1)
                    m, r = inv(2, i)
                    if i >= 3:
                        eng.wait_ge(xn_st[i % 3], 16 * (i // 3))
                        eng.wait_ge(t3_done, i - 2)
                    eng.tensor_scalar(XN[i % 3], h2[:, i, :], m, r, ALU.subtract, ALU.mult).then_inc(xn2_out, 1)
                i = j - 8
                if 0 <= i < NT:
                    eng.wait_ge(rt_done, i + 1)
                    eng.tensor_copy(LG[:, i, :], bank[4][:, 0:NR]).then_inc(lg_out, 1)

            nd = [0]

            def step(ins):
                nd[0] += 1
                ins.then_inc(rt_dve, 1)
                eng.wait_ge(rt_dve, nd[0])

            def bc(t, n=E):
                return t.unsqueeze(2).broadcast_to([P, NT, n])

            w8b = w8.unsqueeze(1).broadcast_to([P, NT, E])
            eng.wait_ge(zq_done, NT)
            eng.wait_ge(lg_out, NT)
            step(eng.tensor_tensor(sq24, LG[:, :, 2 * E:NR], LG[:, :, 2 * E:NR], ALU.mult))
            step(eng.tensor_reduce(nrm[:, 0, :], sq24, AX.X, ALU.add))
            assert nd[0] == RD["nsq"]
            eng.wait_ge(rt_act, 1)
            step(eng.tensor_scalar(nrm[:, 1, :], nrm[:, 1, :], 1e-12, None, ALU.max))
            step(eng.reciprocal(nrm[:, 2, :], nrm[:, 1, :]))
            step(eng.tensor_tensor(al8, LG[:, :, E:2 * E], bc(nrm[:, 2, :]), ALU.mult))
            step(eng.scalar_tensor_tensor(Lg, al8, 0.02, LG[:, :, 0:E], ALU.mult, ALU.add))
            step(eng.tensor_tensor(Lg, Lg, ebias[:, :].unsqueeze(1).broadcast_to([P, NT, E]), ALU.add))
            eng.wait_ge(rc_out, 14)
            for c, (L, oh) in enumerate(((Lg, oh1), (L2t, oh2))):
                step(eng.tensor_reduce(mx[:, c, :], L, AX.X, ALU.max))
                step(eng.tensor_tensor(eqt, L, bc(mx[:, c, :]), ALU.is_equal))
                step(eng.tensor_tensor(sct, eqt, w8b, ALU.mult))
                step(eng.tensor_reduce(cs[:, c, :], sct, AX.X, ALU.max))
                step(eng.tensor_tensor(oh, w8b, bc(cs[:, c, :]), ALU.is_equal))
                if c == 0:
                    step(eng.scalar_tensor_tensor(L2t, oh1, -1e30, Lg, ALU.mult, ALU.add))
            step(eng.tensor_tensor(oha, oh1, oh2, ALU.add))
            step(eng.tensor_reduce(cnt, oha.rearrange("p i e -> p e i"), AX.X, ALU.add))
            assert nd[0] == RD["cnt"]
            step(eng.tensor_tensor(gt[:, 3, :], mx[:, 1, :], mx[:, 0, :], ALU.subtract))
            assert nd[0] == RD["d"]
            eng.wait_ge(rt_pe, 1)
            step(eng.tensor_tensor(tlm, bank[0][:, 0:E].unsqueeze(2).broadcast_to([P, E, NT]),
                                   i41[:, 0:NT].unsqueeze(1).broadcast_to([P, E, NT]), ALU.is_gt))
            step(eng.tensor_reduce(tl, tlm, AX.X, ALU.add))
            step(eng.tensor_tensor(bmt, tl.unsqueeze(1).broadcast_to([P, E, E]), emask, ALU.mult))
            step(eng.tensor_reduce(bs[:, 0:E], bmt, AX.X, ALU.add))
            step(eng.tensor_tensor(bs[:, E:2 * E], bs[:, 0:E], tl, ALU.add))
            step(eng.tensor_scalar(bs[:, :], bs[:, :], float(P), None, ALU.mult))
            eng.wait_ge(rt_pe, 2)
            step(eng.tensor_tensor(P8, bank[1][:, 0:NI].rearrange("p (i e) -> p i e", e=E),
                                   bs[:, 0:E].unsqueeze(1).broadcast_to([P, NT, E]), ALU.add))
            for c, oh in enumerate((oh1, oh2)):
                step(eng.tensor_tensor(sct, oh, P8, ALU.mult))
                step(eng.tensor_reduce(pos[:, NT * c:NT * (c + 1)], sct, AX.X, ALU.add))
            eng.wait_ge(rt_act, 2)
            step(eng.tensor_scalar(gt[:, 3, :], gt[:, 2, :], 1.0, None, ALU.add))
            step(eng.reciprocal(gt[:, 0, :], gt[:, 3, :]))
            step(eng.tensor_tensor(gt[:, 1, :], gt[:, 2, :], gt[:, 0, :], ALU.mult))
            J2 = 2 * NT
            step(eng.tensor_tensor(ge, pos.unsqueeze(2).broadcast_to([P, J2, SLOTS + 1]),
                                   i41.unsqueeze(1).broadcast_to([P, J2, SLOTS + 1]), ALU.is_ge))
            step(eng.tensor_reduce(slot_, ge[:, :, 1:SLOTS + 1], AX.X, ALU.add))
            step(eng.tensor_tensor(av[:, :, 0, :], ge[:, :, 0:SLOTS], ge[:, :, 1:SLOTS + 1], ALU.subtract))
            step(eng.scalar_tensor_tensor(row_, slot_, -float(P), pos, ALU.mult, ALU.add))
            step(eng.tensor_tensor(av[:, :, 1, :], av[:, :, 0, :],
                                   gt[:, 0:2, :].rearrange("p c i -> p (c i)").unsqueeze(2).broadcast_to([P, J2, SLOTS]), ALU.mult))
            for c in range(2):
                step(eng.tensor_tensor(av[:, NT * c:NT * (c + 1), 0, :], av[:, NT * c:NT * (c + 1), 0, :],
                                       tokid.unsqueeze(2).broadcast_to([P, NT, SLOTS]), ALU.mult))
            for q in range(4):
                step(eng.tensor_tensor(Bh[:, 8 * q:8 * q + 8, :], irow.unsqueeze(1).broadcast_to([P, 8, P]),
                                       row_[:, 8 * q:8 * q + 8].unsqueeze(2).broadcast_to([P, 8, P]), ALU.is_equal))
                assert nd[0] == RD["B"] + q
            step(eng.tensor_tensor(exm, i41[:, 0:SLOTS].unsqueeze(2).broadcast_to([P, SLOTS, E]),
                                   bs[:, E:2 * E].unsqueeze(1).broadcast_to([P, SLOTS, E]), ALU.is_ge))
            step(eng.tensor_reduce(lst[:, 2, :], exm, AX.X, ALU.add))
            step(eng.tensor_scalar(lst[:, 2, :], lst[:, 2, :], float(E - 1), None, ALU.min))
            step(eng.tensor_copy(ex[:, :], lst[:, 2, :]))
            eng.wait_ge(rt_pe, 3)
            step(eng.tensor_copy(lst[:, 0:2, :], bank[2][:, 0:2 * SLOTS].rearrange("p (v k) -> p v k", v=2)))
            step(eng.tensor_copy(gates[:, :], lst[:, 1, :]))
            step(eng.tensor_scalar(lst[:, 3, :], lst[:, 0, :], 0.0, None, ALU.is_equal))
            step(eng.tensor_scalar(lst[:, 3, :], lst[:, 3, :], trash, None, ALU.mult))
            step(eng.scalar_tensor_tensor(lst[:, 0, :], lst[:, 0, :], -1.0, lst[:, 3, :], ALU.add, ALU.add))
            eng.tensor_copy(idx[:, :], lst[:, 0, :]).then_inc(idx_out, 1)

            def relu(s):
                for m in range(2):
                    eng.wait_ge(l1_done, 2 * s + m + 1)
                    if m == 0 and not (isinstance(s, int) and s == 0):
                        eng.wait_ge(hid_done, 2 * s)
                    eng.tensor_scalar(RL[:, HID // 2 * m:HID // 2 * (m + 1)], bank[m][:, 0:HID // 2], 0.0, None, ALU.max).then_inc(relu_out, 1)

            def y_evac(s, k, g):
                eng.wait_ge(l2_done, s + 1)
                if not (isinstance(g, int) and g == 0):
                    eng.wait_ge(y_add, 64 * g)
                eng.tensor_scalar(YO[k], bank[7][:, 0:D], gates[:, ds(s, 1)], None, ALU.mult).then_inc(yo_out, 1)

            def results(g, last):
                for k in range(4):
                    if not (last and k == 3):
                        relu(4 * g + k + 1)
                    y_evac(4 * g + k, k, g)

            relu(0)
            results(0, False)
            with eng.Fori(1, SLOTS // 4 - 1) as g:
                results(g, False)
            results(SLOTS // 4 - 1, True)



def kernel(**inputs):
    import numpy as np
    import concourse.bacc as bacc
    from concourse.bass_utils import run_bass_kernel_spmd as run

    nc = bacc.Bacc("TRN2", target_bir_lowering=False, num_devices=1)
    arrays, io = {}, {}
    for name, a in inputs.items():
        a = np.ascontiguousarray(a)
        arrays["in_" + name] = a
        io[name] = nc.dram_tensor("in_" + name, a.shape, mybir.dt.from_np(a.dtype), kind="ExternalInput").ap()
    B, T, D = inputs["x"].shape
    out = nc.dram_tensor("out_0", (B, (T + 3) // 4 * 2, D), F32, kind="ExternalOutput").ap()
    audio_tower_kernel(nc, io, out)
    r = run(nc, [arrays], core_ids=[0])
    return r.results[0]["out_0"]
```

```python
from contextlib import ExitStack

import concourse.bass as bass
from concourse import mybir
from concourse.bass import IndirectOffsetOnAxis, ds

F32 = mybir.dt.float32
I32 = mybir.dt.int32
ALU = mybir.AluOpType
ACT = mybir.ActivationFunctionType
AX = mybir.AxisListType


def audio_tower_kernel(nc, io, out):
    B, T_IN, D = io["x"].shape
    SEG = 128
    S = SEG // 2
    H, HD = io["L0_attn_ttt_g"].shape
    E, _, HID = io["L0_ffn_w_fast1"].shape
    DR = io["L0_ffn_probe_w"].shape[0]
    P = 128
    NT = B * S // P
    R = B * H
    KB = D - P
    S_IN = (T_IN + 1) // 2
    BLK = 8
    NB = S // BLK
    G4 = 4
    NG = B * S // 512

    with ExitStack() as ctx:
        def sb(name, shape, dt=F32):
            return ctx.enter_context(nc.sbuf_tensor(name, shape, dt))

        def dram(name, shape, dt=F32):
            return nc.dram_tensor(name, shape, dt, kind="Internal").ap()

        sems = {}

        def sem(name):
            sems[name] = ctx.enter_context(nc.semaphore(name))
            return sems[name]

        arena = sb("arena", [P, 48128])
        at = 0

        def cut(n):
            nonlocal at
            at += n
            return arena[:, at - n:at]

        X = cut(NT * D)
        KQM = cut(R * 2 * S)
        GW = cut(R * HD)
        CC = cut(S * HD)
        MN = cut(S * 2 * BLK)
        W1A = cut(E * HID)
        W1B = cut(E * HID)
        W2 = cut(E * HID // P * D)
        xs = X.rearrange("p (i d) -> p i d", d=D)
        hmix = CC[:, 0:NT * D].rearrange("p (i d) -> p i d", d=D)
        xnTs = W2[:, 0:2 * NT * P].rearrange("p (i c t) -> p i c t", c=2, t=P)
        hTa = W2[:, 2 * NT * P:3 * NT * P]
        hTb = W2[0:KB + 1, 3 * NT * P:4 * NT * P]
        vk = W2[:, 0:NT * D].rearrange("p (i d) -> p i d", d=D)
        Wd = [MN[:, 0:D], MN[KB:P, D:2 * D]]
        qst = X[:, 2048:2048 + 4 * D].rearrange("p (i d) -> p i d", d=D)
        xT_sb = [KQM[:, k * 2 * P:(k + 1) * 2 * P] for k in range(2)]
        Sm = [KQM[:, 512 + k * P:512 + (k + 1) * P] for k in range(2)]
        Ex = [KQM[:, 768 + k * P:768 + (k + 1) * P] for k in range(2)]
        ExT = [KQM[:, 1024 + k * P:1024 + (k + 1) * P] for k in range(2)]
        kqm = KQM.rearrange("p (r c t) -> p r c t", c=2, t=S)
        gw = GW.rearrange("p (r e) -> p r e", e=HD)

        far_sb = X[0:R, 0:32 * HD]
        ablk = [X[0:R, 2048 + 512 * k:2048 + 512 * (k + 1)] for k in range(2)]
        mn = MN[0:R, :].rearrange("p (s w) -> p s w", w=2 * BLK)
        cc = CC[0:R, :].rearrange("p (t e) -> p t e", e=HD)

        PRS = sb("PRS", [P, 2 * 14 * HD])
        PR = [PRS[:, 14 * HD * k:14 * HD * (k + 1)].rearrange("p (n e) -> p n e", e=HD) for k in range(2)]
        Wkq = [PRS[:, 0:2 * D].rearrange("p (h c e) -> p h c e", h=H, c=2),
               PRS[0:KB, 2 * D:4 * D].rearrange("p (h c e) -> p h c e", h=H, c=2)]
        NQV = 2 * D + H
        Wqv = [PRS[:, 4 * D:4 * D + NQV], PRS[0:KB + 1, 4 * D + NQV:4 * D + 2 * NQV]]
        Gst = sb("Gst", [R, 4, HD])
        U = sb("U", [R, 2, HD])
        JK = sb("JK", [R, HD])
        PG = sb("PG", [R, HD])
        PC = sb("PC", [R, HD])
        Wv_ = sb("Wv_", [R, HD])
        M2 = sb("M2", [R, 2, HD])
        MY = sb("MY", [R, 2, 2 * BLK])
        sc = sb("sc", [R, 8])
        usum = sb("usum", [R, 2])
        UC = sb("UC", [R, HD])
        y1 = sb("y1", [R, 2])
        eta96 = sb("eta96", [R, S])
        b0r = sb("b0r", [R, HD])
        b0m = sb("b0m", [R, 2])
        g2r = sb("g2r", [R, HD])
        ident = sb("ident", [P, P])
        maskbd = KQM[:, 1280:1280 + P]
        negc = sb("negc", [S, S])
        mv = sb("mv", [P, NT, 2])
        st6 = sb("st6", [P, 2, 6])
        rowm = sb("rowm", [P, NT])
        negm = sb("negm", [P, NT])
        esum = sb("esum", [P, NT])
        rinv = sb("rinv", [P, NT])
        std0 = sb("std0", [P, NT])
        rstd0 = sb("rstd0", [P, NT])
        epsc = sb("epsc", [P, 3])
        bdc = sb("bdc", [P, 2])
        etal = sb("etal", [P, H, NT])
        etaT = X[0:H * NT, 2048 + 4 * D:2048 + 4 * D + P]
        w0h = sb("w0h", [HD, H, HD])
        w0m = sb("w0m", [HD, H])
        cmean = sb("cmean", [P, 3 * NT])
        gtok = sb("gtok", [P, D])
        btok = sb("btok", [P, D])

        def tiles(region, at, n, w=D):
            return [region[:, at + w * k:at + w * (k + 1)] for k in range(n)]

        ZS = tiles(X, 0, 5)
        TN = tiles(X, 960, 2)
        XN = tiles(X, 1344, 3)
        tT1 = tiles(X, 1920, 2, 2 * P)
        tT2 = tiles(X, 2432, 2, 2 * P)
        tT3 = tiles(MN, 0, 2, 2 * P)
        QR = tiles(MN, 512, 2)
        h2 = hmix
        Wo = [PRS[:, 0:D], PRS[KB:P, D:2 * D]]
        Wu = [PRS[:, 2 * D:3 * D], PRS[KB:P, 3 * D:4 * D]]
        SQ = PRS[:, 768:768 + D]
        bup = PRS[:, 960:960 + D]
        b0t = sb("b0t", [P, D])
        gcol = sb("gcol", [P, 2, 4])
        emb = sb("emb", [E, DR + 4])
        enT = sb("enT", [DR, E])
        rw = sb("rw", [E, D])
        pw = sb("pw", [DR, D])
        ones8 = sb("ones8", [E, P])
        dg8 = sb("dg8", [E, E])
        dgj = sb("dgj", [E, DR])
        Wr = sb("Wr", [P, 2, 2 * E + DR])
        NR = 2 * E + DR
        LG = CC[:, NT * D:NT * (D + NR)].rearrange("p (i n) -> p i n", n=NR)
        rz = sb("rz", [P, 3, 2 * H])
        mvs = sb("mvs", [P, 3, 3, 4])
        s6 = sb("s6", [P, 3, 6])

        w1a = W1A.rearrange("p (e n) -> p e n", n=HID)
        w1b = W1B.rearrange("p (e n) -> p e n", n=HID)
        KH = HID // P
        w2 = W2.rearrange("p (e k d) -> p e k d", k=KH, d=D)
        mg = sb("mg", [P, 2, E])
        ebias = sb("ebias", [P, E])
        TK = 2
        SLOTS = TK * B * S // P + E
        NI = NT * E
        ka = 0

        def kcut(n):
            nonlocal ka
            ka += n
            return KQM[:, ka - n:ka]

        def rv(n=E):
            return kcut(NT * n).rearrange("p (i e) -> p i e", e=n)
        sq24, Lg, al8, eqt, sct, oh1, oh2, oha, L2t, gsel = rv(DR), rv(), rv(), rv(), rv(), rv(), rv(), rv(), rv(), rv()
        P8 = rv()
        nrm = kcut(3 * NT).rearrange("p (k i) -> p k i", k=3)
        mx = kcut(2 * NT).rearrange("p (c i) -> p c i", c=2)
        cs = kcut(2 * NT).rearrange("p (c i) -> p c i", c=2)
        gt = kcut(4 * NT).rearrange("p (c i) -> p c i", c=4)
        pos = kcut(2 * NT)
        slot_ = kcut(2 * NT)
        row_ = kcut(2 * NT)
        ge = kcut(2 * NT * (SLOTS + 1)).rearrange("p (j k) -> p j k", k=SLOTS + 1)
        av = kcut(2 * NT * 2 * SLOTS).rearrange("p (j v k) -> p j v k", v=2, k=SLOTS)
        Bh = kcut(2 * NT * P).rearrange("p (j r) -> p j r", r=P)
        cnt = kcut(E)
        tlm = kcut(E * NT).rearrange("p (e k) -> p e k", k=NT)
        tl = kcut(E)
        bmt = kcut(E * E).rearrange("p (a b) -> p a b", b=E)
        bs = kcut(2 * E)
        exm = kcut(SLOTS * E).rearrange("p (k e) -> p k e", e=E)
        lst = kcut(4 * SLOTS).rearrange("p (v k) -> p v k", v=4)
        ga = 0

        def gcut(n):
            nonlocal ga
            ga += n
            return GW[:, ga - n:ga]
        w8 = gcut(E)
        irow = gcut(P)
        i41 = gcut(SLOTS + 1)
        tokid = gcut(NT)
        tri = gcut(P)
        ones = gcut(P)
        emask = gcut(E * E).rearrange("p (a b) -> p a b", b=E)
        trash = gcut(1)
        XG = [gcut(2 * P) for k in range(4)]
        xgT = gcut(2 * P)
        RL = gcut(HID)
        HT2 = gcut(HID)
        YO = [gcut(D) for k in range(4)]
        b2r = gcut(E * D)
        idx = sb("idx", [P, SLOTS], I32)
        ex = sb("ex", [P, SLOTS], I32)
        gates = sb("gates", [P, SLOTS])
        fat = sb("fat", [P, E])

        bank = [ctx.enter_context(nc.psum_tensor(f"bank{k}", [P, 512], F32)) for k in range(8)]

        hmix_d = dram("hmix_d", (NT * P, D))
        q_d = dram("q_d", (NT * P, D))
        c_d = dram("c_d", (NT * P, D))
        km_d = dram("km_d", (S, R, S))
        xn_d = dram("xn_d", (NT * P + P, D))
        acc_d = dram("acc_d", (NT * P + P, D))

        consts = sem("consts")
        x_zero = sem("x_zero")
        x_in = [sem(f"x_in{c}") for c in range(4)]
        w_in = sem("w_in")
        xT_done = sem("xT_done")
        xT_out = sem("xT_out")
        s_done = sem("s_done")
        mx_out = sem("mx_out")
        negm_out = sem("negm_out")
        exp_out = sem("exp_out")
        rinv_out = sem("rinv_out")
        eT_done = sem("eT_done")
        eT_out = sem("eT_out")
        o_done = sem("o_done")
        h_out = sem("h_out")
        stat_a = sem("stat_a")
        stat_b = sem("stat_b")
        std_out = sem("std_out")
        rstd_out = sem("rstd_out")
        xn_out = sem("xn_out")
        hmix_st = sem("hmix_st")
        xnT_done = sem("xnT_done")
        xnT_out = sem("xnT_out")
        hd_done = sem("hd_done")
        hT_out = sem("hT_out")
        wprep = sem("wprep")
        kq_done = sem("kq_done")
        k_out = sem("k_out")
        q_out = sem("q_out")
        qv_done = sem("qv_done")
        qt_out = sem("qt_out")
        vk_out = sem("vk_out")
        q_st = [sem(f"q_st{k}") for k in range(4)]
        eta_done = sem("eta_done")
        eta_out = sem("eta_out")
        gram_done = sem("gram_done")
        km_out = sem("km_out")
        qm_out = sem("qm_out")
        c_chain = sem("c_chain")
        c_out = sem("c_out")
        rows_in = sem("rows_in")
        w0_out = sem("w0_out")
        b0_out = sem("b0_out")
        gw_rep = sem("gw_rep")
        km_st = sem("km_st")
        mn_zero = sem("mn_zero")
        mn_in = sem("mn_in")
        mnb_in = sem("mnb_in")
        mnb_out = sem("mnb_out")
        mne_out = sem("mne_out")
        eta_in = sem("eta_in")
        c_st = sem("c_st")
        c_in = sem("c_in")
        rt_in = sem("rt_in")
        rt_prep = sem("rt_prep")
        rt_mm = sem("rt_mm")
        b0t_out = sem("b0t_out")
        post_w = sem("post_w")
        h_in = sem("h_in")
        hb_out = sem("hb_out")
        qr_in = [sem(f"qr_in{k}") for k in range(2)]
        qb_out = sem("qb_out")
        zq_done = sem("zq_done")
        zs_out = sem("zs_out")
        sq_out = sem("sq_out")
        sqz_out = sem("sqz_out")
        rz_out = sem("rz_out")
        zn_out = sem("zn_out")
        yg_out = sem("yg_out")
        y_out = sem("y_out")
        st_a = sem("st_a")
        st_y = sem("st_y")
        st_t = sem("st_t")
        st_h = sem("st_h")
        sd_y = sem("sd_y")
        sd_t = sem("sd_t")
        sd_h = sem("sd_h")
        ri_out = sem("ri_out")
        yn_out = sem("yn_out")
        tn_out = sem("tn_out")
        xn2_out = sem("xn2_out")
        t1_done = sem("t1_done")
        t2_done = sem("t2_done")
        t3_done = sem("t3_done")
        t1_out = sem("t1_out")
        t2_out = sem("t2_out")
        t3_out = sem("t3_out")
        wo_done = sem("wo_done")
        up_done = sem("up_done")
        h2_out = sem("h2_out")
        rt_done = sem("rt_done")
        lg_out = sem("lg_out")
        xn_st = [sem(f"xn_st{k}") for k in range(3)]
        w1b_zero = sem("w1b_zero")
        w1_in = sem("w1_in")
        w2_in = sem("w2_in")
        w_sc = sem("w_sc")
        w_acc = sem("w_acc")
        eb_out = sem("eb_out")
        rc_out = sem("rc_out")
        z_st = sem("z_st")
        b2_in = sem("b2_in")
        rt_dve = sem("rt_dve")
        rt_act = sem("rt_act")
        rt_pe = sem("rt_pe")
        idx_out = sem("idx_out")
        acc_st = sem("acc_st")
        xg_in = [sem(f"xg_in{k}") for k in range(4)]
        xgT_done = sem("xgT_done")
        xgT_out = sem("xgT_out")
        l1_done = sem("l1_done")
        relu_out = sem("relu_out")
        hid_done = sem("hid_done")
        hid_out = sem("hid_out")
        l2_done = sem("l2_done")
        yb_out = sem("yb_out")
        yo_out = sem("yo_out")
        y_add = sem("y_add")
        out_st = sem("out_st")
        u_out = sem("u_out")
        v_step = sem("v_step")
        uc_out = sem("uc_out")
        rr_out = sem("rr_out")
        r_out = sem("r_out")
        my_out = sem("my_out")
        m2_out = sem("m2_out")
        prb_out = sem("prb_out")
        pr_out = sem("pr_out")
        g_out = sem("g_out")
        g_in = [sem(f"g_in{k}") for k in range(4)]
        grp_done = sem("grp_done")
        nxt_done = sem("nxt_done")
        far_done = sem("far_done")
        far_out = sem("far_out")
        a_in = [sem(f"a_in{t}") for t in range(BLK)]
        block = ctx.enter_context(nc.Block())

        SC = float(D) ** -0.5

        def grp_count(t):
            return 1 + (BLK - 2) * (t // BLK) + t % BLK + 1

        SP1, SP2 = 4, 7
        NGR = R // 4 // NG

        def gram_row(m):
            g, n = divmod(m, NGR)
            return 32 * (n // 2) + 8 * g + 4 * (n % 2)

        RD = {"nsq": 2, "cnt": 20, "d": 21, "B": 43}

        @block.gpsimd
        def _(eng):
            eng.memset(ident[:, :], 0.0).then_inc(consts, 1)
            eng.memset(maskbd[:, :], 0.0).then_inc(consts, 1)
            eng.memset(negc[:, :], -1.0).then_inc(consts, 1)
            eng.wait_ge(consts, 3)
            eng.affine_select(out=ident[:, :], in_=ident[:, :], compare_op=ALU.not_equal, fill=1.0,
                              base=0, pattern=[[-1, P]], channel_multiplier=1).then_inc(consts, 1)
            eng.wait_ge(consts, 4)
            eng.memset(maskbd[0:S, S:P], -1e30).then_inc(consts, 1)
            eng.memset(maskbd[S:P, 0:S], -1e30).then_inc(consts, 1)
            eng.wait_ge(consts, 6)
            eng.affine_select(out=negc[:, :], in_=negc[:, :], compare_op=ALU.is_ge, fill=0.0,
                              base=0, pattern=[[1, S]], channel_multiplier=-1).then_inc(consts, 1)
            eng.wait_ge(consts, 7)
            eng.memset(W1B[KB:P, :], 0.0).then_inc(w1b_zero, 1)
            eng.wait_ge(w1b_zero, 1)
            eng.wait_ge(w0_out, 3)
            for h in range(H):
                eng.tensor_copy(gw[0:HD, 32 * h:32 * h + 32, :],
                                w0h[:, h, :].unsqueeze(1).broadcast_to([HD, 32, HD])).then_inc(gw_rep, 1)
            eng.wait_ge(gw_rep, 3)
            eng.wait_ge(hd_done, 2 * NG)
            eng.memset(MN, 0.0).then_inc(mn_zero, 1)

            eng.wait_ge(qv_done, NT)
            for k in range(2):
                eng.memset(PR[k][:, :, :], 0.0).then_inc(gw_rep, 1)
            eng.wait_ge(mne_out, 1)
            eng.wait_ge(mnb_in, 16 * (NB - 2))
            eng.tensor_tensor(mn[:, 2 * BLK:S, :], mn[:, 2 * BLK:S, :],
                              eta96[:, 2 * BLK:S].unsqueeze(2).broadcast_to([R, S - 2 * BLK, 2 * BLK]), ALU.mult).then_inc(mnb_out, 1)

            def add_w1(c, n, half):
                w = io["L0_ffn_" + n][2 * c:2 * c + 2]
                if half == 0:
                    eng.wait_ge(w_sc, 8 * (c + 1))
                    eng.dma_start(w1a[:, 2 * c:2 * c + 2, :], w[:, 0:P, :].rearrange("e p n -> p e n"), accum_op=ALU.add).then_inc(w_acc, 16)
                else:
                    eng.dma_start(w1b[0:KB, 2 * c:2 * c + 2, :], w[:, P:D, :].rearrange("e p n -> p e n"), accum_op=ALU.add).then_inc(w_acc, 16)

            def add_w2(c, n, half):
                e = 2 * c + half
                eng.wait_ge(w_sc, 32 + 6 * (c + 1))
                eng.dma_start(w2[:, e, :, :], io["L0_ffn_" + n][e].rearrange("(k p) d -> p k d", p=P), accum_op=ALU.add).then_inc(w_acc, 16)

            for t in range(S):
                J, i = divmod(t, BLK)
                if J < NB - 1:
                    first = max(0, i + 2 - BLK)
                    n = BLK - first
                    eng.wait_ge(m2_out, t + 1)
                    eng.wait_ge(my_out, 2 * (t + 1))
                    if t >= 2:
                        eng.wait_ge(nxt_done, t - 1)
                    eng.tensor_tensor(PR[t % 2][0:R, BLK - 2:BLK - 2 + n, :],
                                      M2[:, t % 2, :].unsqueeze(1).broadcast_to([R, n, HD]),
                                      MY[:, t % 2, BLK + first:2 * BLK].unsqueeze(2).broadcast_to([R, n, HD]),
                                      ALU.mult).then_inc(prb_out, 1)
                for c in range(4):
                    for half in range(2):
                        if t == 8 * c + 9 + half:
                            add_w1(c, "w_fast1", half)
                        if t == 8 * c + 14 + half:
                            if half == 0:
                                eng.wait_ge(w_acc, 16 * (4 * c + 2))
                            add_w1(c, "h_fast1", half)
                        if t == 6 * c + 39 + half:
                            add_w2(c, "w_fast2", half)
                        if t == 6 * c + 42 + half:
                            if half == 0:
                                eng.wait_ge(w_acc, 16 * (16 + 4 * c + 2))
                            add_w2(c, "h_fast2", half)

            eng.wait_ge(h_in, 32)

            def y_tile(i):
                k = i % 2
                eng.wait_ge(qr_in[k], 16 * (i // 2 + 1))
                eng.tensor_tensor(QR[k], QR[k], btok[:, :], ALU.add).then_inc(qb_out, 1)
                eng.wait_ge(zn_out, i + 1)
                eng.tensor_tensor(ZS[i % 5], ZS[i % 5], gtok[:, :], ALU.mult).then_inc(yg_out, 1)
                eng.wait_ge(yg_out, i + 1)
                eng.wait_ge(qb_out, i + 1)
                eng.tensor_tensor(ZS[i % 5], ZS[i % 5], QR[k], ALU.add).then_inc(y_out, 1)

            for i in range(NT):
                eng.tensor_tensor(h2[:, i, :], h2[:, i, :], bup, ALU.add).then_inc(hb_out, 1)
                y_tile(i)

            eng.wait_ge(zq_done, NT)
            eng.iota(w8, [[-1, E]], base=E, channel_multiplier=0, allow_small_or_imprecise_dtypes=True).then_inc(rc_out, 1)
            eng.iota(irow, [[1, P]], base=0, channel_multiplier=0, allow_small_or_imprecise_dtypes=True).then_inc(rc_out, 1)
            eng.iota(i41, [[P, SLOTS + 1]], base=0, channel_multiplier=0, allow_small_or_imprecise_dtypes=True).then_inc(rc_out, 1)
            eng.iota(tokid, [[P, NT]], base=1, channel_multiplier=1, allow_small_or_imprecise_dtypes=True).then_inc(rc_out, 1)
            eng.iota(trash, [[1, 1]], base=NT * P + 1, channel_multiplier=1, allow_small_or_imprecise_dtypes=True).then_inc(rc_out, 1)
            eng.memset(tri, 1.0).then_inc(rc_out, 1)
            eng.memset(ones, 1.0).then_inc(rc_out, 1)
            eng.memset(emask, 1.0).then_inc(rc_out, 1)
            for k in range(4):
                eng.memset(XG[k], 0.0).then_inc(rc_out, 1)
            eng.wait_ge(rc_out, 12)
            eng.affine_select(out=tri, in_=tri, compare_op=ALU.is_gt, fill=0.0, base=0, pattern=[[1, P]],
                              channel_multiplier=-1).then_inc(rc_out, 1)
            eng.affine_select(out=emask, in_=emask, compare_op=ALU.is_gt, fill=0.0, base=0, pattern=[[1, E], [-1, E]],
                              channel_multiplier=0).then_inc(rc_out, 1)
            for k in range(4):
                eng.memset(XG[k][:, D:D + 1], 1.0).then_inc(rc_out, 1)

            def gather(s):
                if s >= 4:
                    eng.wait_ge(xgT_done, s - 3)
                eng.indirect_dma_start(out=XG[s % 4][:, 0:D], out_offset=None, in_=xn_d,
                                       in_offset=IndirectOffsetOnAxis(ap=idx[:, s:s + 1], axis=0)).then_inc(xg_in[s % 4], 16)

            def add(s):
                eng.wait_ge(yo_out, s + 1)
                if s >= 1:
                    eng.wait_ge(y_add, 16 * s)
                eng.indirect_dma_start(out=acc_d, out_offset=IndirectOffsetOnAxis(ap=idx[:, s:s + 1], axis=0), in_=YO[s % 4],
                                       in_offset=None, compute_op=ALU.add).then_inc(y_add, 16)

            eng.wait_ge(rc_out, 18)
            eng.wait_ge(idx_out, 1)
            eng.wait_ge(z_st, 32)
            for k in range(3):
                eng.wait_ge(xn_st[k], 16 * len(range(k, NT, 3)))
            for s in range(4):
                gather(s)
            eng.wait_ge(acc_st, 16)
            for s in range(SLOTS):
                add(s)
                if s + 4 < SLOTS:
                    gather(s + 4)
        CONSTS = 7

        @block.sync
        def _(eng):
            for c in range(4):
                eng.wait_ge(x_zero, c + 1)
                for b2 in range(2):
                    src = io["x"].rearrange("(i b) t d -> b t i d", b=2)[b2, 0:T_IN:2, 4 * c:4 * c + 4, :]
                    eng.dma_start(xs[S * b2:S * b2 + S_IN, 4 * c:4 * c + 4, :], src).then_inc(x_in[c], 16)
            for a, r in ((0, slice(0, P)), (1, slice(P, D))):
                eng.dma_start(Wd[a], io["L0_attn_W_down"][r, :]).then_inc(w_in, 16)
                for c, n in ((0, "Wk"), (1, "Wq")):
                    eng.dma_start(Wkq[a][:, :, c, :], io["L0_attn_" + n][r, :].rearrange("k (h e) -> k h e", h=H)).then_inc(w_in, 16)
                n = r.stop - r.start
                eng.dma_start(Wqv[a][0:n, 0:D], io["L0_attn_Wq"][r, :]).then_inc(w_in, 16)
                eng.dma_start(Wqv[a][0:n, D:2 * D], io["L0_attn_Wv"][r, :]).then_inc(w_in, 16)
                eng.dma_start(Wqv[a][0:n, 2 * D:NQV], io["L0_attn_lr_w"][r, :]).then_inc(w_in, 16)
                eng.dma_start(bdc[0:n, a:a + 1], io["L0_attn_b_down"][r].rearrange("(k o) -> k o", o=1)).then_inc(w_in, 16)
            eng.wait_ge(wprep, 3)
            eng.dma_start(Wqv[1][KB:KB + 1, 2 * D:NQV], io["L0_attn_lr_b"].rearrange("(o k) -> o k", o=1)).then_inc(w_in, 16)
            eng.dma_start(gtok[:, :], io["L0_attn_ttt_g"].rearrange("h e -> (h e)").partition_broadcast(P)).then_inc(w_in, 16)
            eng.dma_start(btok[:, :], io["L0_attn_ttt_b"].rearrange("h e -> (h e)").partition_broadcast(P)).then_inc(w_in, 16)
            eng.dma_start(w0h[:, :, :], io["L0_attn_W1"].rearrange("h d e -> d h e")).then_inc(rows_in, 16)
            for h in range(H):
                rows = slice(32 * h, 32 * h + 32)
                eng.dma_start(b0r[rows, :], io["L0_attn_b1"][h, 0, :].partition_broadcast(32)).then_inc(rows_in, 16)
                eng.dma_start(g2r[rows, :], io["L0_attn_ttt_g"][h, :].partition_broadcast(32)).then_inc(rows_in, 16)
            eng.dma_start(b0t[:, :], io["L0_attn_b1"].rearrange("h o e -> (o h e)").partition_broadcast(P)).then_inc(rt_in, 16)
            eng.dma_start(emb[:, 0:DR], io["L0_ffn_router_emb"]).then_inc(rt_in, 16)
            eng.dma_start(rw[:, :], io["L0_ffn_router_w"]).then_inc(rt_in, 16)
            eng.dma_start(pw[:, :], io["L0_ffn_probe_w"]).then_inc(rt_in, 16)
            for c, n in enumerate(("post_g", "post_b", "norm_g", "norm_b")):
                for k in range(2):
                    eng.dma_start(gcol[:, k, c:c + 1], io["L0_attn_" + n][KB * k:KB * k + P].rearrange("(k o) -> k o", o=1)).then_inc(rt_in, 16)
            for k in range(2):
                eng.dma_start(mg[:, k, :], io[f"L0_ffn_m_gate{k + 1}"].partition_broadcast(P)).then_inc(rt_in, 16)
            eng.dma_start(ebias[:, :], io["L0_ffn_energy"].partition_broadcast(P)).then_inc(rt_in, 16)
            eng.dma_start(fat[:, :], io["L0_ffn_fatigue"].partition_broadcast(P)).then_inc(rt_in, 16)
            eng.wait_ge(w1b_zero, 1)
            eng.dma_start(W1B[KB:KB + 1, :], io["L0_ffn_b1"].rearrange("e (o n) -> o (e n)", o=1)).then_inc(rt_in, 16)
            for c in range(4):
                e2 = slice(2 * c, 2 * c + 2)
                eng.dma_start(w1a[:, e2, :], io["L0_ffn_w_slow1"][e2, 0:P, :].rearrange("e p n -> p e n")).then_inc(w1_in, 16)
                eng.dma_start(w1b[0:KB, e2, :], io["L0_ffn_w_slow1"][e2, P:D, :].rearrange("e p n -> p e n")).then_inc(w1_in, 16)
            eng.wait_ge(h_out, NT)
            eng.dma_start(hmix_d.rearrange("(i p) d -> p i d", p=P), hmix).then_inc(hmix_st, 16)
            def spread(J, t0, t1):
                eng.wait_ge(far_out, 4 * (J + 1))
                if J >= 2:
                    eng.wait_ge(grp_done, grp_count(BLK * (J - 2) + BLK - 3))
                for t in range(t0, t1):
                    eng.dma_start(ablk[J % 2][:, HD * t:HD * (t + 1)], far_sb[t:R:32, :]).then_inc(a_in[t], 16)

            cdv = c_d.rearrange("(i p) d -> p i d", p=P)
            for g in range(NG):
                for i in range(4 * g, 4 * g + 4):
                    eng.wait_ge(qt_out, i + 1)
                    eng.dma_start(q_d[i * P:(i + 1) * P, :], qst[:, i % 4, :]).then_inc(q_st[i % 4], 16)
                if g == NG - 1:
                    for k in range(4):
                        eng.wait_ge(q_st[k], 16 * NT // 4)
                    spread(0, 0, BLK)
                    eng.wait_ge(eta_out, 1)
                    eng.dma_start(eta96[:, :], etaT).then_inc(eta_in, 16)
                eng.wait_ge(c_out, g + 1)
                eng.dma_start(cdv[:, 4 * g:4 * g + 4, :], vk[:, 4 * g:4 * g + 4, :]).then_inc(c_st, 16)
                for h in range(H):
                    rows = slice(32 * h + 8 * g, 32 * h + 8 * g + 8)
                    eng.wait_ge(km_out, NGR * g + 2 * (h + 1))
                    eng.dma_start(km_d[:, rows, :], kqm[HD:P, rows, 0, :]).then_inc(km_st, 16)
                if g == 0:
                    eng.wait_ge(hmix_st, 16)
                eng.wait_ge(c_st, 16 * (g + 1))
                for h in range(H):
                    rows = slice(32 * h + 8 * g, 32 * h + 8 * g + 8)
                    eng.dma_start(cc[rows, :, :],
                                  c_d.rearrange("(b t) (h e) -> h b t e", t=S, h=H)[h, 8 * g:8 * g + 8]).then_inc(c_in, 16)
            eng.wait_ge(km_st, 16 * H * NG)
            eng.wait_ge(mn_zero, 1)
            for J in range(NB):
                n = min(2 * BLK, S - BLK * J)
                eng.dma_start(mn[:, BLK * J:BLK * (J + 1), 0:n],
                              km_d[BLK * J:BLK * (J + 1), :, BLK * J:BLK * J + n].rearrange("s r w -> r s w")).then_inc(mn_in if J < 2 else mnb_in, 16)
            for t in range(S):
                eng.wait_ge(g_out, t + 1)
                eng.dma_start(GW[HD + t:HD + t + 1, :], Gst[:, t % 4, :]).then_inc(g_in[t % 4], 16)
                J = t // BLK
                if t % BLK == 5 and J < NB - 1:
                    spread(J + 1, 0, SP1)
                if t % BLK == 6 and J < NB - 1:
                    spread(J + 1, SP1, SP2)
                if t % BLK == 7 and J < NB - 1:
                    spread(J + 1, SP2, BLK)
                if t < 2 * E and t % 2 == 0:
                    eng.dma_start(w2[:, t // 2, :, :], io["L0_ffn_w_slow2"][t // 2].rearrange("(k p) d -> p k d", p=P)).then_inc(w2_in, 16)
            for k in range(4):
                eng.wait_ge(g_in[k], 16 * S // 4)
            eng.wait_ge(m2_out, S)
            eng.wait_ge(grp_done, grp_count(S - 3))
            for i in range(2):
                eng.dma_start(QR[i], q_d[P * i:P * (i + 1), :]).then_inc(qr_in[i % 2], 16)
            eng.dma_start(bup, io["L0_attn_b_up"].partition_broadcast(P)).then_inc(h_in, 16)
            eng.dma_start(h2, hmix_d.rearrange("(i p) d -> p i d", p=P)).then_inc(h_in, 16)
            for w, n in ((Wo, "Wo"), (Wu, "W_up")):
                eng.dma_start(w[0], io["L0_attn_" + n][0:P, :]).then_inc(post_w, 16)
                eng.dma_start(w[1], io["L0_attn_" + n][P:D, :]).then_inc(post_w, 16)
            for j in range(NT + 7):
                i = j + 2
                if i < NT:
                    eng.wait_ge(y_out, i - 1)
                    eng.dma_start(QR[i % 2], q_d[P * i:P * (i + 1), :]).then_inc(qr_in[i % 2], 16)
                i = j - 7
                if 0 <= i:
                    eng.wait_ge(xn2_out, i + 1)
                    eng.dma_start(xn_d[P * i:P * (i + 1), :], XN[i % 3]).then_inc(xn_st[i % 3], 16)
            eng.dma_start(acc_d[0:NT * P, :].rearrange("(i p) d -> p i d", p=P), h2).then_inc(acc_st, 16)
            eng.wait_ge(zq_done, NT)
            eng.dma_start(b2r, io["L0_ffn_b2"].rearrange("e d -> (e d)").partition_broadcast(P)).then_inc(b2_in, 16)
            eng.wait_ge(rc_out, 12)
            for d in (xn_d, acc_d):
                eng.dma_start(d[NT * P:, :], XG[0][:, 0:D]).then_inc(z_st, 16)
            eng.wait_ge(y_add, 16 * SLOTS)
            eng.dma_start(out.rearrange("b t d -> (b t) d"), acc_d[0:NT * P, :]).then_inc(out_st, 16)
            eng.wait_ge(out_st, 16)
        NW = 7 * 2 + 1 + 2

        @block.tensor
        def _(eng):
            eng.wait_ge(consts, CONSTS)

            def xT(i):
                eng.wait_ge(x_in[i // 4], 32)
                if i >= 2:
                    eng.wait_ge(xT_out, i - 1)
                eng.transpose(bank[i % 2][:, 0:P], xs[:, i, 0:P], ident[:, :])
                eng.transpose(bank[i % 2][:, P:2 * P], xs[:, i, KB:D], ident[:, :]).then_inc(xT_done, 1)

            def scores(i):
                eng.wait_ge(xT_out, i + 1)
                if i >= 2:
                    eng.wait_ge(mx_out, i - 1)
                ps = bank[2 + i % 2][:, 0:P]
                xa, xb = xT_sb[i % 2][:, 0:P], xT_sb[i % 2][KB:P, P:2 * P]
                eng.matmul(ps, xa, xa, start=True, stop=False)
                eng.matmul(ps, xb, xb, start=False, stop=True).then_inc(s_done, 1)

            def eT(i):
                eng.wait_ge(exp_out, i + 1)
                if i >= 2:
                    eng.wait_ge(eT_out, i - 1)
                eng.transpose(bank[4 + i % 2][:, 0:P], Ex[i % 2], ident[:, :]).then_inc(eT_done, 1)

            def mix(i):
                eng.wait_ge(eT_out, i + 1)
                if i >= 2:
                    eng.wait_ge(h_out, i - 1)
                eng.matmul(bank[6 + i % 2][:, 0:D], ExT[i % 2], xs[:, i, :], start=True, stop=True).then_inc(o_done, 1)

            for j in range(NT + 3):
                if j < NT:
                    xT(j)
                if 0 <= j - 1 < NT:
                    scores(j - 1)
                if 0 <= j - 2 < NT:
                    eT(j - 2)
                if 0 <= j - 3 < NT:
                    mix(j - 3)

            def xnT(i):
                eng.wait_ge(xn_out, i + 1)
                if i >= 2:
                    eng.wait_ge(xnT_out, i - 1)
                eng.transpose(bank[i % 2][:, 0:P], xs[:, i, 0:P], ident[:, :])
                eng.transpose(bank[i % 2][:, P:2 * P], xs[:, i, KB:D], ident[:, :]).then_inc(xnT_done, 1)

            def down(g):
                eng.wait_ge(xnT_out, 4 * (g + 1))
                if g == 0:
                    eng.wait_ge(w_in, 16 * NW)
                if g >= 2:
                    eng.wait_ge(far_out, g - 1)
                if g >= 1:
                    eng.wait_ge(hT_out, 2 * g)
                tiles = slice(4 * g, 4 * g + 4)
                for m, (a, b) in enumerate(((0, P), (P, D))):
                    ps = bank[2 + m][0:b - a, :]
                    eng.matmul(ps, Wd[0][:, a:b], xnTs[:, tiles, 0, :], start=True, stop=False)
                    eng.matmul(ps, Wd[1][:, a:b], xnTs[KB:P, tiles, 1, :], start=False, stop=True).then_inc(hd_done, 1)

            for g in range(NG):
                for i in range(4 * g, 4 * g + 4):
                    xnT(i)
                if g == 1 or g == 2:
                    down(g - 1)

            eng.wait_ge(rt_prep, 5)
            eng.transpose(bank[6][0:DR, 0:E], emb[:, 0:DR], ident[0:E, 0:E]).then_inc(rt_mm, 1)

            def router():
                eng.wait_ge(rt_prep, 6)
                for k in range(2):
                    ch = slice(KB * k, KB * k + P)
                    o = NR * k
                    eng.matmul(bank[7][:, o:o + E], rw[:, ch], ident[0:E, 0:E], start=True, stop=False, skip_group_check=True)
                    eng.matmul(bank[7][:, o:o + E], ones8[:, :], dg8[:, :], start=False, stop=True, skip_group_check=True)
                    eng.matmul(bank[7][:, o + E:o + 2 * E], pw[:, ch], enT[:, :], start=True, stop=True, skip_group_check=True)
                    eng.matmul(bank[7][:, o + 2 * E:o + NR], pw[:, ch], ident[0:DR, 0:DR], start=True, stop=True,
                               skip_group_check=True).then_inc(rt_mm, 1)

            def kq(n):
                g, h = divmod(n, H)
                eng.wait_ge(hT_out, 2 * (g + 1))
                if n >= 2:
                    eng.wait_ge(k_out, n - 1)
                    eng.wait_ge(q_out, n - 1)
                cols = slice(512 * g, 512 * (g + 1))
                ps = bank[4 + n % 2]
                eng.matmul(ps[:, :], Wkq[0][:, h, :, :].rearrange("p c e -> p (c e)"), hTa[:, cols], start=True, stop=False)
                eng.matmul(ps[:, :], Wkq[1][:, h, :, :].rearrange("p c e -> p (c e)"), hTb[0:KB, cols], start=False, stop=True).then_inc(kq_done, 1)

            def qv(i):
                if i == 0:
                    eng.wait_ge(wprep, 4)
                if i >= 2:
                    eng.wait_ge(qt_out, i - 1)
                    eng.wait_ge(vk_out, i - 1)
                cols = slice(P * i, P * (i + 1))
                ps = bank[6 + i % 2][:, 0:NQV]
                eng.matmul(ps, hTa[:, cols], Wqv[0], start=True, stop=False)
                eng.matmul(ps, hTb[:, cols], Wqv[1], start=False, stop=True).then_inc(qv_done, 1)

            def grams(m):
                g, n = divmod(m, NGR)
                ps = bank[m % 2]
                if m == 0:
                    eng.wait_ge(xnT_out, NT)
                if m >= 2:
                    eng.wait_ge(qm_out, m - 1)
                for j in range(4):
                    row = gram_row(m) + j
                    mm = eng.matmul(ps[0:S, P * j:P * (j + 1)], kqm[0:HD, row, 0, :],
                                    kqm[0:HD, row, :, :].rearrange("p c t -> p (c t)"), start=True, stop=True)
                mm.then_inc(gram_done, 1)

            def far(J, first, last):
                K = HD + BLK * max(0, J - 1)
                for j in range(first, last):
                    b, h = divmod(j, H)
                    row = 32 * h + b
                    if j % 24 == 0 and J >= 1:
                        eng.wait_ge(far_out, 4 * (J - 1) + j // 24 + 1 if J > 1 else 4)
                    far_bank = bank[2 + b // 8 % 2 if J == 0 else 4 + b // 8]
                    mm = eng.matmul(far_bank[32 * h:32 * h + 32, HD * (b % 8):HD * (b % 8 + 1)],
                                    kqm[0:K, row, 0:2, :].rearrange("p c t -> p (c t)")[:, BLK * J:BLK * J + 32],
                                    gw[0:K, row, :], start=True, stop=True)
                    if j % 24 == 23:
                        mm.then_inc(far_done, 1)

            idr = ident[0:R, 0:R]

            def add_far(a):
                eng.wait_ge(a_in[a % BLK], 16 * (a // BLK + 1))
                return eng.matmul(bank[a // BLK % 2][0:R, HD * (a % BLK):HD * (a % BLK + 1)], idr,
                                  ablk[a // BLK % 2][:, HD * (a % BLK):HD * (a % BLK + 1)],
                                  start=False, stop=False, skip_group_check=True)

            FAR = [0, 24, 48, 72, R, R, R, R, R]

            def open_z(J):
                eng.matmul(bank[J % 2][0:R, :], idr, b0r[:, :].unsqueeze(1).broadcast_to([R, BLK, HD]),
                           start=True, stop=False, skip_group_check=True)

            for g in range(NG):
                for h in range(H):
                    kq(H * g + h)
                if g == 0:
                    router()
                    eng.wait_ge(rt_prep, 7)
                for i in range(4 * g, 4 * g + 4):
                    qv(i)
                eng.wait_ge(k_out, H * (g + 1))
                eng.wait_ge(q_out, H * (g + 1))
                if g == 0:
                    eng.wait_ge(gw_rep, 3)
                eng.wait_ge(hT_out, min(2 * NG, 2 * g + 4))
                if g >= 2:
                    eng.wait_ge(far_out, g - 1)
                far(0, 24 * g, 24 * (g + 1))
                if g == NG - 1:
                    eng.wait_ge(vk_out, NT)
                    eng.transpose(bank[4][0:H * NT, 0:P], etal[:, :, :].rearrange("p h i -> p (h i)"), ident[:, :]).then_inc(eta_done, 1)
                for m in range(NGR * g, NGR * (g + 1)):
                    grams(m)
                if g + 2 < NG:
                    down(g + 2)
            eng.wait_ge(b0_out, 3)
            eng.wait_ge(eta_out, 1)
            eng.wait_ge(gw_rep, 5)
            eng.wait_ge(km_out, R // 4)
            eng.wait_ge(qm_out, R // 4)
            open_z(0)
            for t in range(BLK):
                eng.wait_ge(a_in[t], 16)
            eng.matmul(bank[0][0:R, :], idr, ablk[0], start=False, stop=False, skip_group_check=True).then_inc(grp_done, 1)
            open_z(1)
            for t in range(S - 2):
                J, i = divmod(t, BLK)
                n = max(0, BLK - (i + 2))
                a = t + 2
                if n:
                    eng.wait_ge(pr_out, grp_count(t) - 1)
                    mm = eng.matmul(bank[J % 2][0:R, HD * (i + 2):], ident[:, 0:R], PR[t % 2][:, 0:n, :],
                                    start=False, stop=False, skip_group_check=True)
                    if J >= 1:
                        mm = add_far(a)
                    mm.then_inc(grp_done, 1)
                if J < NB - 1:
                    first = max(0, i + 2 - BLK)
                    if i == BLK - 1:
                        eng.wait_ge(u_out, t + 2)
                    eng.wait_ge(prb_out, t + 1)
                    mm = eng.matmul(bank[(J + 1) % 2][0:R, HD * first:], ident[:, 0:R], PR[t % 2][:, BLK - 2:2 * BLK - 2 - first, :],
                                    start=False, stop=False, skip_group_check=True)
                    if not n:
                        mm = add_far(a)
                    mm.then_inc(nxt_done, 1)
                    if i == BLK - 1 and J + 2 < NB:
                        open_z(J + 2)
                    if i == 0 and J == 0:
                        eng.wait_ge(qm_out, R // 4)
                    if i == 0 and J >= 1:
                        for k in range(4):
                            eng.wait_ge(g_in[k], 16 * (BLK * J // 4))
                    far(J + 1, FAR[i], FAR[i + 1])

            def zq(i):
                if i == 0:
                    for k in range(4):
                        eng.wait_ge(g_in[k], 16 * S // 4)
                    eng.wait_ge(u_out, S)
                if i >= 2:
                    eng.wait_ge(zs_out, i - 1)
                for b2 in range(2):
                    for h in range(H):
                        row = 32 * h + 2 * i + b2
                        mm = eng.matmul(bank[i % 2][S * b2:S * (b2 + 1), HD * h:HD * (h + 1)], kqm[:, row, 1, :], gw[:, row, :],
                                        start=True, stop=True)
                mm.then_inc(zq_done, 1)

            for j in range(NT + 8):
                if j < NT:
                    zq(j)
                i = j - 4
                if 0 <= i < NT:
                    if i == 0:
                        eng.wait_ge(post_w, 64)
                    eng.wait_ge(t1_out, 2 * i + 2)
                    if i >= 1:
                        eng.wait_ge(tn_out, i)
                    eng.matmul(bank[2][:, 0:D], tT1[i % 2][:, 0:P], Wo[0], start=True, stop=False)
                    eng.matmul(bank[2][:, 0:D], tT1[i % 2][KB:P, P:2 * P], Wo[1], start=False, stop=True).then_inc(wo_done, 1)
                i = j - 6
                if 0 <= i < NT:
                    eng.wait_ge(t2_out, 2 * i + 2)
                    if i >= 1:
                        eng.wait_ge(h2_out, i)
                    eng.matmul(bank[3][:, 0:D], tT2[i % 2][:, 0:P], Wu[0], start=True, stop=False)
                    eng.matmul(bank[3][:, 0:D], tT2[i % 2][KB:P, P:2 * P], Wu[1], start=False, stop=True).then_inc(up_done, 1)
                i = j - 8
                if 0 <= i < NT:
                    eng.wait_ge(t3_out, i + 1)
                    if i >= 1:
                        eng.wait_ge(lg_out, i)
                    eng.matmul(bank[4][:, 0:NR], tT3[i % 2][:, 0:P], Wr[:, 0, :], start=True, stop=False)
                    eng.matmul(bank[4][:, 0:NR], tT3[i % 2][KB:P, P:2 * P], Wr[KB:P, 1, :], start=False, stop=True).then_inc(rt_done, 1)
                if 0 <= j - 3 < NT:
                    i = j - 3
                    eng.wait_ge(yn_out, i + 1)
                    if i >= 1:
                        eng.wait_ge(t1_out, 2 * i)
                    eng.transpose(bank[5][:, 0:P], ZS[i % 5][:, 0:P], ident[:, :])
                    eng.transpose(bank[5][:, P:2 * P], ZS[i % 5][:, KB:D], ident[:, :]).then_inc(t1_done, 1)
                if 0 <= j - 5 < NT:
                    i = j - 5
                    eng.wait_ge(tn_out, i + 1)
                    if i >= 1:
                        eng.wait_ge(t2_out, 2 * i)
                    eng.transpose(bank[6][:, 0:P], TN[i % 2][:, 0:P], ident[:, :])
                    eng.transpose(bank[6][:, P:2 * P], TN[i % 2][:, KB:D], ident[:, :]).then_inc(t2_done, 1)
                if 0 <= j - 7 < NT:
                    i = j - 7
                    eng.wait_ge(xn2_out, i + 1)
                    if i >= 1:
                        eng.wait_ge(t3_out, i)
                    eng.transpose(bank[7][:, 0:P], XN[i % 3][:, 0:P], ident[:, :])
                    eng.transpose(bank[7][:, P:2 * P], XN[i % 3][:, KB:D], ident[:, :]).then_inc(t3_done, 1)

            eng.wait_ge(rc_out, 14)
            eng.wait_ge(rt_dve, RD["cnt"])
            eng.matmul(bank[0][:, 0:E], ones, cnt, start=True, stop=True).then_inc(rt_pe, 1)
            eng.matmul(bank[1][:, 0:NI], tri, oha.rearrange("p i e -> p (i e)"), start=True, stop=False, skip_group_check=True)
            for i in range(NT - 1):
                n = NT - 1 - i
                mm = eng.matmul(bank[1][:, E * (i + 1):NI], ones, oha[:, i, :].unsqueeze(1).broadcast_to([P, n, E]),
                                start=False, stop=i == NT - 2, skip_group_check=True)
            mm.then_inc(rt_pe, 1)
            for j in range(2 * NT):
                if j % 8 == 0:
                    eng.wait_ge(rt_dve, RD["B"] + j // 8)
                mm = eng.matmul(bank[2][:, 0:2 * SLOTS], Bh[:, j, :], av[:, j, :, :], start=j == 0, stop=j == 2 * NT - 1)
            mm.then_inc(rt_pe, 1)

            eng.wait_ge(rc_out, 18)
            eng.wait_ge(idx_out, 1)
            eng.wait_ge(w_acc, 16 * 32)

            def x_T(s, k, g):
                eng.wait_ge(xg_in[k], 16 * (g + 1))
                eng.transpose(bank[4][:, 0:P], XG[k][:, 0:P], ident[:, :])
                eng.transpose(bank[4][:, P:2 * P], XG[k][:, P:2 * P], ident[:, :]).then_inc(xgT_done, 1)

            def layer1(s):
                e = eng.value_load(ex[0:1, ds(s, 1)], min_val=0, max_val=E - 1)
                eng.wait_ge(xgT_out, s + 1)
                for m in range(2):
                    ps = bank[m][:, 0:HID // 2]
                    o = HID // 2 * m
                    eng.matmul(ps, xgT[:, 0:P], W1A[:, ds(e * HID + o, HID // 2)], start=True, stop=False)
                    eng.matmul(ps, xgT[:, P:2 * P], W1B[:, ds(e * HID + o, HID // 2)], start=False, stop=True).then_inc(l1_done, 1)

            def layer2(s):
                e = eng.value_load(ex[0:1, ds(s, 1)], min_val=0, max_val=E - 1)
                if not (isinstance(s, int) and s == 0):
                    eng.wait_ge(yb_out, s)
                eng.wait_ge(hid_out, 2 * s + 2)
                for c in range(KH):
                    mm = eng.matmul(bank[7][:, 0:D], HT2[:, P * c:P * (c + 1)], W2[:, ds(e * (KH * D) + D * c, D)],
                                    start=c == 0, stop=c == KH - 1)
                mm.then_inc(l2_done, 1)

            def hid_T(s):
                eng.wait_ge(relu_out, 2 * s + 2)
                for c in range(KH):
                    mm = eng.transpose(bank[5 + c // 3][:, P * (c % 3):P * (c % 3 + 1)], RL[:, P * c:P * (c + 1)], ident[:, :])
                    if c % 3 == 2:
                        mm.then_inc(hid_done, 1)

            def slots(g, first, last):
                for k in range(4):
                    s = 4 * g + k
                    layer1(s)
                    if not (last and k == 3):
                        x_T(s + 1, (k + 1) % 4, g + (k + 1) // 4)
                    if not (first and k == 0):
                        layer2(s - 1)
                    hid_T(s)

            x_T(0, 0, 0)
            slots(0, True, False)
            with eng.Fori(1, SLOTS // 4 - 1) as g:
                slots(g, False, False)
            slots(SLOTS // 4 - 1, False, True)
            layer2(SLOTS - 1)

        @block.scalar
        def _(eng):
            for j in range(NT + 3):
                if j < NT:
                    eng.wait_ge(xT_done, j + 1)
                    if j >= 2:
                        eng.wait_ge(s_done, j - 1)
                    eng.activation(xT_sb[j % 2], bank[j % 2][:, 0:2 * P], ACT.Copy).then_inc(xT_out, 1)
                if 0 <= j - 1 < NT:
                    i = j - 1
                    eng.wait_ge(negm_out, i + 1)
                    if i >= 2:
                        eng.wait_ge(eT_done, i - 1)
                    eng.activation(Ex[i % 2], Sm[i % 2], ACT.Exp, bias=negm[:, i:i + 1], scale=SC,
                                   accum_out=esum[:, i:i + 1]).then_inc(exp_out, 1)
                if 0 <= j - 2 < NT:
                    i = j - 2
                    eng.wait_ge(eT_done, i + 1)
                    if i >= 2:
                        eng.wait_ge(o_done, i - 1)
                    eng.activation(ExT[i % 2], bank[4 + i % 2][:, 0:P], ACT.Copy).then_inc(eT_out, 1)
            eng.wait_ge(stat_b, NT)
            eng.activation(std0[:, :], mv[:, :, 1], ACT.Sqrt, bias=epsc[:, 0:1]).then_inc(std_out, 1)
            eng.wait_ge(rt_prep, 1)
            eng.activation(emb[:, DR + 1:DR + 2], emb[:, DR:DR + 1], ACT.Sqrt).then_inc(std_out, 1)
            def silu(g):
                cols = slice(512 * g, 512 * (g + 1))
                eng.wait_ge(hd_done, 2 * g + 2)
                eng.activation(hTa[:, cols], bank[2][:, :], ACT.Silu, bias=bdc[:, 0:1]).then_inc(hT_out, 1)
                eng.activation(hTb[0:KB, cols], bank[3][0:KB, :], ACT.Silu, bias=bdc[0:KB, 1:2]).then_inc(hT_out, 1)

            for g in range(NG):
                for i in range(4 * g, 4 * g + 4):
                    eng.wait_ge(xnT_done, i + 1)
                    eng.activation(xnTs[:, i, :, :], bank[i % 2][:, 0:2 * P].rearrange("p (c t) -> p c t", c=2), ACT.Copy).then_inc(xnT_out, 1)
                if g == 1 or g == 2:
                    silu(g - 1)
            EV = [2, 3, 4, 5]

            def far_evac(J, k):
                eng.wait_ge(far_done, 4 * J + k + 1)
                if J >= 1:
                    for t in range(BLK):
                        eng.wait_ge(a_in[t], 16 * J)
                src = bank[2 + k % 2 if J == 0 else 4 + k]
                eng.activation(far_sb[:, 512 * k:512 * (k + 1)], src[0:R, :], ACT.Copy).then_inc(far_out, 1)

            for g in range(NG):
                for n in range(H * g, H * g + H):
                    h = n % H
                    eng.wait_ge(kq_done, n + 1)
                    eng.activation(kqm[0:HD, 32 * h + 8 * g:32 * h + 8 * g + 8, 0, :],
                                   bank[4 + n % 2][0:HD, :].rearrange("p (r t) -> p r t", t=S), ACT.Copy).then_inc(k_out, 1)
                for i in range(4 * g, 4 * g + 4):
                    eng.wait_ge(qv_done, i + 1)
                    if i >= 4:
                        eng.wait_ge(q_st[i % 4], 16 * (i // 4))
                    eng.activation(qst[:, i % 4, :], bank[6 + i % 2][:, 0:D], ACT.Copy).then_inc(qt_out, 1)
                far_evac(0, g)
                if g == NG - 1:
                    eng.wait_ge(eta_done, 1)
                    eng.activation(etaT, bank[4][0:H * NT, 0:P], ACT.Sigmoid).then_inc(eta_out, 1)
                for m in range(NGR * g, NGR * (g + 1)):
                    row = gram_row(m)
                    eng.wait_ge(gram_done, m + 1)
                    eng.activation(kqm[HD:P, row:row + 4, 0, :],
                                   bank[m % 2][0:S, :].rearrange("p (r c t) -> p r c t", c=2, t=S)[:, :, 0, :],
                                   ACT.Copy, scale=-1.0, bias=-1.0).then_inc(km_out, 1)
                if g + 2 < NG:
                    silu(g + 2)
            HH = HID // 2
            pieces = []
            for e in range(E):
                for m in range(2):
                    pieces.append((W1A[:, HID * e + HH * m:HID * e + HH * (m + 1)], mg[:, 0, e:e + 1], w1_in))
                for m in range(2):
                    pieces.append((W1B[0:KB, HID * e + HH * m:HID * e + HH * (m + 1)], mg[0:KB, 0, e:e + 1], w1_in))
            for e in range(E):
                for m in range(3):
                    o = KH * D * e + 2 * D * m
                    pieces.append((W2[:, o:o + 2 * D], mg[:, 1, e:e + 1], w2_in))
            eng.wait_ge(rt_in, 16 * 17)

            for t in range(S):
                J, i = divmod(t, BLK)
                eng.wait_ge(u_out, t + 1)
                if t >= 1:
                    eng.wait_ge(m2_out, t)
                eng.activation(UC[:, :], U[:, t % 2, :], ACT.Identity, scale=-float(HD), bias=usum[:, t % 2:t % 2 + 1]).then_inc(uc_out, 1)
                eng.wait_ge(rr_out, t + 1)
                eng.activation(sc[:, 2 + t % 2:3 + t % 2], sc[:, 1:2], ACT.Sqrt).then_inc(r_out, 1)
                if J < NB - 1 and i in EV:
                    far_evac(J + 1, EV.index(i))
                if t < len(pieces):
                    w, m, ready = pieces[t]
                    eng.wait_ge(ready, 16 * E)
                    eng.activation(w, w, ACT.Copy, scale=m).then_inc(w_sc, 1)
                eng.wait_ge(m2_out, t + 1)
                eng.wait_ge(my_out, 2 * (t + 1))
                if t >= 4:
                    eng.wait_ge(g_in[t % 4], 16 * (t // 4))
                eng.activation(Gst[:, t % 4, :], M2[:, t % 2, :], ACT.Copy, scale=y1[:, t % 2:t % 2 + 1]).then_inc(g_out, 1)

            def sd(ready, n, k, i, eps, done):
                eng.wait_ge(ready, i + 1)
                eng.activation(mvs[:, k, i % 3, 2:3], mvs[:, k, i % 3, 1:2], ACT.Sqrt, bias=epsc[:, eps:eps + 1]).then_inc(done, 1)

            for j in range(NT + 8):
                if j < NT:
                    eng.wait_ge(sq_out, 2 * j + 2)
                    eng.activation(rz[:, j % 3, H:2 * H], rz[:, j % 3, 0:H], ACT.Sqrt, bias=epsc[:, 1:2], scale=1.0 / HD).then_inc(sqz_out, 1)
                i = j - 2
                if 0 <= i < NT:
                    sd(st_y, 0, 0, i, 1, sd_y)
                i = j - 4
                if 0 <= i < NT:
                    sd(st_t, 0, 1, i, 1, sd_t)
                i = j - 6
                if 0 <= i < NT:
                    sd(st_h, 0, 2, i, 0, sd_h)
                i = j - 3
                if 0 <= i < NT:
                    eng.wait_ge(t1_done, i + 1)
                    if i >= 2:
                        eng.wait_ge(wo_done, i - 1)
                    for c in range(2):
                        eng.activation(tT1[i % 2][:, P * c:P * (c + 1)], bank[5][:, P * c:P * (c + 1)], ACT.Identity,
                                       scale=gcol[:, c, 0:1], bias=gcol[:, c, 1:2]).then_inc(t1_out, 1)
                i = j - 5
                if 0 <= i < NT:
                    eng.wait_ge(t2_done, i + 1)
                    if i >= 2:
                        eng.wait_ge(up_done, i - 1)
                    for c in range(2):
                        eng.activation(tT2[i % 2][:, P * c:P * (c + 1)], bank[6][:, P * c:P * (c + 1)], ACT.Identity,
                                       scale=gcol[:, c, 2:3], bias=gcol[:, c, 3:4]).then_inc(t2_out, 1)
                i = j - 7
                if 0 <= i < NT:
                    eng.wait_ge(t3_done, i + 1)
                    if i >= 2:
                        eng.wait_ge(rt_done, i - 1)
                    eng.activation(tT3[i % 2], bank[7][:, 0:2 * P], ACT.Copy).then_inc(t3_out, 1)

            eng.wait_ge(rt_dve, RD["nsq"])
            eng.activation(nrm[:, 1, :], nrm[:, 0, :], ACT.Sqrt).then_inc(rt_act, 1)
            eng.wait_ge(rt_dve, RD["d"])
            eng.activation(gt[:, 2, :], gt[:, 3, :], ACT.Exp).then_inc(rt_act, 1)

            def x_out(s):
                eng.wait_ge(xgT_done, s + 1)
                if not (isinstance(s, int) and s == 0):
                    eng.wait_ge(l1_done, 2 * s)
                eng.activation(xgT, bank[4][:, 0:2 * P], ACT.Copy).then_inc(xgT_out, 1)

            def square(s):
                if not (isinstance(s, int) and s == 0):
                    eng.wait_ge(l2_done, s)
                for m in range(2):
                    eng.wait_ge(hid_done, 2 * s + m + 1)
                    eng.activation(HT2[:, HH * m:HH * (m + 1)], bank[5 + m][:, 0:HH], ACT.Square).then_inc(hid_out, 1)

            x_out(0)
            x_out(1)
            square(0)
            with eng.Fori(1, SLOTS - 1) as s:
                x_out(s + 1)
                square(s)
            square(SLOTS - 1)


        @block.vector
        def _(eng):
            for c in range(4):
                eng.memset(X[:, 4 * D * c:4 * D * (c + 1)], 0.0).then_inc(x_zero, 1)
            eng.memset(epsc[:, 1:2], 1e-6)
            eng.memset(epsc[:, 0:1], 1e-5).then_inc(wprep, 1)
            eng.memset(hTb[KB:KB + 1, :], 1.0).then_inc(wprep, 1)
            eng.memset(Wqv[1][KB:KB + 1, :], 0.0).then_inc(wprep, 1)
            for j in range(NT + 3):
                if 0 <= j - 1 < NT:
                    i = j - 1
                    eng.wait_ge(s_done, i + 1)
                    if i >= 2:
                        eng.wait_ge(exp_out, i - 1)
                    if i == 0:
                        eng.wait_ge(consts, CONSTS)
                    eng.tensor_tensor_reduce(Sm[i % 2], bank[2 + i % 2][:, 0:P], maskbd[:, :], 1.0, -3e38,
                                             ALU.add, ALU.max, rowm[:, i:i + 1]).then_inc(mx_out, 1)
                    eng.wait_ge(mx_out, i + 1)
                    eng.tensor_scalar(negm[:, i:i + 1], rowm[:, i:i + 1], -SC, None, ALU.mult).then_inc(negm_out, 1)
                if 0 <= j - 2 < NT:
                    i = j - 2
                    eng.wait_ge(exp_out, i + 1)
                    eng.reciprocal(rinv[:, i:i + 1], esum[:, i:i + 1]).then_inc(rinv_out, 1)
                if 0 <= j - 3 < NT:
                    i = j - 3
                    eng.wait_ge(o_done, i + 1)
                    eng.wait_ge(rinv_out, i + 1)
                    eng.tensor_scalar(hmix[:, i, :], bank[6 + i % 2][:, 0:D], rinv[:, i:i + 1], None, ALU.mult).then_inc(h_out, 1)
                    eng.wait_ge(h_out, i + 1)
                    eng.bn_stats(st6[:, i % 2, :], hmix[:, i, :]).then_inc(stat_a, 1)
                    eng.wait_ge(stat_a, i + 1)
                    eng.bn_aggr(mv[:, i, :], st6[:, i % 2, :]).then_inc(stat_b, 1)
            eng.wait_ge(rows_in, 16 * 7)
            eng.tensor_reduce(w0m[:, :], w0h[:, :, :], AX.X, ALU.add).then_inc(w0_out, 1)
            eng.tensor_reduce(b0m[:, 0:1], b0r[:, :], AX.X, ALU.add).then_inc(b0_out, 1)
            eng.tensor_tensor(g2r[:, :], g2r[:, :], g2r[:, :], ALU.mult)
            eng.wait_ge(w0_out, 1)
            eng.tensor_scalar(w0m[:, :], w0m[:, :], -1.0 / HD, None, ALU.mult).then_inc(w0_out, 1)
            eng.wait_ge(b0_out, 1)
            eng.tensor_scalar(b0m[:, 1:2], b0m[:, 0:1], -1.0 / HD, None, ALU.mult).then_inc(b0_out, 1)
            eng.wait_ge(w0_out, 2)
            eng.tensor_tensor(w0h[:, :, :], w0h[:, :, :], w0m[:, :].unsqueeze(2).broadcast_to([HD, H, HD]), ALU.add).then_inc(w0_out, 1)
            eng.wait_ge(b0_out, 2)
            eng.tensor_scalar(b0r[:, :], b0r[:, :], b0m[:, 1:2], None, ALU.add).then_inc(b0_out, 1)
            eng.wait_ge(rt_in, 16 * 17)
            eng.tensor_tensor_reduce(dgj[:, :], emb[:, 0:DR], emb[:, 0:DR], 1.0, 0.0, ALU.mult, ALU.add, emb[:, DR:DR + 1]).then_inc(rt_prep, 1)
            eng.wait_ge(std_out, 1)
            eng.reciprocal(rstd0[:, :], std0[:, :]).then_inc(rstd_out, 1)
            eng.wait_ge(rstd_out, 1)
            for i in range(NT):
                eng.tensor_scalar(xs[:, i, :], hmix[:, i, :], mv[:, i, 0:1], rstd0[:, i:i + 1],
                                  ALU.subtract, ALU.mult).then_inc(xn_out, 1)
            eng.wait_ge(rt_in, 16 * 17)
            eng.tensor_scalar(fat[:, :], fat[:, :], -0.1, None, ALU.mult).then_inc(eb_out, 1)
            eng.wait_ge(eb_out, 1)
            eng.scalar_tensor_tensor(ebias[:, :], ebias[:, :], 0.1, fat[:, :], ALU.mult, ALU.add).then_inc(eb_out, 1)
            eng.wait_ge(std_out, 2)
            eng.tensor_scalar(emb[:, DR + 2:DR + 3], emb[:, DR + 1:DR + 2], 0.02 / D, 0.02 / D, ALU.mult, ALU.add).then_inc(rt_prep, 1)
            eng.tensor_scalar(emb[:, DR + 3:DR + 4], emb[:, DR + 1:DR + 2], 1e-12, None, ALU.max).then_inc(rt_prep, 1)
            eng.memset(ones8[:, :], 1.0)
            eng.wait_ge(rt_prep, 3)
            eng.reciprocal(emb[:, DR + 3:DR + 4], emb[:, DR + 3:DR + 4]).then_inc(rt_prep, 1)
            eng.tensor_scalar(dg8[:, :], ident[0:E, 0:E], emb[:, DR + 2:DR + 3], None, ALU.mult)
            eng.wait_ge(rt_prep, 4)
            eng.tensor_scalar(emb[:, 0:DR], emb[:, 0:DR], emb[:, DR + 3:DR + 4], None, ALU.mult).then_inc(rt_prep, 1)
            eng.wait_ge(w_in, 16 * NW)
            for a, n in ((0, P), (1, KB)):
                w = Wqv[a][0:n, D:2 * D].rearrange("p (h e) -> p h e", h=H)
                ins = eng.tensor_tensor(w, w, Wkq[a][:, :, 0, :], ALU.subtract)
            ins.then_inc(wprep, 1)
            eng.wait_ge(rt_mm, 1)
            eng.tensor_copy(enT[:, :], bank[6][0:DR, 0:E]).then_inc(rt_prep, 1)
            for g in range(NG):
                for n in range(H * g, H * g + H):
                    h = n % H
                    eng.wait_ge(kq_done, n + 1)
                    eng.tensor_copy(kqm[0:HD, 32 * h + 8 * g:32 * h + 8 * g + 8, 1, :],
                                    bank[4 + n % 2][HD:P, :].rearrange("p (r t) -> p r t", t=S)).then_inc(q_out, 1)
                if g == 0:
                    eng.wait_ge(rt_mm, 3)
                    eng.tensor_copy(Wr[:, :, :].rearrange("p c n -> p (c n)"), bank[7][:, 0:2 * NR]).then_inc(rt_prep, 1)
                for i in range(4 * g, 4 * g + 4):
                    eng.wait_ge(qv_done, i + 1)
                    if i % 4 == 0:
                        eng.wait_ge(hd_done, 2 * (g + 1))
                    eng.wait_ge(qt_out, i + 1)
                    eng.tensor_copy(etal[:, :, i], bank[6 + i % 2][:, 2 * D:NQV])
                    eng.tensor_tensor(vk[:, i, :], btok[:, :], bank[6 + i % 2][:, D:2 * D], ALU.subtract).then_inc(vk_out, 1)
                for n in range(NGR):
                    m = NGR * g + n
                    row = gram_row(m)
                    eng.wait_ge(gram_done, m + 1)
                    eng.wait_ge(km_out, m + 1)
                    eng.scalar_tensor_tensor(kqm[HD:P, row:row + 4, 1, :],
                                             bank[m % 2][0:S, :].rearrange("p (r c t) -> p r c t", c=2, t=S)[:, :, 1, :],
                                             1.0, negc[:, :].unsqueeze(1).broadcast_to([S, 4, S]),
                                             ALU.add, ALU.mult).then_inc(qm_out, 1)
                    v = vk[:, 4 * g:4 * g + 4, :]
                    vh = v.rearrange("p i (h e) -> p (i h) e", h=H)
                    cm = cmean[:, 12 * g:12 * g + 12]
                    if n == 0:
                        eng.wait_ge(vk_out, 4 * g + 4)
                        eng.tensor_tensor(v, v, gtok[:, :].unsqueeze(1).broadcast_to([P, 4, D]), ALU.mult).then_inc(c_chain, 1)
                    elif n == 1:
                        eng.wait_ge(c_chain, 3 * g + 1)
                        eng.tensor_reduce(cm, vh, AX.X, ALU.add).then_inc(c_chain, 1)
                    elif n == 2:
                        eng.wait_ge(c_chain, 3 * g + 2)
                        eng.tensor_scalar(cm, cm, 1.0 / HD, None, ALU.mult).then_inc(c_chain, 1)
                    elif n == 4 and g == 0:
                        b0v = b0t[:, :].rearrange("p (h e) -> p h e", h=H)
                        eng.wait_ge(c_out, 1)
                        eng.tensor_reduce(cmean[:, 0:H], b0v, AX.X, ALU.add).then_inc(b0t_out, 1)
                        eng.wait_ge(b0t_out, 1)
                        eng.tensor_scalar(cmean[:, 0:H], cmean[:, 0:H], 1.0 / HD, None, ALU.mult).then_inc(b0t_out, 1)
                        eng.wait_ge(b0t_out, 2)
                        eng.tensor_tensor(b0v, b0v, cmean[:, 0:H].unsqueeze(2).broadcast_to([P, H, HD]), ALU.subtract).then_inc(b0t_out, 1)
                    elif n == 3:
                        eng.wait_ge(c_chain, 3 * g + 3)
                        eng.tensor_tensor(vh, vh, cm.unsqueeze(2).broadcast_to([P, 12, HD]), ALU.subtract).then_inc(c_out, 1)

            eng.wait_ge(eta_in, 16)
            eng.tensor_scalar(eta96[:, :], eta96[:, :], 1.0 / HD, None, ALU.mult).then_inc(mne_out, 1)
            eng.wait_ge(mne_out, 1)
            eng.wait_ge(mn_in, 16 * 2)
            S2 = 2 * BLK
            eng.tensor_tensor(mn[:, 0:S2, :], mn[:, 0:S2, :], eta96[:, 0:S2].unsqueeze(2).broadcast_to([R, S2, 2 * BLK]), ALU.mult).then_inc(mne_out, 1)
            eng.wait_ge(mne_out, 2)
            eng.wait_ge(gw_rep, 5)
            eng.wait_ge(c_in, 16 * H * NG)

            def z_next(t):
                J, i = divmod(t, BLK)
                z = bank[J % 2][0:R, HD * i:HD * (i + 1)]
                if J >= 1 and i <= 1:
                    eng.wait_ge(nxt_done, t - 1)
                else:
                    eng.wait_ge(grp_done, grp_count(t - 2) if i >= 2 else 1)
                if t == 0:
                    eng.tensor_scalar(U[:, 0, :], z, 1.0, None, ALU.mult, ALU.add, accum_out=usum[:, 0:1]).then_inc(u_out, 1)
                    return
                ip = (t - 1) % BLK
                eng.wait_ge(m2_out, t)
                eng.scalar_tensor_tensor(U[:, t % 2, :], M2[:, (t - 1) % 2, :], MY[:, (t - 1) % 2, ip + 1:ip + 2], z,
                                         ALU.mult, ALU.add, accum_out=usum[:, t % 2:t % 2 + 1]).then_inc(u_out, 1)

            z_next(0)
            for t in range(S):
                J, i = divmod(t, BLK)
                u = U[:, t % 2, :]
                if t >= 1:
                    n = BLK - ((t - 1) % BLK + 2)
                    if n > 0:
                        if t >= 3 and (t - 3) % BLK < BLK - 2:
                            eng.wait_ge(grp_done, grp_count(t - 3))
                        j0 = (t - 1) % BLK + 2
                        eng.tensor_tensor(PR[(t - 1) % 2][0:R, 0:n, :],
                                          M2[:, (t - 1) % 2, :].unsqueeze(1).broadcast_to([R, n, HD]),
                                          MY[:, (t - 1) % 2, j0:j0 + n].unsqueeze(2).broadcast_to([R, n, HD]),
                                          ALU.mult).then_inc(pr_out, 1)
                eng.wait_ge(u_out, t + 1)
                eng.tensor_tensor_reduce(JK[:, :], u, u, 1.0 / HD, 1e-6, ALU.mult, ALU.add, sc[:, 0:1]).then_inc(v_step, 1)
                eng.wait_ge(v_step, 6 * t + 1)
                eng.reciprocal(sc[:, 1:2], sc[:, 0:1]).then_inc(rr_out, 1)
                eng.tensor_tensor_reduce(PG[:, :], u, g2r[:, :], 1.0, 0.0, ALU.mult, ALU.add, sc[:, 4:5]).then_inc(v_step, 1)
                eng.wait_ge(v_step, 6 * t + 2)
                eng.scalar_tensor_tensor(PC[:, :], sc[:, 4:5].broadcast_to([R, HD]), -1.0 / HD, PG[:, :],
                                         ALU.mult, ALU.add).then_inc(v_step, 1)
                eng.wait_ge(v_step, 6 * t + 3)
                eng.wait_ge(r_out, t + 1)
                r = sc[:, 2 + t % 2:3 + t % 2]
                eng.scalar_tensor_tensor(Wv_[:, :], PC[:, :], r, cc[:, t, :], ALU.mult, ALU.add).then_inc(v_step, 1)
                if t >= 2:
                    eng.wait_ge(g_out, t - 1)
                    if t - 2 < BLK * (NB - 1):
                        eng.wait_ge(prb_out, t - 1)
                if t == S2:
                    eng.wait_ge(mnb_out, 1)
                eng.tensor_tensor(MY[:, t % 2, :], mn[:, t, :], r.broadcast_to([R, 2 * BLK]), ALU.mult).then_inc(my_out, 1)
                eng.wait_ge(v_step, 6 * t + 4)
                eng.tensor_tensor_reduce(JK[:, :], Wv_[:, :], u, 1.0 / HD ** 2, 0.0, ALU.mult, ALU.add, sc[:, 5:6]).then_inc(v_step, 1)
                eng.tensor_tensor(y1[:, t % 2:t % 2 + 1], eta96[:, t:t + 1], r, ALU.mult).then_inc(my_out, 1)
                eng.wait_ge(v_step, 6 * t + 5)
                eng.tensor_tensor(sc[:, 6:7], sc[:, 5:6], sc[:, 1:2], ALU.mult).then_inc(v_step, 1)
                eng.wait_ge(v_step, 6 * t + 6)
                eng.wait_ge(uc_out, t + 1)
                eng.scalar_tensor_tensor(M2[:, t % 2, :], UC[:, :], sc[:, 6:7], Wv_[:, :], ALU.mult, ALU.add).then_inc(m2_out, 1)
                if t + 1 < S:
                    z_next(t + 1)

            nri = [0]

            def inv(k, i):
                nri[0] += 1
                eng.reciprocal(mvs[:, k, i % 3, 3:4], mvs[:, k, i % 3, 2:3]).then_inc(ri_out, 1)
                eng.wait_ge(ri_out, nri[0])
                return mvs[:, k, i % 3, 0:1], mvs[:, k, i % 3, 3:4]

            nst = [0]

            def stat(k, i, src, done):
                nst[0] += 1
                eng.bn_stats(s6[:, k, :], src).then_inc(st_a, 1)
                eng.wait_ge(st_a, nst[0])
                eng.bn_aggr(mvs[:, k, i % 3, 0:2], s6[:, k, :]).then_inc(done, 1)

            for j in range(NT + 9):
                if j < NT:
                    i = j
                    eng.wait_ge(zq_done, i + 1)
                    if i == 0:
                        eng.wait_ge(b0t_out, 3)
                    if i >= 5:
                        eng.wait_ge(t1_done, i - 4)
                    eng.tensor_tensor(ZS[i % 5], bank[i % 2][:, 0:D], b0t[:, :], ALU.add).then_inc(zs_out, 1)
                    eng.wait_ge(zs_out, i + 1)
                    eng.tensor_tensor(SQ, ZS[i % 5], ZS[i % 5], ALU.mult).then_inc(sq_out, 1)
                    eng.wait_ge(sq_out, 2 * i + 1)
                    eng.tensor_reduce(rz[:, i % 3, 0:H], SQ.rearrange("p (h e) -> p h e", h=H), AX.X, ALU.add).then_inc(sq_out, 1)
                i = j - 1
                if 0 <= i < NT:
                    eng.wait_ge(sqz_out, i + 1)
                    eng.reciprocal(rz[:, i % 3, 0:H], rz[:, i % 3, H:2 * H]).then_inc(rz_out, 1)
                    eng.wait_ge(rz_out, i + 1)
                    z3 = ZS[i % 5].rearrange("p (h e) -> p h e", h=H)
                    eng.tensor_tensor(z3, z3, rz[:, i % 3, 0:H].unsqueeze(2).broadcast_to([P, H, HD]), ALU.mult).then_inc(zn_out, 1)
                i = j - 2
                if 0 <= i < NT:
                    eng.wait_ge(y_out, i + 1)
                    stat(0, i, ZS[i % 5], st_y)
                i = j - 3
                if 0 <= i < NT:
                    eng.wait_ge(sd_y, i + 1)
                    m, r = inv(0, i)
                    eng.tensor_scalar(ZS[i % 5], ZS[i % 5], m, r, ALU.subtract, ALU.mult).then_inc(yn_out, 1)
                i = j - 4
                if 0 <= i < NT:
                    eng.wait_ge(wo_done, i + 1)
                    stat(1, i, bank[2][:, 0:D], st_t)
                    eng.wait_ge(sd_t, i + 1)
                    m, r = inv(1, i)
                    if i >= 2:
                        eng.wait_ge(t2_done, i - 1)
                    eng.tensor_scalar(TN[i % 2], bank[2][:, 0:D], m, r, ALU.subtract, ALU.mult).then_inc(tn_out, 1)
                i = j - 6
                if 0 <= i < NT:
                    eng.wait_ge(up_done, i + 1)
                    eng.wait_ge(hb_out, i + 1)
                    eng.tensor_tensor(h2[:, i, :], bank[3][:, 0:D], h2[:, i, :], ALU.add).then_inc(h2_out, 1)
                    eng.wait_ge(h2_out, i + 1)
                    stat(2, i, h2[:, i, :], st_h)
                i = j - 7
                if 0 <= i < NT:
                    eng.wait_ge(sd_h, i + 1)
                    m, r = inv(2, i)
                    if i >= 3:
                        eng.wait_ge(xn_st[i % 3], 16 * (i // 3))
                        eng.wait_ge(t3_done, i - 2)
                    eng.tensor_scalar(XN[i % 3], h2[:, i, :], m, r, ALU.subtract, ALU.mult).then_inc(xn2_out, 1)
                i = j - 8
                if 0 <= i < NT:
                    eng.wait_ge(rt_done, i + 1)
                    eng.tensor_copy(LG[:, i, :], bank[4][:, 0:NR]).then_inc(lg_out, 1)

            nd = [0]

            def step(ins):
                nd[0] += 1
                ins.then_inc(rt_dve, 1)
                eng.wait_ge(rt_dve, nd[0])

            def bc(t, n=E):
                return t.unsqueeze(2).broadcast_to([P, NT, n])

            w8b = w8.unsqueeze(1).broadcast_to([P, NT, E])
            eng.wait_ge(zq_done, NT)
            eng.wait_ge(lg_out, NT)
            step(eng.tensor_tensor(sq24, LG[:, :, 2 * E:NR], LG[:, :, 2 * E:NR], ALU.mult))
            step(eng.tensor_reduce(nrm[:, 0, :], sq24, AX.X, ALU.add))
            assert nd[0] == RD["nsq"]
            eng.wait_ge(rt_act, 1)
            step(eng.tensor_scalar(nrm[:, 1, :], nrm[:, 1, :], 1e-12, None, ALU.max))
            step(eng.reciprocal(nrm[:, 2, :], nrm[:, 1, :]))
            step(eng.tensor_tensor(al8, LG[:, :, E:2 * E], bc(nrm[:, 2, :]), ALU.mult))
            step(eng.scalar_tensor_tensor(Lg, al8, 0.02, LG[:, :, 0:E], ALU.mult, ALU.add))
            step(eng.tensor_tensor(Lg, Lg, ebias[:, :].unsqueeze(1).broadcast_to([P, NT, E]), ALU.add))
            eng.wait_ge(rc_out, 14)
            for c, (L, oh) in enumerate(((Lg, oh1), (L2t, oh2))):
                step(eng.tensor_reduce(mx[:, c, :], L, AX.X, ALU.max))
                step(eng.tensor_tensor(eqt, L, bc(mx[:, c, :]), ALU.is_equal))
                step(eng.tensor_tensor(sct, eqt, w8b, ALU.mult))
                step(eng.tensor_reduce(cs[:, c, :], sct, AX.X, ALU.max))
                step(eng.tensor_tensor(oh, w8b, bc(cs[:, c, :]), ALU.is_equal))
                if c == 0:
                    step(eng.scalar_tensor_tensor(L2t, oh1, -1e30, Lg, ALU.mult, ALU.add))
            step(eng.tensor_tensor(oha, oh1, oh2, ALU.add))
            step(eng.tensor_reduce(cnt, oha.rearrange("p i e -> p e i"), AX.X, ALU.add))
            assert nd[0] == RD["cnt"]
            step(eng.tensor_tensor(gt[:, 3, :], mx[:, 1, :], mx[:, 0, :], ALU.subtract))
            assert nd[0] == RD["d"]
            eng.wait_ge(rt_pe, 1)
            step(eng.tensor_tensor(tlm, bank[0][:, 0:E].unsqueeze(2).broadcast_to([P, E, NT]),
                                   i41[:, 0:NT].unsqueeze(1).broadcast_to([P, E, NT]), ALU.is_gt))
            step(eng.tensor_reduce(tl, tlm, AX.X, ALU.add))
            step(eng.tensor_tensor(bmt, tl.unsqueeze(1).broadcast_to([P, E, E]), emask, ALU.mult))
            step(eng.tensor_reduce(bs[:, 0:E], bmt, AX.X, ALU.add))
            step(eng.tensor_tensor(bs[:, E:2 * E], bs[:, 0:E], tl, ALU.add))
            step(eng.tensor_scalar(bs[:, :], bs[:, :], float(P), None, ALU.mult))
            eng.wait_ge(rt_pe, 2)
            step(eng.tensor_tensor(P8, bank[1][:, 0:NI].rearrange("p (i e) -> p i e", e=E),
                                   bs[:, 0:E].unsqueeze(1).broadcast_to([P, NT, E]), ALU.add))
            for c, oh in enumerate((oh1, oh2)):
                step(eng.tensor_tensor(sct, oh, P8, ALU.mult))
                step(eng.tensor_reduce(pos[:, NT * c:NT * (c + 1)], sct, AX.X, ALU.add))
            eng.wait_ge(rt_act, 2)
            step(eng.tensor_scalar(gt[:, 3, :], gt[:, 2, :], 1.0, None, ALU.add))
            step(eng.reciprocal(gt[:, 0, :], gt[:, 3, :]))
            step(eng.tensor_tensor(gt[:, 1, :], gt[:, 2, :], gt[:, 0, :], ALU.mult))
            J2 = 2 * NT
            step(eng.tensor_tensor(ge, pos.unsqueeze(2).broadcast_to([P, J2, SLOTS + 1]),
                                   i41.unsqueeze(1).broadcast_to([P, J2, SLOTS + 1]), ALU.is_ge))
            step(eng.tensor_reduce(slot_, ge[:, :, 1:SLOTS + 1], AX.X, ALU.add))
            step(eng.tensor_tensor(av[:, :, 0, :], ge[:, :, 0:SLOTS], ge[:, :, 1:SLOTS + 1], ALU.subtract))
            step(eng.scalar_tensor_tensor(row_, slot_, -float(P), pos, ALU.mult, ALU.add))
            step(eng.tensor_tensor(av[:, :, 1, :], av[:, :, 0, :],
                                   gt[:, 0:2, :].rearrange("p c i -> p (c i)").unsqueeze(2).broadcast_to([P, J2, SLOTS]), ALU.mult))
            for c in range(2):
                step(eng.tensor_tensor(av[:, NT * c:NT * (c + 1), 0, :], av[:, NT * c:NT * (c + 1), 0, :],
                                       tokid.unsqueeze(2).broadcast_to([P, NT, SLOTS]), ALU.mult))
            for q in range(4):
                step(eng.tensor_tensor(Bh[:, 8 * q:8 * q + 8, :], irow.unsqueeze(1).broadcast_to([P, 8, P]),
                                       row_[:, 8 * q:8 * q + 8].unsqueeze(2).broadcast_to([P, 8, P]), ALU.is_equal))
                assert nd[0] == RD["B"] + q
            step(eng.tensor_tensor(exm, i41[:, 0:SLOTS].unsqueeze(2).broadcast_to([P, SLOTS, E]),
                                   bs[:, E:2 * E].unsqueeze(1).broadcast_to([P, SLOTS, E]), ALU.is_ge))
            step(eng.tensor_reduce(lst[:, 2, :], exm, AX.X, ALU.add))
            step(eng.tensor_scalar(lst[:, 2, :], lst[:, 2, :], float(E - 1), None, ALU.min))
            step(eng.tensor_copy(ex[:, :], lst[:, 2, :]))
            eng.wait_ge(rt_pe, 3)
            step(eng.tensor_copy(lst[:, 0:2, :], bank[2][:, 0:2 * SLOTS].rearrange("p (v k) -> p v k", v=2)))
            step(eng.tensor_copy(gates[:, :], lst[:, 1, :]))
            step(eng.tensor_scalar(lst[:, 3, :], lst[:, 0, :], 0.0, None, ALU.is_equal))
            step(eng.tensor_scalar(lst[:, 3, :], lst[:, 3, :], trash, None, ALU.mult))
            step(eng.scalar_tensor_tensor(lst[:, 0, :], lst[:, 0, :], -1.0, lst[:, 3, :], ALU.add, ALU.add))
            eng.tensor_copy(idx[:, :], lst[:, 0, :]).then_inc(idx_out, 1)

            def relu(s):
                for m in range(2):
                    eng.wait_ge(l1_done, 2 * s + m + 1)
                    if m == 0 and not (isinstance(s, int) and s == 0):
                        eng.wait_ge(hid_done, 2 * s)
                    eng.tensor_scalar(RL[:, HID // 2 * m:HID // 2 * (m + 1)], bank[m][:, 0:HID // 2], 0.0, None, ALU.max).then_inc(relu_out, 1)

            def y_evac(s, k, g):
                e = eng.value_load(ex[0:1, ds(s, 1)], min_val=0, max_val=E - 1)
                if not (isinstance(g, int) and g == 0):
                    eng.wait_ge(y_add, 64 * g)
                eng.wait_ge(l2_done, s + 1)
                eng.tensor_tensor(YO[k], bank[7][:, 0:D], b2r[:, ds(e * D, D)], ALU.add).then_inc(yb_out, 1)
                eng.wait_ge(yb_out, s + 1)
                eng.tensor_scalar(YO[k], YO[k], gates[:, ds(s, 1)], None, ALU.mult).then_inc(yo_out, 1)

            def results(g, last):
                for k in range(4):
                    if not (last and k == 3):
                        relu(4 * g + k + 1)
                    y_evac(4 * g + k, k, g)

            relu(0)
            eng.wait_ge(b2_in, 16)
            results(0, False)
            with eng.Fori(1, SLOTS // 4 - 1) as g:
                results(g, False)
            results(SLOTS // 4 - 1, True)



def kernel(**inputs):
    import numpy as np
    import concourse.bacc as bacc
    from concourse.bass_utils import run_bass_kernel_spmd as run

    nc = bacc.Bacc("TRN2", target_bir_lowering=False, num_devices=1)
    arrays, io = {}, {}
    for name, a in inputs.items():
        a = np.ascontiguousarray(a)
        arrays["in_" + name] = a
        io[name] = nc.dram_tensor("in_" + name, a.shape, mybir.dt.from_np(a.dtype), kind="ExternalInput").ap()
    B, T, D = inputs["x"].shape
    out = nc.dram_tensor("out_0", (B, (T + 3) // 4 * 2, D), F32, kind="ExternalOutput").ap()
    audio_tower_kernel(nc, io, out)
    r = run(nc, [arrays], core_ids=[0])
    return r.results[0]["out_0"]
```

```python
from contextlib import ExitStack

import concourse.bass as bass
from concourse import mybir
from concourse.bass import IndirectOffsetOnAxis, ds

F32 = mybir.dt.float32
I32 = mybir.dt.int32
BF16 = mybir.dt.bfloat16
ALU = mybir.AluOpType
ACT = mybir.ActivationFunctionType
AX = mybir.AxisListType


def audio_tower_kernel(nc, io, out):
    B, T_IN, D = io["x"].shape
    SEG = 128
    S = SEG // 2
    H, HD = io["L0_attn_ttt_g"].shape
    E, _, HID = io["L0_ffn_w_fast1"].shape
    DR = io["L0_ffn_probe_w"].shape[0]
    P = 128
    NT = B * S // P
    R = B * H
    KB = D - P
    S_IN = (T_IN + 1) // 2
    BLK = 8
    NB = S // BLK
    NG = B * S // 512

    with ExitStack() as ctx:
        def sb(name, shape, dt=F32):
            return ctx.enter_context(nc.sbuf_tensor(name, shape, dt))

        def dram(name, shape, dt=F32):
            return nc.dram_tensor(name, shape, dt, kind="Internal").ap()

        sems = {}

        def sem(name):
            sems[name] = ctx.enter_context(nc.semaphore(name))
            return sems[name]

        arena = sb("arena", [P, 48128])
        at = 0

        def cut(n):
            nonlocal at
            at += n
            return arena[:, at - n:at]

        X = cut(NT * D)
        KQM = cut(R * 2 * S)
        GW = cut(R * HD)
        CC = cut(S * HD)
        MN = cut(S * 2 * BLK)
        W1A = cut(E * HID)
        W1B = cut(E * HID)
        W1 = arena[:, at - 2 * E * HID:at].rearrange("p (c n) -> p c n", c=2)
        W2 = cut(E * HID // P * D)
        xs = X.rearrange("p (i d) -> p i d", d=D)
        hmix = CC[:, 0:NT * D].rearrange("p (i d) -> p i d", d=D)
        xnTs = W2[:, 0:2 * NT * P].rearrange("p (i c t) -> p i c t", c=2, t=P)
        hTa = W2[:, 2 * NT * P:3 * NT * P]
        hTb = W2[0:KB + 1, 3 * NT * P:4 * NT * P]
        vk = W2[:, 0:NT * D].rearrange("p (i d) -> p i d", d=D)
        Wd = [MN[:, 0:D], MN[KB:P, D:2 * D]]
        qst = X[:, 2048:2048 + 4 * D].rearrange("p (i d) -> p i d", d=D)
        xT_sb = [KQM[:, k * 2 * P:(k + 1) * 2 * P] for k in range(2)]
        Sm = [KQM[:, 512 + k * P:512 + (k + 1) * P] for k in range(2)]
        Ex = [KQM[:, 768 + k * P:768 + (k + 1) * P] for k in range(2)]
        ExT = [KQM[:, 1024 + k * P:1024 + (k + 1) * P] for k in range(2)]
        kqm = KQM.rearrange("p (r c t) -> p r c t", c=2, t=S)
        gw = GW.rearrange("p (r e) -> p r e", e=HD)

        far_sb = X[0:R, 0:32 * HD]
        ablk = [X[0:R, 2048 + 512 * k:2048 + 512 * (k + 1)] for k in range(2)]
        mn = MN[0:R, :].rearrange("p (s w) -> p s w", w=2 * BLK)
        cc = CC[0:R, :].rearrange("p (t e) -> p t e", e=HD)

        PRS = sb("PRS", [P, 2 * 14 * HD])
        PR = [PRS[:, 14 * HD * k:14 * HD * (k + 1)].rearrange("p (n e) -> p n e", e=HD) for k in range(2)]
        Wkq = [PRS[:, 0:2 * D].rearrange("p (h c e) -> p h c e", h=H, c=2),
               PRS[0:KB, 2 * D:4 * D].rearrange("p (h c e) -> p h c e", h=H, c=2)]
        NQV = 2 * D + H
        Wqv = [PRS[:, 4 * D:4 * D + NQV], PRS[0:KB + 1, 4 * D + NQV:4 * D + 2 * NQV]]
        Gst = sb("Gst", [R, 4, HD])
        U = sb("U", [R, 2, HD])
        JK = sb("JK", [R, HD])
        PG = sb("PG", [R, HD])
        PC = sb("PC", [R, HD])
        Wv_ = sb("Wv_", [R, HD])
        M2 = sb("M2", [R, 2, HD])
        MY = sb("MY", [R, 2, 2 * BLK])
        sc = sb("sc", [R, 8])
        usum = sb("usum", [R, 2])
        UC = sb("UC", [R, HD])
        y1 = sb("y1", [R, 2])
        eta96 = sb("eta96", [R, S])
        b0r = sb("b0r", [R, HD])
        b0m = sb("b0m", [R, 2])
        g2r = sb("g2r", [R, HD])
        ident = sb("ident", [P, P])
        maskbd = KQM[:, 1280:1280 + P]
        negc = sb("negc", [S, S])
        mv = sb("mv", [P, NT, 2])
        st6 = sb("st6", [P, 2, 6])
        rowm = sb("rowm", [P, NT])
        negm = sb("negm", [P, NT])
        esum = sb("esum", [P, NT])
        rinv = sb("rinv", [P, NT])
        std0 = sb("std0", [P, NT])
        rstd0 = sb("rstd0", [P, NT])
        epsc = sb("epsc", [P, 3])
        bdc = sb("bdc", [P, 2])
        etal = sb("etal", [P, H, NT])
        etaT = X[0:H * NT, 2048 + 4 * D:2048 + 4 * D + P]
        w0h = sb("w0h", [HD, H, HD])
        w0m = sb("w0m", [HD, H])
        cmean = sb("cmean", [P, 3 * NT])
        gtok = sb("gtok", [P, D])
        btok = sb("btok", [P, D])

        def tiles(region, at, n, w=D):
            return [region[:, at + w * k:at + w * (k + 1)] for k in range(n)]

        DB = D + 8
        ZS = tiles(X, 0, 5, DB)
        TN = tiles(X, 5 * DB, 2, DB)
        one_col = X[:, 0:7 * DB].rearrange("p (k n) -> p k n", n=DB)[:, :, D:D + 1]
        XN = tiles(X, 7 * DB, 3)
        tT1 = tiles(X, 2048, 2, 2 * P)
        tT2 = tiles(X, 2560, 2, 2 * P)
        tT3 = tiles(MN, 0, 2, 2 * P)
        QR = tiles(MN, 512, 2)
        h2 = hmix
        Wo = [PRS[:, 0:D], PRS[0:KB + 1, D:2 * D]]
        Wu = [PRS[:, 2 * D:3 * D], PRS[0:KB + 1, 3 * D:4 * D]]
        SQ = tiles(PRS, 4 * D, 2)
        bias_rows = PRS[0:1, 6 * D:8 * D]
        bup = PRS[0:1, 8 * D:9 * D]
        b0t = sb("b0t", [P, D])
        gcol = sb("gcol", [P, 2, 4])
        emb = sb("emb", [E, DR + 4])
        enT = sb("enT", [DR, E])
        rw = sb("rw", [E, D])
        pw = sb("pw", [DR, D])
        ones8 = sb("ones8", [E, P])
        dg8 = sb("dg8", [E, E])
        dgj = sb("dgj", [E, DR])
        Wr = sb("Wr", [P, 2, 2 * E + DR])
        NR = 2 * E + DR
        LG = CC[:, NT * D:NT * (D + NR)].rearrange("p (i n) -> p i n", n=NR)
        rz = sb("rz", [P, 3, 2 * H])
        mvs = sb("mvs", [P, 3, 3, 4])
        s6 = sb("s6", [P, 3, 6])

        w1a = W1A.rearrange("p (e n) -> p e n", n=HID)
        w1b = W1B.rearrange("p (e n) -> p e n", n=HID)
        KH = HID // P
        w2 = W2.rearrange("p (e k d) -> p e k d", k=KH, d=D)
        mg = sb("mg", [P, 2, E])
        ebias = sb("ebias", [P, E])
        TK = 2
        SLOTS = TK * B * S // P + E - 1
        LASTG = (SLOTS - 1) // 4
        NI = NT * E
        ka = 0

        def kcut(n):
            nonlocal ka
            ka += n
            return KQM[:, ka - n:ka]

        def khalf(n):
            return kcut(n // 2).bitcast(BF16)

        def rv(n=E):
            return kcut(NT * n).rearrange("p (i e) -> p i e", e=n)
        Lb, Lg, al8, eqt, sct, scu, oh1, oh2, L2t, P8 = [rv() for k in range(10)]
        oha = khalf(NI).rearrange("p (i e) -> p i e", e=E)
        mx = kcut(2 * NT).rearrange("p (c i) -> p c i", c=2)
        cs = kcut(2 * NT).rearrange("p (c i) -> p c i", c=2)
        gt = kcut(4 * NT).rearrange("p (c i) -> p c i", c=4)
        gp = khalf(3 * 2 * NT).rearrange("p (v j) -> p v j", v=3)
        gr = kcut(2 * 2 * NT).rearrange("p (v j) -> p v j", v=2)
        pos = kcut(2 * NT)
        slot_ = kcut(2 * NT)
        row_ = kcut(2 * NT)
        Aoh = kcut(2 * NT * SLOTS).rearrange("p (j k) -> p j k", k=SLOTS)
        av = khalf(2 * NT * 5 * SLOTS).rearrange("p (j v k) -> p j v k", v=5, k=SLOTS)
        Bh = khalf(2 * NT * P).rearrange("p (j r) -> p j r", r=P)
        cnt = khalf(E)
        tlm = kcut(E * NT).rearrange("p (e k) -> p e k", k=NT)
        tl = kcut(E)
        bmt = kcut(E * E).rearrange("p (a b) -> p a b", b=E)
        bs = kcut(2 * E)
        exm = kcut(SLOTS * E).rearrange("p (k e) -> p k e", e=E)
        exf = kcut(SLOTS)
        pad = kcut(SLOTS)
        lst = kcut(5 * SLOTS).rearrange("p (v k) -> p v k", k=SLOTS)
        tok1 = kcut(SLOTS)
        nrm = CC[:, NT * (D + NR):NT * (D + NR + 3)].rearrange("p (k i) -> p k i", k=3)
        psq = CC[:, NT * (D + NR + 3):NT * (D + NR + 3) + DR]
        W1S = [X[:, 2 * HID * k:2 * HID * (k + 1)].rearrange("p (c n) -> p c n", c=2) for k in range(2)]
        ga = 0

        def gcut(n):
            nonlocal ga
            ga += n
            return GW[:, ga - n:ga]
        w8 = gcut(E)
        irow = gcut(P)
        k128 = gcut(SLOTS)
        ik = gcut(SLOTS)
        i128 = gcut(NT)
        p1 = gcut(1)
        tri = gcut(P)
        tri_b = gcut(P // 2).bitcast(BF16)
        ones_b = gcut(P // 2).bitcast(BF16)
        emask = gcut(E * E).rearrange("p (a b) -> p a b", b=E)
        trash = gcut(1)
        XG = [gcut(2 * P) for k in range(4)]
        xgT = gcut(2 * P)
        RL = gcut(HID)
        HT2 = gcut(HID)
        YO = [gcut(D) for k in range(4)]
        b2r = gcut(E * D)
        idx = sb("idx", [P, SLOTS], I32)
        ex = sb("ex", [P, SLOTS], I32)
        gates = sb("gates", [P, SLOTS])
        fat = sb("fat", [P, E])

        bank = [ctx.enter_context(nc.psum_tensor(f"bank{k}", [P, 512], F32)) for k in range(8)]

        hmix_d = dram("hmix_d", (NT * P, D))
        q_d = dram("q_d", (NT * P, D))
        c_d = dram("c_d", (NT * P, D))
        km_d = dram("km_d", (S, R, S))
        xn_d = dram("xn_d", (NT * P + P, D))
        acc_d = dram("acc_d", (NT * P + P, D))

        consts = sem("consts")
        x_zero = sem("x_zero")
        x_in = [sem(f"x_in{c}") for c in range(4)]
        w_in = sem("w_in")
        xT_done = sem("xT_done")
        xT_out = sem("xT_out")
        s_done = sem("s_done")
        mx_out = sem("mx_out")
        negm_out = sem("negm_out")
        exp_out = sem("exp_out")
        rinv_out = sem("rinv_out")
        eT_done = sem("eT_done")
        eT_out = sem("eT_out")
        o_done = sem("o_done")
        h_out = sem("h_out")
        stat_a = sem("stat_a")
        stat_b = sem("stat_b")
        std_out = sem("std_out")
        rstd_out = sem("rstd_out")
        xn_out = sem("xn_out")
        hmix_st = sem("hmix_st")
        xnT_done = sem("xnT_done")
        xnT_out = sem("xnT_out")
        hd_done = sem("hd_done")
        hT_out = sem("hT_out")
        wprep = sem("wprep")
        kq_done = sem("kq_done")
        k_out = sem("k_out")
        q_out = sem("q_out")
        qv_done = sem("qv_done")
        qt_out = sem("qt_out")
        vk_out = sem("vk_out")
        q_st = [sem(f"q_st{k}") for k in range(4)]
        eta_done = sem("eta_done")
        eta_out = sem("eta_out")
        gram_done = sem("gram_done")
        km_out = sem("km_out")
        qm_out = sem("qm_out")
        c_chain = sem("c_chain")
        c_out = sem("c_out")
        rows_in = sem("rows_in")
        w0_out = sem("w0_out")
        b0_out = sem("b0_out")
        gw_rep = sem("gw_rep")
        km_st = sem("km_st")
        mn_zero = sem("mn_zero")
        mn_in = sem("mn_in")
        mnb_in = sem("mnb_in")
        mnb_out = sem("mnb_out")
        mne_out = sem("mne_out")
        eta_in = sem("eta_in")
        c_st = sem("c_st")
        c_in = sem("c_in")
        rt_in = sem("rt_in")
        rt_prep = sem("rt_prep")
        prep_mm = sem("prep_mm")
        b0t_out = sem("b0t_out")
        post_w = sem("post_w")
        h_in = sem("h_in")
        pb_out = sem("pb_out")
        wg_out = sem("wg_out")
        qr_in = [sem(f"qr_in{k}") for k in range(2)]
        qb_out = sem("qb_out")
        zq_done = sem("zq_done")
        zs_out = sem("zs_out")
        sq_out = sem("sq_out")
        sqz_out = sem("sqz_out")
        zn_out = sem("zn_out")
        yg_out = sem("yg_out")
        y_out = sem("y_out")
        st_a = sem("st_a")
        st_y = sem("st_y")
        st_t = sem("st_t")
        st_h = sem("st_h")
        sd_y = sem("sd_y")
        sd_t = sem("sd_t")
        sd_h = sem("sd_h")
        ri_out = sem("ri_out")
        yn_out = sem("yn_out")
        tn_out = sem("tn_out")
        xn2_out = sem("xn2_out")
        t1_done = sem("t1_done")
        t2_done = sem("t2_done")
        t3_done = sem("t3_done")
        t1_out = sem("t1_out")
        t2_out = sem("t2_out")
        t3_out = sem("t3_out")
        wo_done = sem("wo_done")
        up_done = sem("up_done")
        h2_out = sem("h2_out")
        rt_done = sem("rt_done")
        lg_out = sem("lg_out")
        xn_st = [sem(f"xn_st{k}") for k in range(3)]
        w1b_zero = sem("w1b_zero")
        w1_in = sem("w1_in")
        w2_in = sem("w2_in")
        w_sc = sem("w_sc")
        w_acc = sem("w_acc")
        eb_out = sem("eb_out")
        rc_out = sem("rc_out")
        z_st = sem("z_st")
        b2_in = sem("b2_in")
        rt_dve = sem("rt_dve")
        rt_pool = sem("rt_pool")
        rt_act = sem("rt_act")
        rt_pe = sem("rt_pe")
        idx_out = sem("idx_out")
        acc_st = sem("acc_st")
        xg_in = [sem(f"xg_in{k}") for k in range(4)]
        xgT_done = sem("xgT_done")
        xgT_out = sem("xgT_out")
        l1_done = sem("l1_done")
        relu_out = sem("relu_out")
        hid_out = sem("hid_out")
        w1_copied = sem("w1_copied")
        l2_done = sem("l2_done")
        yb_out = sem("yb_out")
        yo_out = sem("yo_out")
        y_add = sem("y_add")
        u_out = sem("u_out")
        v_step = sem("v_step")
        uc_out = sem("uc_out")
        rr_out = sem("rr_out")
        r_out = sem("r_out")
        my_out = sem("my_out")
        m2_out = sem("m2_out")
        prb_out = sem("prb_out")
        pr_out = sem("pr_out")
        g_out = sem("g_out")
        g_in = [sem(f"g_in{k}") for k in range(4)]
        grp_done = sem("grp_done")
        nxt_done = sem("nxt_done")
        far_done = sem("far_done")
        far_out = sem("far_out")
        a_in = [sem(f"a_in{t}") for t in range(BLK)]
        block = ctx.enter_context(nc.Block())

        CONSTS = 7
        NW = 7 * 2 + 1 + 2
        SC = float(D) ** -0.5

        def grp_count(t):
            return 1 + (BLK - 2) * (t // BLK) + t % BLK + 1

        SP1, SP2 = 4, 7
        NGR = R // 4 // NG

        def gram_row(m):
            g, n = divmod(m, NGR)
            return 32 * (n // 2) + 8 * g + 4 * (n % 2)

        def inverses(j):
            n = sum(0 <= jj - back < NT for back in (3, 5, 1, 7) for jj in range(j))
            return n + sum(0 <= j - back < NT for back in (3, 5, 1))

        NQB = 2 * NT // 8
        RC = 21
        STEPS = ["base logits", "norm floor", "norm inverse", "align", "logits",
                 "max 1", "eq 1", "tie 1", "first 1", "onehot 1", "rest", "max 2", "eq 2", "gap", "tie 2", "first 2", "onehot 2",
                 "both", "counts", "slots of", "gate sum", "slots", "gate 1", "before", "gate 2", "base", "gate part 1", "end", "gate rest 1",
                 "places", "gate part 2", "of 1", "pos 1", "of 2", "gate rest 2", "pos 2", "gate part 3",
                 "slot scaled", "slot", "row", "slot onehot", "gates 1", "gates 2",
                 "place onehot 0", "place onehot 1", "place onehot 2", "place onehot 3",
                 "ended", "expert", "expert index", "lists", "token", "gate low", "pad", "gates"]
        RT = {name: k + 1 for k, name in enumerate(STEPS)}

        @block.gpsimd
        def _(eng):
            eng.memset(ident[:, :], 0.0).then_inc(consts, 1)
            eng.memset(maskbd[:, :], 0.0).then_inc(consts, 1)
            eng.memset(negc[:, :], -1.0).then_inc(consts, 1)
            eng.wait_ge(consts, 3)
            eng.affine_select(out=ident[:, :], in_=ident[:, :], compare_op=ALU.not_equal, fill=1.0,
                              base=0, pattern=[[-1, P]], channel_multiplier=1).then_inc(consts, 1)
            eng.wait_ge(consts, 4)
            eng.memset(maskbd[0:S, S:P], -1e30).then_inc(consts, 1)
            eng.memset(maskbd[S:P, 0:S], -1e30).then_inc(consts, 1)
            eng.wait_ge(consts, 6)
            eng.affine_select(out=negc[:, :], in_=negc[:, :], compare_op=ALU.is_ge, fill=0.0,
                              base=0, pattern=[[1, S]], channel_multiplier=-1).then_inc(consts, 1)
            eng.wait_ge(consts, 7)
            eng.memset(W1B[KB:P, :], 0.0).then_inc(w1b_zero, 1)
            eng.wait_ge(w1b_zero, 1)
            eng.wait_ge(w0_out, 3)
            for h in range(H):
                eng.tensor_copy(gw[0:HD, 32 * h:32 * h + 32, :],
                                w0h[:, h, :].unsqueeze(1).broadcast_to([HD, 32, HD])).then_inc(gw_rep, 1)
            eng.wait_ge(gw_rep, 3)
            for i in range(NT):
                if i == NT // 2:
                    eng.wait_ge(hd_done, 2 * NG)
                    eng.memset(MN, 0.0).then_inc(mn_zero, 1)
                eng.wait_ge(qt_out, i + 1)
                if i == 0:
                    eng.wait_ge(w_in, 16 * NW)
                eng.tensor_tensor(qst[:, i % 4, :], qst[:, i % 4, :], btok[:, :], ALU.add).then_inc(qb_out, 1)

            eng.wait_ge(qv_done, NT)
            for k in range(2):
                eng.memset(PR[k][:, :, :], 0.0).then_inc(gw_rep, 1)
            eng.wait_ge(mne_out, 1)
            eng.wait_ge(mnb_in, 16 * (NB - 2))
            eng.tensor_tensor(mn[:, 2 * BLK:S, :], mn[:, 2 * BLK:S, :],
                              eta96[:, 2 * BLK:S].unsqueeze(2).broadcast_to([R, S - 2 * BLK, 2 * BLK]), ALU.mult).then_inc(mnb_out, 1)

            def add_w1(c, n, half):
                w = io["L0_ffn_" + n][2 * c:2 * c + 2]
                if half == 0:
                    eng.wait_ge(w_sc, 8 * (c + 1))
                    eng.dma_start(w1a[:, 2 * c:2 * c + 2, :], w[:, 0:P, :].rearrange("e p n -> p e n"), accum_op=ALU.add).then_inc(w_acc, 16)
                else:
                    eng.dma_start(w1b[0:KB, 2 * c:2 * c + 2, :], w[:, P:D, :].rearrange("e p n -> p e n"), accum_op=ALU.add).then_inc(w_acc, 16)

            def add_w2(c, n, half):
                e = 2 * c + half
                eng.wait_ge(w_sc, 32 + 6 * (c + 1))
                eng.dma_start(w2[:, e, :, :], io["L0_ffn_" + n][e].rearrange("(k p) d -> p k d", p=P), accum_op=ALU.add).then_inc(w_acc, 16)

            for t in range(S):
                J, i = divmod(t, BLK)
                if J < NB - 1:
                    first = max(0, i + 2 - BLK)
                    n = BLK - first
                    eng.wait_ge(m2_out, t + 1)
                    eng.wait_ge(my_out, 2 * (t + 1))
                    if t >= 2:
                        eng.wait_ge(nxt_done, t - 1)
                    eng.tensor_tensor(PR[t % 2][0:R, BLK - 2:BLK - 2 + n, :],
                                      M2[:, t % 2, :].unsqueeze(1).broadcast_to([R, n, HD]),
                                      MY[:, t % 2, BLK + first:2 * BLK].unsqueeze(2).broadcast_to([R, n, HD]),
                                      ALU.mult).then_inc(prb_out, 1)
                for c in range(4):
                    for half in range(2):
                        if t == 8 * c + 9 + half:
                            add_w1(c, "w_fast1", half)
                        if t == 8 * c + 14 + half:
                            if half == 0:
                                eng.wait_ge(w_acc, 16 * (4 * c + 2))
                            add_w1(c, "h_fast1", half)
                        if t == 6 * c + 39 + half:
                            add_w2(c, "w_fast2", half)
                        if t == 6 * c + 42 + half:
                            if half == 0:
                                eng.wait_ge(w_acc, 16 * (16 + 4 * c + 2))
                            add_w2(c, "h_fast2", half)

            def y_tile(i):
                z = ZS[i % 5][:, 0:D]
                z3 = z.rearrange("p (h e) -> p h e", h=H)
                eng.wait_ge(ri_out, inverses(i + 1))
                eng.tensor_tensor(z3, z3, rz[:, i % 3, 0:H].unsqueeze(2).broadcast_to([P, H, HD]), ALU.mult).then_inc(zn_out, 1)
                eng.wait_ge(zn_out, i + 1)
                eng.tensor_tensor(z, z, gtok[:, :], ALU.mult).then_inc(yg_out, 1)
                eng.wait_ge(yg_out, i + 1)
                eng.wait_ge(qr_in[i % 2], 16 * (i // 2 + 1))
                eng.tensor_tensor(z, z, QR[i % 2], ALU.add).then_inc(y_out, 1)

            for i in range(NT):
                y_tile(i)

            eng.wait_ge(zq_done, NT)
            eng.iota(w8, [[-1, E]], base=E, channel_multiplier=0, allow_small_or_imprecise_dtypes=True).then_inc(rc_out, 1)
            eng.iota(irow, [[1, P]], base=0, channel_multiplier=0, allow_small_or_imprecise_dtypes=True).then_inc(rc_out, 1)
            eng.iota(k128, [[P, SLOTS]], base=0, channel_multiplier=0, allow_small_or_imprecise_dtypes=True).then_inc(rc_out, 1)
            eng.iota(ik, [[1, SLOTS]], base=0, channel_multiplier=0, allow_small_or_imprecise_dtypes=True).then_inc(rc_out, 1)
            eng.iota(p1, [[1, 1]], base=1, channel_multiplier=1, allow_small_or_imprecise_dtypes=True).then_inc(rc_out, 1)
            eng.iota(i128, [[P, NT]], base=0, channel_multiplier=0, allow_small_or_imprecise_dtypes=True).then_inc(rc_out, 1)
            eng.iota(trash, [[1, 1]], base=NT * P + 1, channel_multiplier=1, allow_small_or_imprecise_dtypes=True).then_inc(rc_out, 1)
            eng.memset(tri, 1.0).then_inc(rc_out, 1)
            eng.memset(ones_b, 1.0).then_inc(rc_out, 1)
            eng.memset(emask, float(P)).then_inc(rc_out, 1)
            for k in range(4):
                eng.memset(XG[k], 0.0).then_inc(rc_out, 1)
            eng.wait_ge(rc_out, 14)
            eng.affine_select(out=tri, in_=tri, compare_op=ALU.is_gt, fill=0.0, base=0, pattern=[[1, P]],
                              channel_multiplier=-1).then_inc(rc_out, 1)
            eng.affine_select(out=emask, in_=emask, compare_op=ALU.is_gt, fill=0.0, base=0, pattern=[[1, E], [-1, E]],
                              channel_multiplier=0).then_inc(rc_out, 1)
            for k in range(4):
                eng.memset(XG[k][:, D:D + 1], 1.0).then_inc(rc_out, 1)
            eng.wait_ge(rc_out, 16)
            eng.tensor_copy(tri_b, tri).then_inc(rc_out, 1)
            eng.wait_ge(rt_dve, RT["slot onehot"])
            for c in range(TK):
                j = slice(NT * c, NT * (c + 1))
                eng.tensor_tensor(av[:, j, 0, :], Aoh[:, j, :], i128.unsqueeze(2).broadcast_to([P, NT, SLOTS]),
                                  ALU.mult).then_inc(rt_pool, 1)
            eng.tensor_tensor(av[:, :, 4, :], Aoh, gp[:, 2, :].unsqueeze(2).broadcast_to([P, 2 * NT, SLOTS]),
                              ALU.mult).then_inc(rt_pool, 1)
            def gather(s):
                if s >= 4:
                    eng.wait_ge(xgT_done, s - 3)
                eng.indirect_dma_start(out=XG[s % 4][:, 0:D], out_offset=None, in_=xn_d,
                                       in_offset=IndirectOffsetOnAxis(ap=idx[:, s:s + 1], axis=0)).then_inc(xg_in[s % 4], 16)

            def add(s):
                eng.wait_ge(yo_out, s + 1)
                if s >= 1:
                    eng.wait_ge(y_add, 16 * s)
                eng.indirect_dma_start(out=acc_d, out_offset=IndirectOffsetOnAxis(ap=idx[:, s:s + 1], axis=0), in_=YO[s % 4],
                                       in_offset=None, compute_op=ALU.add).then_inc(y_add, 16)

            eng.wait_ge(idx_out, 1)
            eng.wait_ge(z_st, 32)
            for k in range(3):
                eng.wait_ge(xn_st[k], 16 * len(range(k, NT, 3)))
            for s in range(4):
                gather(s)
            eng.wait_ge(acc_st, 16)
            for s in range(SLOTS):
                add(s)
                if s + 4 < SLOTS:
                    gather(s + 4)

        @block.sync
        def _(eng):
            for c in range(4):
                eng.wait_ge(x_zero, c + 1)
                for b2 in range(2):
                    src = io["x"].rearrange("(i b) t d -> b t i d", b=2)[b2, 0:T_IN:2, 4 * c:4 * c + 4, :]
                    eng.dma_start(xs[S * b2:S * b2 + S_IN, 4 * c:4 * c + 4, :], src).then_inc(x_in[c], 16)
            for a, r in ((0, slice(0, P)), (1, slice(P, D))):
                eng.dma_start(Wd[a], io["L0_attn_W_down"][r, :]).then_inc(w_in, 16)
                for c, n in ((0, "Wk"), (1, "Wq")):
                    eng.dma_start(Wkq[a][:, :, c, :], io["L0_attn_" + n][r, :].rearrange("k (h e) -> k h e", h=H)).then_inc(w_in, 16)
                n = r.stop - r.start
                eng.dma_start(Wqv[a][0:n, 0:D], io["L0_attn_Wq"][r, :]).then_inc(w_in, 16)
                eng.dma_start(Wqv[a][0:n, D:2 * D], io["L0_attn_Wv"][r, :]).then_inc(w_in, 16)
                eng.dma_start(Wqv[a][0:n, 2 * D:NQV], io["L0_attn_lr_w"][r, :]).then_inc(w_in, 16)
                eng.dma_start(bdc[0:n, a:a + 1], io["L0_attn_b_down"][r].rearrange("(k o) -> k o", o=1)).then_inc(w_in, 16)
            eng.wait_ge(wprep, 3)
            eng.dma_start(Wqv[1][KB:KB + 1, 2 * D:NQV], io["L0_attn_lr_b"].rearrange("(o k) -> o k", o=1)).then_inc(w_in, 16)
            eng.dma_start(gtok[:, :], io["L0_attn_ttt_g"].rearrange("h e -> (h e)").partition_broadcast(P)).then_inc(w_in, 16)
            eng.dma_start(btok[:, :], io["L0_attn_ttt_b"].rearrange("h e -> (h e)").partition_broadcast(P)).then_inc(w_in, 16)
            eng.dma_start(w0h[:, :, :], io["L0_attn_W1"].rearrange("h d e -> d h e")).then_inc(rows_in, 16)
            for h in range(H):
                rows = slice(32 * h, 32 * h + 32)
                eng.dma_start(b0r[rows, :], io["L0_attn_b1"][h, 0, :].partition_broadcast(32)).then_inc(rows_in, 16)
                eng.dma_start(g2r[rows, :], io["L0_attn_ttt_g"][h, :].partition_broadcast(32)).then_inc(rows_in, 16)
            eng.dma_start(b0t[:, :], io["L0_attn_b1"].rearrange("h o e -> (o h e)").partition_broadcast(P)).then_inc(rt_in, 16)
            eng.dma_start(emb[:, 0:DR], io["L0_ffn_router_emb"]).then_inc(rt_in, 16)
            eng.dma_start(rw[:, :], io["L0_ffn_router_w"]).then_inc(rt_in, 16)
            eng.dma_start(pw[:, :], io["L0_ffn_probe_w"]).then_inc(rt_in, 16)
            for c, n in enumerate(("post_g", "post_b", "norm_g", "norm_b")):
                for k in range(2):
                    m = P if k == 0 else KB
                    eng.dma_start(gcol[0:m, k, c:c + 1], io["L0_attn_" + n][P * k:P * k + m].rearrange("(k o) -> k o", o=1)).then_inc(rt_in, 16)
            for k in range(2):
                eng.dma_start(mg[:, k, :], io[f"L0_ffn_m_gate{k + 1}"].partition_broadcast(P)).then_inc(rt_in, 16)
            eng.dma_start(ebias[:, :], io["L0_ffn_energy"].partition_broadcast(P)).then_inc(rt_in, 16)
            eng.dma_start(fat[:, :], io["L0_ffn_fatigue"].partition_broadcast(P)).then_inc(rt_in, 16)
            eng.wait_ge(w1b_zero, 1)
            eng.dma_start(W1B[KB:KB + 1, :], io["L0_ffn_b1"].rearrange("e (o n) -> o (e n)", o=1)).then_inc(rt_in, 16)
            for c in range(4):
                e2 = slice(2 * c, 2 * c + 2)
                eng.dma_start(w1a[:, e2, :], io["L0_ffn_w_slow1"][e2, 0:P, :].rearrange("e p n -> p e n")).then_inc(w1_in, 16)
                eng.dma_start(w1b[0:KB, e2, :], io["L0_ffn_w_slow1"][e2, P:D, :].rearrange("e p n -> p e n")).then_inc(w1_in, 16)
            eng.wait_ge(h_out, NT)
            eng.dma_start(hmix_d.rearrange("(i p) d -> p i d", p=P), hmix).then_inc(hmix_st, 16)
            def spread(J, t0, t1):
                eng.wait_ge(far_out, 4 * (J + 1))
                if J >= 2:
                    eng.wait_ge(grp_done, grp_count(BLK * (J - 2) + BLK - 3))
                for t in range(t0, t1):
                    eng.dma_start(ablk[J % 2][:, HD * t:HD * (t + 1)], far_sb[t:R:32, :]).then_inc(a_in[t], 16)

            cdv = c_d.rearrange("(i p) d -> p i d", p=P)
            for g in range(NG):
                for i in range(4 * g, 4 * g + 4):
                    eng.wait_ge(qb_out, i + 1)
                    eng.dma_start(q_d[i * P:(i + 1) * P, :], qst[:, i % 4, :]).then_inc(q_st[i % 4], 16)
                if g == NG - 1:
                    for k in range(4):
                        eng.wait_ge(q_st[k], 16 * NT // 4)
                    spread(0, 0, BLK)
                    eng.wait_ge(eta_out, 1)
                    eng.dma_start(eta96[:, :], etaT).then_inc(eta_in, 16)
                eng.wait_ge(c_out, g + 1)
                eng.dma_start(cdv[:, 4 * g:4 * g + 4, :], vk[:, 4 * g:4 * g + 4, :]).then_inc(c_st, 16)
                for h in range(H):
                    rows = slice(32 * h + 8 * g, 32 * h + 8 * g + 8)
                    eng.wait_ge(km_out, NGR * g + 2 * (h + 1))
                    eng.dma_start(km_d[:, rows, :], kqm[HD:P, rows, 0, :]).then_inc(km_st, 16)
                if g == 0:
                    eng.wait_ge(hmix_st, 16)
                eng.wait_ge(c_st, 16 * (g + 1))
                for h in range(H):
                    rows = slice(32 * h + 8 * g, 32 * h + 8 * g + 8)
                    eng.dma_start(cc[rows, :, :],
                                  c_d.rearrange("(b t) (h e) -> h b t e", t=S, h=H)[h, 8 * g:8 * g + 8]).then_inc(c_in, 16)
            eng.wait_ge(km_st, 16 * H * NG)
            eng.wait_ge(mn_zero, 1)
            for J in range(NB):
                n = min(2 * BLK, S - BLK * J)
                eng.dma_start(mn[:, BLK * J:BLK * (J + 1), 0:n],
                              km_d[BLK * J:BLK * (J + 1), :, BLK * J:BLK * J + n].rearrange("s r w -> r s w")).then_inc(mn_in if J < 2 else mnb_in, 16)
            for t in range(S):
                eng.wait_ge(g_out, t + 1)
                eng.dma_start(GW[HD + t:HD + t + 1, :], Gst[:, t % 4, :]).then_inc(g_in[t % 4], 16)
                J = t // BLK
                if t % BLK == 5 and J < NB - 1:
                    spread(J + 1, 0, SP1)
                if t % BLK == 6 and J < NB - 1:
                    spread(J + 1, SP1, SP2)
                if t % BLK == 7 and J < NB - 1:
                    spread(J + 1, SP2, BLK)
                if t < 2 * E and t % 2 == 0:
                    eng.dma_start(w2[:, t // 2, :, :], io["L0_ffn_w_slow2"][t // 2].rearrange("(k p) d -> p k d", p=P)).then_inc(w2_in, 16)
            eng.wait_ge(m2_out, S)
            eng.wait_ge(grp_done, grp_count(S - 3))
            for w, n in ((Wo, "Wo"), (Wu, "W_up")):
                eng.dma_start(w[0], io["L0_attn_" + n][0:P, :]).then_inc(post_w, 16)
                eng.dma_start(w[1][0:KB, :], io["L0_attn_" + n][P:D, :]).then_inc(post_w, 16)
            eng.dma_start(bup, io["L0_attn_b_up"].rearrange("(o k) -> o k", o=1)).then_inc(post_w, 16)
            for i in range(2):
                eng.dma_start(QR[i], q_d[P * i:P * (i + 1), :]).then_inc(qr_in[i % 2], 16)
            eng.dma_start(h2, hmix_d.rearrange("(i p) d -> p i d", p=P)).then_inc(h_in, 16)
            eng.wait_ge(pb_out, 2)
            for k, w in enumerate((Wo, Wu)):
                eng.dma_start(w[1][KB:KB + 1, :], bias_rows[:, D * k:D * (k + 1)]).then_inc(post_w, 16)
            for j in range(NT + 7):
                i = j + 2
                if i < NT:
                    eng.wait_ge(y_out, i - 1)
                    eng.dma_start(QR[i % 2], q_d[P * i:P * (i + 1), :]).then_inc(qr_in[i % 2], 16)
                i = j - 7
                if 0 <= i:
                    eng.wait_ge(xn2_out, i + 1)
                    eng.dma_start(xn_d[P * i:P * (i + 1), :], XN[i % 3]).then_inc(xn_st[i % 3], 16)
            eng.dma_start(acc_d[0:NT * P, :].rearrange("(i p) d -> p i d", p=P), h2).then_inc(acc_st, 16)
            eng.wait_ge(zq_done, NT)
            eng.dma_start(b2r, io["L0_ffn_b2"].rearrange("e d -> (e d)").partition_broadcast(P)).then_inc(b2_in, 16)
            eng.wait_ge(rc_out, 14)
            for d in (xn_d, acc_d):
                eng.dma_start(d[NT * P:, :], XG[0][:, 0:D]).then_inc(z_st, 16)
            eng.wait_ge(y_add, 16 * SLOTS)
            eng.dma_start(out.rearrange("b t d -> (b t) d"), acc_d[0:NT * P, :]).then_inc(acc_st, 16)
            eng.wait_ge(acc_st, 32)

        @block.tensor
        def _(eng):
            eng.wait_ge(consts, CONSTS)

            def xT(i):
                eng.wait_ge(x_in[i // 4], 32)
                if i >= 2:
                    eng.wait_ge(xT_out, i - 1)
                eng.transpose(bank[i % 2][:, 0:P], xs[:, i, 0:P], ident[:, :])
                eng.transpose(bank[i % 2][:, P:2 * P], xs[:, i, KB:D], ident[:, :]).then_inc(xT_done, 1)

            def scores(i):
                eng.wait_ge(xT_out, i + 1)
                if i >= 2:
                    eng.wait_ge(mx_out, i - 1)
                ps = bank[2 + i % 2][:, 0:P]
                xa, xb = xT_sb[i % 2][:, 0:P], xT_sb[i % 2][KB:P, P:2 * P]
                eng.matmul(ps, xa, xa, start=True, stop=False)
                eng.matmul(ps, xb, xb, start=False, stop=True).then_inc(s_done, 1)

            def eT(i):
                eng.wait_ge(exp_out, i + 1)
                if i >= 2:
                    eng.wait_ge(eT_out, i - 1)
                eng.transpose(bank[4 + i % 2][:, 0:P], Ex[i % 2], ident[:, :]).then_inc(eT_done, 1)

            def mix(i):
                eng.wait_ge(eT_out, i + 1)
                if i >= 2:
                    eng.wait_ge(h_out, i - 1)
                eng.matmul(bank[6 + i % 2][:, 0:D], ExT[i % 2], xs[:, i, :], start=True, stop=True).then_inc(o_done, 1)

            for j in range(NT + 3):
                if j < NT:
                    xT(j)
                if 0 <= j - 1 < NT:
                    scores(j - 1)
                if 0 <= j - 2 < NT:
                    eT(j - 2)
                if 0 <= j - 3 < NT:
                    mix(j - 3)

            def xnT(i):
                eng.wait_ge(xn_out, i + 1)
                if i >= 2:
                    eng.wait_ge(xnT_out, i - 1)
                eng.transpose(bank[i % 2][:, 0:P], xs[:, i, 0:P], ident[:, :])
                eng.transpose(bank[i % 2][:, P:2 * P], xs[:, i, KB:D], ident[:, :]).then_inc(xnT_done, 1)

            def down(g):
                eng.wait_ge(xnT_out, 4 * (g + 1))
                if g == 0:
                    eng.wait_ge(w_in, 16 * NW)
                if g >= 2:
                    eng.wait_ge(far_out, g - 1)
                if g >= 1:
                    eng.wait_ge(hT_out, 2 * g)
                tiles = slice(4 * g, 4 * g + 4)
                for m, (a, b) in enumerate(((0, P), (P, D))):
                    ps = bank[2 + m][0:b - a, :]
                    eng.matmul(ps, Wd[0][:, a:b], xnTs[:, tiles, 0, :], start=True, stop=False)
                    eng.matmul(ps, Wd[1][:, a:b], xnTs[KB:P, tiles, 1, :], start=False, stop=True).then_inc(hd_done, 1)

            for g in range(NG):
                for i in range(4 * g, 4 * g + 4):
                    xnT(i)
                if g == 1 or g == 2:
                    down(g - 1)

            eng.wait_ge(rt_prep, 5)
            eng.transpose(bank[6][0:DR, 0:E], emb[:, 0:DR], ident[0:E, 0:E]).then_inc(prep_mm, 1)

            def router():
                eng.wait_ge(rt_prep, 6)
                for k in range(2):
                    ch = slice(KB * k, KB * k + P)
                    o = NR * k
                    eng.matmul(bank[7][:, o:o + E], rw[:, ch], ident[0:E, 0:E], start=True, stop=False, skip_group_check=True)
                    eng.matmul(bank[7][:, o:o + E], ones8[:, :], dg8[:, :], start=False, stop=True, skip_group_check=True)
                    eng.matmul(bank[7][:, o + E:o + 2 * E], pw[:, ch], enT[:, :], start=True, stop=True, skip_group_check=True)
                    eng.matmul(bank[7][:, o + 2 * E:o + NR], pw[:, ch], ident[0:DR, 0:DR], start=True, stop=True,
                               skip_group_check=True).then_inc(prep_mm, 1)

            def kq(n):
                g, h = divmod(n, H)
                eng.wait_ge(hT_out, 2 * (g + 1))
                if n >= 2:
                    eng.wait_ge(k_out, n - 1)
                    eng.wait_ge(q_out, n - 1)
                cols = slice(512 * g, 512 * (g + 1))
                ps = bank[4 + n % 2]
                eng.matmul(ps[:, :], Wkq[0][:, h, :, :].rearrange("p c e -> p (c e)"), hTa[:, cols], start=True, stop=False)
                eng.matmul(ps[:, :], Wkq[1][:, h, :, :].rearrange("p c e -> p (c e)"), hTb[0:KB, cols], start=False, stop=True).then_inc(kq_done, 1)

            def qv(i):
                if i == 0:
                    eng.wait_ge(wprep, 4)
                if i >= 2:
                    eng.wait_ge(qt_out, i - 1)
                    eng.wait_ge(vk_out, i - 1)
                cols = slice(P * i, P * (i + 1))
                ps = bank[6 + i % 2][:, 0:NQV]
                eng.matmul(ps, hTa[:, cols], Wqv[0], start=True, stop=False)
                eng.matmul(ps, hTb[:, cols], Wqv[1], start=False, stop=True).then_inc(qv_done, 1)

            def grams(m):
                g, n = divmod(m, NGR)
                ps = bank[m % 2]
                if m == 0:
                    eng.wait_ge(xnT_out, NT)
                if m >= 2:
                    eng.wait_ge(qm_out, m - 1)
                for j in range(4):
                    row = gram_row(m) + j
                    mm = eng.matmul(ps[0:S, P * j:P * (j + 1)], kqm[0:HD, row, 0, :],
                                    kqm[0:HD, row, :, :].rearrange("p c t -> p (c t)"), start=True, stop=True)
                mm.then_inc(gram_done, 1)

            def far(J, first, last):
                K = HD + BLK * max(0, J - 1)
                for j in range(first, last):
                    b, h = divmod(j, H)
                    row = 32 * h + b
                    if j % 24 == 0 and J >= 1:
                        eng.wait_ge(far_out, 4 * (J - 1) + j // 24 + 1 if J > 1 else 4)
                    far_bank = bank[2 + b // 8 % 2 if J == 0 else 4 + b // 8]
                    mm = eng.matmul(far_bank[32 * h:32 * h + 32, HD * (b % 8):HD * (b % 8 + 1)],
                                    kqm[0:K, row, 0:2, :].rearrange("p c t -> p (c t)")[:, BLK * J:BLK * J + 32],
                                    gw[0:K, row, :], start=True, stop=True)
                    if j % 24 == 23:
                        mm.then_inc(far_done, 1)

            idr = ident[0:R, 0:R]

            def add_far(a):
                eng.wait_ge(a_in[a % BLK], 16 * (a // BLK + 1))
                return eng.matmul(bank[a // BLK % 2][0:R, HD * (a % BLK):HD * (a % BLK + 1)], idr,
                                  ablk[a // BLK % 2][:, HD * (a % BLK):HD * (a % BLK + 1)],
                                  start=False, stop=False, skip_group_check=True)

            FAR = [0, 24, 48, 72, R, R, R, R, R]

            def open_z(J):
                eng.matmul(bank[J % 2][0:R, :], idr, b0r[:, :].unsqueeze(1).broadcast_to([R, BLK, HD]),
                           start=True, stop=False, skip_group_check=True)

            for g in range(NG):
                for h in range(H):
                    kq(H * g + h)
                if g == 0:
                    router()
                    eng.wait_ge(rt_prep, 7)
                for i in range(4 * g, 4 * g + 4):
                    qv(i)
                eng.wait_ge(k_out, H * (g + 1))
                eng.wait_ge(q_out, H * (g + 1))
                if g == 0:
                    eng.wait_ge(gw_rep, 3)
                eng.wait_ge(hT_out, min(2 * NG, 2 * g + 4))
                if g >= 2:
                    eng.wait_ge(far_out, g - 1)
                far(0, 24 * g, 24 * (g + 1))
                if g == NG - 1:
                    eng.wait_ge(vk_out, NT)
                    eng.transpose(bank[4][0:H * NT, 0:P], etal[:, :, :].rearrange("p h i -> p (h i)"), ident[:, :]).then_inc(eta_done, 1)
                for m in range(NGR * g, NGR * (g + 1)):
                    grams(m)
                if g + 2 < NG:
                    down(g + 2)
            eng.wait_ge(b0_out, 3)
            eng.wait_ge(eta_out, 1)
            eng.wait_ge(gw_rep, 5)
            eng.wait_ge(km_out, R // 4)
            eng.wait_ge(qm_out, R // 4)
            open_z(0)
            for t in range(BLK):
                eng.wait_ge(a_in[t], 16)
            eng.matmul(bank[0][0:R, :], idr, ablk[0], start=False, stop=False, skip_group_check=True).then_inc(grp_done, 1)
            open_z(1)
            for t in range(S - 2):
                J, i = divmod(t, BLK)
                n = max(0, BLK - (i + 2))
                a = t + 2
                if n:
                    eng.wait_ge(pr_out, grp_count(t) - 1)
                    mm = eng.matmul(bank[J % 2][0:R, HD * (i + 2):], ident[:, 0:R], PR[t % 2][:, 0:n, :],
                                    start=False, stop=False, skip_group_check=True)
                    if J >= 1:
                        mm = add_far(a)
                    mm.then_inc(grp_done, 1)
                if J < NB - 1:
                    first = max(0, i + 2 - BLK)
                    if i == BLK - 1:
                        eng.wait_ge(u_out, t + 2)
                    eng.wait_ge(prb_out, t + 1)
                    mm = eng.matmul(bank[(J + 1) % 2][0:R, HD * first:], ident[:, 0:R], PR[t % 2][:, BLK - 2:2 * BLK - 2 - first, :],
                                    start=False, stop=False, skip_group_check=True)
                    if not n:
                        mm = add_far(a)
                    mm.then_inc(nxt_done, 1)
                    if i == BLK - 1 and J + 2 < NB:
                        open_z(J + 2)
                    if i == 0 and J == 0:
                        eng.wait_ge(qm_out, R // 4)
                    if i == 0 and J >= 1:
                        for k in range(4):
                            eng.wait_ge(g_in[k], 16 * (BLK * J // 4))
                    far(J + 1, FAR[i], FAR[i + 1])

            def zq(i):
                if i == 0:
                    for k in range(4):
                        eng.wait_ge(g_in[k], 16 * S // 4)
                    eng.wait_ge(u_out, S)
                if i >= 2:
                    eng.wait_ge(zs_out, i - 1)
                for b2 in range(2):
                    for h in range(H):
                        row = 32 * h + 2 * i + b2
                        mm = eng.matmul(bank[i % 2][S * b2:S * (b2 + 1), HD * h:HD * (h + 1)], kqm[:, row, 1, :], gw[:, row, :],
                                        start=True, stop=True)
                mm.then_inc(zq_done, 1)

            def bias(k, w, c):
                eng.matmul(bank[6][0:1, D * k:D * (k + 1)], gcol[:, 0, c:c + 1], w[0], start=True, stop=False)
                return eng.matmul(bank[6][0:1, D * k:D * (k + 1)], gcol[0:KB, 1, c:c + 1], w[1][0:KB, :], start=False, stop=True)

            zq(0)
            for j in range(NT + 9):
                if j + 1 < NT:
                    zq(j + 1)
                if j == 1:
                    eng.wait_ge(post_w, 16 * 5)
                    bias(0, Wo, 1)
                    bias(1, Wu, 3).then_inc(prep_mm, 1)
                i = j - 4
                if 0 <= i < NT:
                    if i == 0:
                        eng.wait_ge(wg_out, 4)
                        eng.wait_ge(post_w, 16 * 7)
                    eng.wait_ge(t1_out, i + 1)
                    if i >= 2:
                        eng.wait_ge(tn_out, i - 1)
                    ps = bank[2 + 2 * (i % 2)][:, 0:D]
                    eng.matmul(ps, tT1[i % 2][:, 0:P], Wo[0], start=True, stop=False)
                    eng.matmul(ps, tT1[i % 2][0:KB + 1, P:2 * P], Wo[1], start=False, stop=True).then_inc(wo_done, 1)
                i = j - 6
                if 0 <= i < NT:
                    eng.wait_ge(t2_out, i + 1)
                    if i >= 1:
                        eng.wait_ge(h2_out, i)
                    eng.matmul(bank[3][:, 0:D], tT2[i % 2][:, 0:P], Wu[0], start=True, stop=False)
                    eng.matmul(bank[3][:, 0:D], tT2[i % 2][0:KB + 1, P:2 * P], Wu[1], start=False, stop=True).then_inc(up_done, 1)
                i = j - 8
                if 0 <= i < NT:
                    eng.wait_ge(t3_out, i + 1)
                    eng.matmul(bank[7][:, 2 * P:2 * P + NR], tT3[i % 2][:, 0:P], Wr[:, 0, :], start=True, stop=False)
                    eng.matmul(bank[7][:, 2 * P:2 * P + NR], tT3[i % 2][KB:P, P:2 * P], Wr[KB:P, 1, :], start=False, stop=True).then_inc(rt_done, 1)
                i = j - 3
                if 0 <= i < NT:
                    if i == 0:
                        eng.wait_ge(b0t_out, 4)
                    eng.wait_ge(yn_out, i + 1)
                    if i >= 1:
                        eng.wait_ge(t1_out, i)
                    eng.transpose(bank[5][:, 0:P], ZS[i % 5][:, 0:P], ident[:, :])
                    eng.transpose(bank[5][0:KB + 1, P:2 * P], ZS[i % 5][:, P:D + 1], ident[:, :]).then_inc(t1_done, 1)
                i = j - 5
                if 0 <= i < NT:
                    eng.wait_ge(tn_out, i + 1)
                    eng.wait_ge(pb_out, 1)
                    if i >= 1:
                        eng.wait_ge(t2_out, i)
                    eng.transpose(bank[6][:, 0:P], TN[i % 2][:, 0:P], ident[:, :])
                    eng.transpose(bank[6][0:KB + 1, P:2 * P], TN[i % 2][:, P:D + 1], ident[:, :]).then_inc(t2_done, 1)
                i = j - 7
                if 0 <= i < NT:
                    eng.wait_ge(xn2_out, i + 1)
                    if i >= 1:
                        eng.wait_ge(lg_out, i)
                    eng.transpose(bank[7][:, 0:P], XN[i % 3][:, 0:P], ident[:, :])
                    eng.transpose(bank[7][:, P:2 * P], XN[i % 3][:, KB:D], ident[:, :]).then_inc(t3_done, 1)

            eng.wait_ge(rc_out, RC)
            eng.wait_ge(rt_dve, RT["counts"])
            eng.matmul(bank[0][:, 0:E], ones_b, cnt, start=True, stop=True).then_inc(rt_pe, 1)
            eng.matmul(bank[1][:, 0:NI], tri_b, oha.rearrange("p i e -> p (i e)"), start=True, stop=False, skip_group_check=True)
            for i in range(NT - 1):
                n = NT - 1 - i
                mm = eng.matmul(bank[1][:, E * (i + 1):NI], ones_b, oha[:, i, :].unsqueeze(1).broadcast_to([P, n, E]),
                                start=False, stop=i == NT - 2, skip_group_check=True)
            mm.then_inc(rt_pe, 1)
            eng.wait_ge(rt_pool, 3)
            eng.wait_ge(rt_act, 3)
            for j in range(2 * NT):
                if j % 8 == 0:
                    eng.wait_ge(rt_dve, RT["place onehot 0"] + j // 8)
                mm = eng.matmul(bank[2][:, 0:5 * SLOTS], Bh[:, j, :], av[:, j, :, :],
                                start=j == 0, stop=j == 2 * NT - 1)
            mm.then_inc(rt_pe, 1)

            eng.wait_ge(idx_out, 1)
            eng.wait_ge(w_acc, 16 * 32)

            def x_T(s, k, g):
                eng.wait_ge(xg_in[k], 16 * (g + 1))
                eng.transpose(bank[4][:, 0:P], XG[k][:, 0:P], ident[:, :])
                eng.transpose(bank[4][:, P:2 * P], XG[k][:, P:2 * P], ident[:, :]).then_inc(xgT_done, 1)

            def layer1(s, k):
                if not (isinstance(s, int) and s == 0):
                    eng.wait_ge(relu_out, 2 * s)
                eng.wait_ge(w1_copied, s + 1)
                eng.wait_ge(xgT_out, s + 1)
                for c in range(KH):
                    ps = bank[c // 3][:, P * (c % 3):P * (c % 3 + 1)]
                    eng.matmul(ps, W1S[k % 2][:, 0, P * c:P * (c + 1)], xgT[:, 0:P], start=True, stop=False)
                    mm = eng.matmul(ps, W1S[k % 2][:, 1, P * c:P * (c + 1)], xgT[:, P:2 * P], start=False, stop=True)
                    if c % 3 == 2:
                        mm.then_inc(l1_done, 1)

            def layer2(s):
                e = eng.value_load(ex[0:1, ds(s, 1)], min_val=0, max_val=E - 1)
                if not (isinstance(s, int) and s == 0):
                    eng.wait_ge(yb_out, s)
                eng.wait_ge(hid_out, 2 * s + 2)
                for c in range(KH):
                    mm = eng.matmul(bank[7][:, 0:D], HT2[:, P * c:P * (c + 1)], W2[:, ds(e * (KH * D) + D * c, D)],
                                    start=c == 0, stop=c == KH - 1)
                mm.then_inc(l2_done, 1)

            def slots(g, first, last):
                for k in range(SLOTS - 4 * LASTG if last else 4):
                    s = 4 * g + k
                    layer1(s, k)
                    if not (last and s == SLOTS - 1):
                        x_T(s + 1, (k + 1) % 4, g + (k + 1) // 4)
                    if not (first and k == 0):
                        layer2(s - 1)

            x_T(0, 0, 0)
            slots(0, True, False)
            with eng.Fori(1, LASTG) as g:
                slots(g, False, False)
            slots(LASTG, False, True)
            layer2(SLOTS - 1)

        @block.scalar
        def _(eng):
            for j in range(NT + 3):
                if j < NT:
                    eng.wait_ge(xT_done, j + 1)
                    if j >= 2:
                        eng.wait_ge(s_done, j - 1)
                    eng.activation(xT_sb[j % 2], bank[j % 2][:, 0:2 * P], ACT.Copy).then_inc(xT_out, 1)
                if 0 <= j - 1 < NT:
                    i = j - 1
                    eng.wait_ge(negm_out, i + 1)
                    if i >= 2:
                        eng.wait_ge(eT_done, i - 1)
                    eng.activation(Ex[i % 2], Sm[i % 2], ACT.Exp, bias=negm[:, i:i + 1], scale=SC,
                                   accum_out=esum[:, i:i + 1]).then_inc(exp_out, 1)
                if 0 <= j - 2 < NT:
                    i = j - 2
                    eng.wait_ge(eT_done, i + 1)
                    if i >= 2:
                        eng.wait_ge(o_done, i - 1)
                    eng.activation(ExT[i % 2], bank[4 + i % 2][:, 0:P], ACT.Copy).then_inc(eT_out, 1)
            eng.wait_ge(stat_b, NT)
            eng.activation(std0[:, :], mv[:, :, 1], ACT.Sqrt, bias=epsc[:, 0:1]).then_inc(std_out, 1)
            eng.wait_ge(rt_prep, 1)
            eng.activation(emb[:, DR + 1:DR + 2], emb[:, DR:DR + 1], ACT.Sqrt).then_inc(std_out, 1)
            def silu(g):
                cols = slice(512 * g, 512 * (g + 1))
                eng.wait_ge(hd_done, 2 * g + 2)
                eng.activation(hTa[:, cols], bank[2][:, :], ACT.Silu, bias=bdc[:, 0:1]).then_inc(hT_out, 1)
                eng.activation(hTb[0:KB, cols], bank[3][0:KB, :], ACT.Silu, bias=bdc[0:KB, 1:2]).then_inc(hT_out, 1)

            for g in range(NG):
                for i in range(4 * g, 4 * g + 4):
                    eng.wait_ge(xnT_done, i + 1)
                    eng.activation(xnTs[:, i, :, :], bank[i % 2][:, 0:2 * P].rearrange("p (c t) -> p c t", c=2), ACT.Copy).then_inc(xnT_out, 1)
                if g == 1 or g == 2:
                    silu(g - 1)
            EVAC = [2, 3, 4, 5]

            def far_evac(J, k):
                eng.wait_ge(far_done, 4 * J + k + 1)
                if J >= 1:
                    for t in range(BLK):
                        eng.wait_ge(a_in[t], 16 * J)
                src = bank[2 + k % 2 if J == 0 else 4 + k]
                eng.activation(far_sb[:, 512 * k:512 * (k + 1)], src[0:R, :], ACT.Copy).then_inc(far_out, 1)

            for g in range(NG):
                for n in range(H * g, H * g + H):
                    h = n % H
                    eng.wait_ge(kq_done, n + 1)
                    eng.activation(kqm[0:HD, 32 * h + 8 * g:32 * h + 8 * g + 8, 0, :],
                                   bank[4 + n % 2][0:HD, :].rearrange("p (r t) -> p r t", t=S), ACT.Copy).then_inc(k_out, 1)
                for i in range(4 * g, 4 * g + 4):
                    eng.wait_ge(qv_done, i + 1)
                    if i >= 4:
                        eng.wait_ge(q_st[i % 4], 16 * (i // 4))
                    eng.activation(qst[:, i % 4, :], bank[6 + i % 2][:, 0:D], ACT.Copy).then_inc(qt_out, 1)
                far_evac(0, g)
                if g == NG - 1:
                    eng.wait_ge(eta_done, 1)
                    eng.activation(etaT, bank[4][0:H * NT, 0:P], ACT.Sigmoid).then_inc(eta_out, 1)
                for m in range(NGR * g, NGR * (g + 1)):
                    row = gram_row(m)
                    eng.wait_ge(gram_done, m + 1)
                    eng.activation(kqm[HD:P, row:row + 4, 0, :],
                                   bank[m % 2][0:S, :].rearrange("p (r c t) -> p r c t", c=2, t=S)[:, :, 0, :],
                                   ACT.Copy, scale=-1.0, bias=-1.0).then_inc(km_out, 1)
                if g + 2 < NG:
                    silu(g + 2)
            HH = HID // 2
            pieces = []
            for e in range(E):
                for m in range(2):
                    pieces.append((W1A[:, HID * e + HH * m:HID * e + HH * (m + 1)], mg[:, 0, e:e + 1], w1_in))
                for m in range(2):
                    pieces.append((W1B[0:KB, HID * e + HH * m:HID * e + HH * (m + 1)], mg[0:KB, 0, e:e + 1], w1_in))
            for e in range(E):
                for m in range(3):
                    o = KH * D * e + 2 * D * m
                    pieces.append((W2[:, o:o + 2 * D], mg[:, 1, e:e + 1], w2_in))
            eng.wait_ge(rt_in, 16 * 17)

            for t in range(S):
                J, i = divmod(t, BLK)
                eng.wait_ge(u_out, t + 1)
                if t >= 1:
                    eng.wait_ge(m2_out, t)
                eng.activation(UC[:, :], U[:, t % 2, :], ACT.Identity, scale=-float(HD), bias=usum[:, t % 2:t % 2 + 1]).then_inc(uc_out, 1)
                eng.wait_ge(rr_out, t + 1)
                eng.activation(sc[:, 2 + t % 2:3 + t % 2], sc[:, 1:2], ACT.Sqrt).then_inc(r_out, 1)
                if J < NB - 1 and i in EVAC:
                    far_evac(J + 1, EVAC.index(i))
                if t < len(pieces):
                    w, m, ready = pieces[t]
                    eng.wait_ge(ready, 16 * E)
                    eng.activation(w, w, ACT.Copy, scale=m).then_inc(w_sc, 1)
                eng.wait_ge(m2_out, t + 1)
                eng.wait_ge(my_out, 2 * (t + 1))
                if t >= 4:
                    eng.wait_ge(g_in[t % 4], 16 * (t // 4))
                eng.activation(Gst[:, t % 4, :], M2[:, t % 2, :], ACT.Copy, scale=y1[:, t % 2:t % 2 + 1]).then_inc(g_out, 1)

            def sd(ready, n, k, i, eps, done):
                eng.wait_ge(ready, i + 1)
                eng.activation(mvs[:, k, i % 3, 2:3], mvs[:, k, i % 3, 1:2], ACT.Sqrt, bias=epsc[:, eps:eps + 1]).then_inc(done, 1)

            for j in range(NT + 9):
                if j < NT:
                    eng.wait_ge(zs_out, j + 1)
                    for h in range(H):
                        eng.activation(SQ[j % 2][:, HD * h:HD * (h + 1)], ZS[j % 5][:, HD * h:HD * (h + 1)], ACT.Square, scale=HD ** -0.5,
                                       accum_out=rz[:, j % 3, h:h + 1]).then_inc(sq_out, 1)
                    eng.wait_ge(sq_out, H * (j + 1))
                    eng.activation(rz[:, j % 3, H:2 * H], rz[:, j % 3, 0:H], ACT.Sqrt, bias=epsc[:, 1:2]).then_inc(sqz_out, 1)
                if j == 1:
                    eng.wait_ge(prep_mm, 4)
                    eng.activation(bias_rows, bank[6][0:1, 0:2 * D], ACT.Copy).then_inc(pb_out, 1)
                    for w, c in ((Wo, 0), (Wu, 2)):
                        eng.activation(w[0], w[0], ACT.Copy, scale=gcol[:, 0, c:c + 1]).then_inc(wg_out, 1)
                        eng.activation(w[1][0:KB, :], w[1][0:KB, :], ACT.Copy, scale=gcol[0:KB, 1, c:c + 1]).then_inc(wg_out, 1)
                i = j - 8
                if 0 <= i < NT:
                    eng.wait_ge(rt_done, i + 1)
                    eng.activation(psq, bank[7][:, 2 * P + 2 * E:2 * P + NR], ACT.Square, accum_out=nrm[:, 0, i:i + 1])
                    eng.activation(LG[:, i, :], bank[7][:, 2 * P:2 * P + NR], ACT.Copy).then_inc(lg_out, 1)
                i = j - 3
                if 0 <= i < NT:
                    eng.wait_ge(t1_done, i + 1)
                    if i >= 2:
                        eng.wait_ge(wo_done, i - 1)
                    eng.activation(tT1[i % 2][:, 0:P], bank[5][:, 0:P], ACT.Copy)
                    eng.activation(tT1[i % 2][0:KB + 1, P:2 * P], bank[5][0:KB + 1, P:2 * P], ACT.Copy).then_inc(t1_out, 1)
                i = j - 5
                if 0 <= i < NT:
                    eng.wait_ge(t2_done, i + 1)
                    if i >= 2:
                        eng.wait_ge(up_done, i - 1)
                    eng.activation(tT2[i % 2][:, 0:P], bank[6][:, 0:P], ACT.Copy)
                    eng.activation(tT2[i % 2][0:KB + 1, P:2 * P], bank[6][0:KB + 1, P:2 * P], ACT.Copy).then_inc(t2_out, 1)
                i = j - 7
                if 0 <= i < NT:
                    eng.wait_ge(t3_done, i + 1)
                    if i >= 2:
                        eng.wait_ge(rt_done, i - 1)
                    eng.activation(tT3[i % 2], bank[7][:, 0:2 * P], ACT.Copy).then_inc(t3_out, 1)
                if 0 <= j - 2 < NT:
                    sd(st_y, 0, 0, j - 2, 1, sd_y)
                if 0 <= j - 4 < NT:
                    sd(st_t, 0, 1, j - 4, 1, sd_t)
                if 0 <= j - 6 < NT:
                    sd(st_h, 0, 2, j - 6, 0, sd_h)

            eng.wait_ge(lg_out, NT)
            eng.activation(nrm[:, 1, :], nrm[:, 0, :], ACT.Sqrt).then_inc(rt_act, 1)
            eng.wait_ge(rt_dve, RT["gap"])
            eng.activation(gt[:, 2, :], gt[:, 3, :], ACT.Exp).then_inc(rt_act, 1)
            eng.wait_ge(rt_dve, RT["slot onehot"])
            eng.activation(av[:, :, 1, :], Aoh, ACT.Copy, scale=p1).then_inc(rt_act, 1)

            def x_out(s):
                eng.wait_ge(xgT_done, s + 1)
                if not (isinstance(s, int) and s == 0):
                    eng.wait_ge(l1_done, 2 * s)
                eng.activation(xgT, bank[4][:, 0:2 * P], ACT.Copy).then_inc(xgT_out, 1)

            def square(s):
                if not (isinstance(s, int) and s == 0):
                    eng.wait_ge(l2_done, s)
                for m in range(2):
                    eng.wait_ge(relu_out, 2 * s + m + 1)
                    eng.activation(HT2[:, HH * m:HH * (m + 1)], RL[:, HH * m:HH * (m + 1)], ACT.Square).then_inc(hid_out, 1)

            x_out(0)
            x_out(1)
            square(0)
            with eng.Fori(1, SLOTS - 1) as s:
                x_out(s + 1)
                square(s)
            square(SLOTS - 1)


        @block.vector
        def _(eng):
            for c in range(4):
                eng.memset(X[:, 4 * D * c:4 * D * (c + 1)], 0.0).then_inc(x_zero, 1)
            eng.memset(epsc[:, 1:2], 1e-6)
            eng.memset(epsc[:, 0:1], 1e-5).then_inc(wprep, 1)
            eng.memset(hTb[KB:KB + 1, :], 1.0).then_inc(wprep, 1)
            eng.memset(Wqv[1][KB:KB + 1, :], 0.0).then_inc(wprep, 1)
            for j in range(NT + 3):
                if 0 <= j - 1 < NT:
                    i = j - 1
                    eng.wait_ge(s_done, i + 1)
                    if i >= 2:
                        eng.wait_ge(exp_out, i - 1)
                    if i == 0:
                        eng.wait_ge(consts, CONSTS)
                    eng.tensor_tensor_reduce(Sm[i % 2], bank[2 + i % 2][:, 0:P], maskbd[:, :], 1.0, -3e38,
                                             ALU.add, ALU.max, rowm[:, i:i + 1]).then_inc(mx_out, 1)
                    eng.wait_ge(mx_out, i + 1)
                    eng.tensor_scalar(negm[:, i:i + 1], rowm[:, i:i + 1], -SC, None, ALU.mult).then_inc(negm_out, 1)
                if 0 <= j - 2 < NT:
                    i = j - 2
                    eng.wait_ge(exp_out, i + 1)
                    eng.reciprocal(rinv[:, i:i + 1], esum[:, i:i + 1]).then_inc(rinv_out, 1)
                if 0 <= j - 3 < NT:
                    i = j - 3
                    eng.wait_ge(o_done, i + 1)
                    eng.wait_ge(rinv_out, i + 1)
                    eng.tensor_scalar(hmix[:, i, :], bank[6 + i % 2][:, 0:D], rinv[:, i:i + 1], None, ALU.mult).then_inc(h_out, 1)
                    eng.wait_ge(h_out, i + 1)
                    eng.bn_stats(st6[:, i % 2, :], hmix[:, i, :]).then_inc(stat_a, 1)
                    eng.wait_ge(stat_a, i + 1)
                    eng.bn_aggr(mv[:, i, :], st6[:, i % 2, :]).then_inc(stat_b, 1)
            eng.wait_ge(rows_in, 16 * 7)
            eng.tensor_reduce(w0m[:, :], w0h[:, :, :], AX.X, ALU.add).then_inc(w0_out, 1)
            eng.tensor_reduce(b0m[:, 0:1], b0r[:, :], AX.X, ALU.add).then_inc(b0_out, 1)
            eng.tensor_tensor(g2r[:, :], g2r[:, :], g2r[:, :], ALU.mult)
            eng.wait_ge(w0_out, 1)
            eng.tensor_scalar(w0m[:, :], w0m[:, :], -1.0 / HD, None, ALU.mult).then_inc(w0_out, 1)
            eng.wait_ge(b0_out, 1)
            eng.tensor_scalar(b0m[:, 1:2], b0m[:, 0:1], -1.0 / HD, None, ALU.mult).then_inc(b0_out, 1)
            eng.wait_ge(w0_out, 2)
            eng.tensor_tensor(w0h[:, :, :], w0h[:, :, :], w0m[:, :].unsqueeze(2).broadcast_to([HD, H, HD]), ALU.add).then_inc(w0_out, 1)
            eng.wait_ge(b0_out, 2)
            eng.tensor_scalar(b0r[:, :], b0r[:, :], b0m[:, 1:2], None, ALU.add).then_inc(b0_out, 1)
            eng.wait_ge(rt_in, 16 * 17)
            eng.tensor_tensor_reduce(dgj[:, :], emb[:, 0:DR], emb[:, 0:DR], 1.0, 0.0, ALU.mult, ALU.add, emb[:, DR:DR + 1]).then_inc(rt_prep, 1)
            eng.wait_ge(std_out, 1)
            eng.reciprocal(rstd0[:, :], std0[:, :]).then_inc(rstd_out, 1)
            eng.wait_ge(rstd_out, 1)
            for i in range(NT):
                eng.tensor_scalar(xs[:, i, :], hmix[:, i, :], mv[:, i, 0:1], rstd0[:, i:i + 1],
                                  ALU.subtract, ALU.mult).then_inc(xn_out, 1)
            eng.wait_ge(rt_in, 16 * 17)
            eng.tensor_scalar(fat[:, :], fat[:, :], -0.1, None, ALU.mult).then_inc(eb_out, 1)
            eng.wait_ge(eb_out, 1)
            eng.scalar_tensor_tensor(ebias[:, :], ebias[:, :], 0.1, fat[:, :], ALU.mult, ALU.add).then_inc(eb_out, 1)
            eng.wait_ge(std_out, 2)
            eng.tensor_scalar(emb[:, DR + 2:DR + 3], emb[:, DR + 1:DR + 2], 0.02 / D, 0.02 / D, ALU.mult, ALU.add).then_inc(rt_prep, 1)
            eng.tensor_scalar(emb[:, DR + 3:DR + 4], emb[:, DR + 1:DR + 2], 1e-12, None, ALU.max).then_inc(rt_prep, 1)
            eng.memset(ones8[:, :], 1.0)
            eng.wait_ge(rt_prep, 3)
            eng.reciprocal(emb[:, DR + 3:DR + 4], emb[:, DR + 3:DR + 4]).then_inc(rt_prep, 1)
            eng.tensor_scalar(dg8[:, :], ident[0:E, 0:E], emb[:, DR + 2:DR + 3], None, ALU.mult)
            eng.wait_ge(rt_prep, 4)
            eng.tensor_scalar(emb[:, 0:DR], emb[:, 0:DR], emb[:, DR + 3:DR + 4], None, ALU.mult).then_inc(rt_prep, 1)
            eng.wait_ge(w_in, 16 * NW)
            for a, n in ((0, P), (1, KB)):
                w = Wqv[a][0:n, D:2 * D].rearrange("p (h e) -> p h e", h=H)
                ins = eng.tensor_tensor(w, w, Wkq[a][:, :, 0, :], ALU.subtract)
            ins.then_inc(wprep, 1)
            eng.wait_ge(prep_mm, 1)
            eng.tensor_copy(enT[:, :], bank[6][0:DR, 0:E]).then_inc(rt_prep, 1)
            for g in range(NG):
                for n in range(H * g, H * g + H):
                    h = n % H
                    eng.wait_ge(kq_done, n + 1)
                    eng.tensor_copy(kqm[0:HD, 32 * h + 8 * g:32 * h + 8 * g + 8, 1, :],
                                    bank[4 + n % 2][HD:P, :].rearrange("p (r t) -> p r t", t=S)).then_inc(q_out, 1)
                if g == 0:
                    eng.wait_ge(prep_mm, 3)
                    eng.tensor_copy(Wr[:, :, :].rearrange("p c n -> p (c n)"), bank[7][:, 0:2 * NR]).then_inc(rt_prep, 1)
                for i in range(4 * g, 4 * g + 4):
                    eng.wait_ge(qv_done, i + 1)
                    if i % 4 == 0:
                        eng.wait_ge(hd_done, 2 * (g + 1))
                    eng.wait_ge(qt_out, i + 1)
                    eng.tensor_copy(etal[:, :, i], bank[6 + i % 2][:, 2 * D:NQV])
                    eng.tensor_tensor(vk[:, i, :], btok[:, :], bank[6 + i % 2][:, D:2 * D], ALU.subtract).then_inc(vk_out, 1)
                for n in range(NGR):
                    m = NGR * g + n
                    row = gram_row(m)
                    eng.wait_ge(gram_done, m + 1)
                    eng.wait_ge(km_out, m + 1)
                    eng.scalar_tensor_tensor(kqm[HD:P, row:row + 4, 1, :],
                                             bank[m % 2][0:S, :].rearrange("p (r c t) -> p r c t", c=2, t=S)[:, :, 1, :],
                                             1.0, negc[:, :].unsqueeze(1).broadcast_to([S, 4, S]),
                                             ALU.add, ALU.mult).then_inc(qm_out, 1)
                    v = vk[:, 4 * g:4 * g + 4, :]
                    vh = v.rearrange("p i (h e) -> p (i h) e", h=H)
                    cm = cmean[:, 12 * g:12 * g + 12]
                    if n == 0:
                        eng.wait_ge(vk_out, 4 * g + 4)
                        eng.tensor_tensor(v, v, gtok[:, :].unsqueeze(1).broadcast_to([P, 4, D]), ALU.mult).then_inc(c_chain, 1)
                    elif n == 1:
                        eng.wait_ge(c_chain, 3 * g + 1)
                        eng.tensor_reduce(cm, vh, AX.X, ALU.add).then_inc(c_chain, 1)
                    elif n == 2:
                        eng.wait_ge(c_chain, 3 * g + 2)
                        eng.tensor_scalar(cm, cm, 1.0 / HD, None, ALU.mult).then_inc(c_chain, 1)
                    elif n == 4 and g == 0:
                        b0v = b0t[:, :].rearrange("p (h e) -> p h e", h=H)
                        eng.wait_ge(c_out, 1)
                        eng.tensor_reduce(cmean[:, 0:H], b0v, AX.X, ALU.add).then_inc(b0t_out, 1)
                        eng.wait_ge(b0t_out, 1)
                        eng.tensor_scalar(cmean[:, 0:H], cmean[:, 0:H], 1.0 / HD, None, ALU.mult).then_inc(b0t_out, 1)
                        eng.wait_ge(b0t_out, 2)
                        eng.tensor_tensor(b0v, b0v, cmean[:, 0:H].unsqueeze(2).broadcast_to([P, H, HD]), ALU.subtract).then_inc(b0t_out, 1)
                    elif n == 3:
                        eng.wait_ge(c_chain, 3 * g + 3)
                        eng.tensor_tensor(vh, vh, cm.unsqueeze(2).broadcast_to([P, 12, HD]), ALU.subtract).then_inc(c_out, 1)

            eng.wait_ge(eta_in, 16)
            eng.tensor_scalar(eta96[:, :], eta96[:, :], 1.0 / HD, None, ALU.mult).then_inc(mne_out, 1)
            eng.wait_ge(mne_out, 1)
            eng.wait_ge(mn_in, 16 * 2)
            HEAD = 2 * BLK
            eng.tensor_tensor(mn[:, 0:HEAD, :], mn[:, 0:HEAD, :], eta96[:, 0:HEAD].unsqueeze(2).broadcast_to([R, HEAD, 2 * BLK]), ALU.mult).then_inc(mne_out, 1)
            eng.wait_ge(mne_out, 2)
            eng.wait_ge(gw_rep, 5)
            eng.wait_ge(c_in, 16 * H * NG)

            def z_next(t):
                J, i = divmod(t, BLK)
                z = bank[J % 2][0:R, HD * i:HD * (i + 1)]
                if J >= 1 and i <= 1:
                    eng.wait_ge(nxt_done, t - 1)
                else:
                    eng.wait_ge(grp_done, grp_count(t - 2) if i >= 2 else 1)
                if t == 0:
                    eng.tensor_scalar(U[:, 0, :], z, 1.0, None, ALU.mult, ALU.add, accum_out=usum[:, 0:1]).then_inc(u_out, 1)
                    return
                ip = (t - 1) % BLK
                eng.wait_ge(m2_out, t)
                eng.scalar_tensor_tensor(U[:, t % 2, :], M2[:, (t - 1) % 2, :], MY[:, (t - 1) % 2, ip + 1:ip + 2], z,
                                         ALU.mult, ALU.add, accum_out=usum[:, t % 2:t % 2 + 1]).then_inc(u_out, 1)

            z_next(0)
            for t in range(S):
                J, i = divmod(t, BLK)
                u = U[:, t % 2, :]
                if t >= 1:
                    n = BLK - ((t - 1) % BLK + 2)
                    if n > 0:
                        if t >= 3 and (t - 3) % BLK < BLK - 2:
                            eng.wait_ge(grp_done, grp_count(t - 3))
                        j0 = (t - 1) % BLK + 2
                        eng.tensor_tensor(PR[(t - 1) % 2][0:R, 0:n, :],
                                          M2[:, (t - 1) % 2, :].unsqueeze(1).broadcast_to([R, n, HD]),
                                          MY[:, (t - 1) % 2, j0:j0 + n].unsqueeze(2).broadcast_to([R, n, HD]),
                                          ALU.mult).then_inc(pr_out, 1)
                eng.wait_ge(u_out, t + 1)
                eng.tensor_tensor_reduce(JK[:, :], u, u, 1.0 / HD, 1e-6, ALU.mult, ALU.add, sc[:, 0:1]).then_inc(v_step, 1)
                eng.wait_ge(v_step, 6 * t + 1)
                eng.reciprocal(sc[:, 1:2], sc[:, 0:1]).then_inc(rr_out, 1)
                eng.tensor_tensor_reduce(PG[:, :], u, g2r[:, :], 1.0, 0.0, ALU.mult, ALU.add, sc[:, 4:5]).then_inc(v_step, 1)
                eng.wait_ge(v_step, 6 * t + 2)
                eng.scalar_tensor_tensor(PC[:, :], sc[:, 4:5].broadcast_to([R, HD]), -1.0 / HD, PG[:, :],
                                         ALU.mult, ALU.add).then_inc(v_step, 1)
                eng.wait_ge(v_step, 6 * t + 3)
                eng.wait_ge(r_out, t + 1)
                r = sc[:, 2 + t % 2:3 + t % 2]
                eng.scalar_tensor_tensor(Wv_[:, :], PC[:, :], r, cc[:, t, :], ALU.mult, ALU.add).then_inc(v_step, 1)
                if t >= 2:
                    eng.wait_ge(g_out, t - 1)
                    if t - 2 < BLK * (NB - 1):
                        eng.wait_ge(prb_out, t - 1)
                if t == HEAD:
                    eng.wait_ge(mnb_out, 1)
                eng.tensor_tensor(MY[:, t % 2, :], mn[:, t, :], r.broadcast_to([R, 2 * BLK]), ALU.mult).then_inc(my_out, 1)
                eng.wait_ge(v_step, 6 * t + 4)
                eng.tensor_tensor_reduce(JK[:, :], Wv_[:, :], u, 1.0 / HD ** 2, 0.0, ALU.mult, ALU.add, sc[:, 5:6]).then_inc(v_step, 1)
                eng.tensor_tensor(y1[:, t % 2:t % 2 + 1], eta96[:, t:t + 1], r, ALU.mult).then_inc(my_out, 1)
                eng.wait_ge(v_step, 6 * t + 5)
                eng.tensor_tensor(sc[:, 6:7], sc[:, 5:6], sc[:, 1:2], ALU.mult).then_inc(v_step, 1)
                eng.wait_ge(v_step, 6 * t + 6)
                eng.wait_ge(uc_out, t + 1)
                eng.scalar_tensor_tensor(M2[:, t % 2, :], UC[:, :], sc[:, 6:7], Wv_[:, :], ALU.mult, ALU.add).then_inc(m2_out, 1)
                if t + 1 < S:
                    z_next(t + 1)

            eng.memset(one_col, 1.0).then_inc(b0t_out, 1)
            nri = 0
            nst = 0
            for j in range(NT + 9):
                if j < NT:
                    i = j
                    eng.wait_ge(zq_done, i + 1)
                    if i == 0:
                        eng.wait_ge(b0t_out, 3)
                    if i >= 5:
                        eng.wait_ge(t1_done, i - 4)
                    eng.tensor_tensor(ZS[i % 5][:, 0:D], bank[i % 2][:, 0:D], b0t[:, :], ALU.add).then_inc(zs_out, 1)
                if j == 2:
                    eng.wait_ge(pb_out, 1)
                    eng.tensor_tensor(bias_rows[:, D:2 * D], bias_rows[:, D:2 * D], bup, ALU.add).then_inc(pb_out, 1)
                for back, k, ready in ((3, 0, sd_y), (5, 1, sd_t), (1, None, sqz_out)):
                    i = j - back
                    if 0 <= i < NT:
                        eng.wait_ge(ready, i + 1)
                        if k is None:
                            eng.reciprocal(rz[:, i % 3, 0:H], rz[:, i % 3, H:2 * H]).then_inc(ri_out, 1)
                        else:
                            eng.reciprocal(mvs[:, k, i % 3, 3:4], mvs[:, k, i % 3, 2:3]).then_inc(ri_out, 1)
                        nri += 1
                if nri:
                    eng.wait_ge(ri_out, nri)
                i = j - 3
                if 0 <= i < NT:
                    eng.tensor_scalar(ZS[i % 5][:, 0:D], ZS[i % 5][:, 0:D], mvs[:, 0, i % 3, 0:1], mvs[:, 0, i % 3, 3:4],
                                      ALU.subtract, ALU.mult).then_inc(yn_out, 1)
                i = j - 5
                if 0 <= i < NT:
                    if i >= 2:
                        eng.wait_ge(t2_done, i - 1)
                    eng.tensor_scalar(TN[i % 2][:, 0:D], bank[2 + 2 * (i % 2)][:, 0:D], mvs[:, 1, i % 3, 0:1], mvs[:, 1, i % 3, 3:4],
                                      ALU.subtract, ALU.mult).then_inc(tn_out, 1)
                i = j - 7
                if 0 <= i < NT:
                    eng.wait_ge(sd_h, i + 1)
                    eng.reciprocal(mvs[:, 2, i % 3, 3:4], mvs[:, 2, i % 3, 2:3]).then_inc(ri_out, 1)
                    nri += 1
                i = j - 7
                if 0 <= i < NT:
                    eng.wait_ge(ri_out, nri)
                    if i >= 3:
                        eng.wait_ge(xn_st[i % 3], 16 * (i // 3))
                        eng.wait_ge(t3_done, i - 2)
                    eng.tensor_scalar(XN[i % 3], h2[:, i, :], mvs[:, 2, i % 3, 0:1], mvs[:, 2, i % 3, 3:4],
                                      ALU.subtract, ALU.mult).then_inc(xn2_out, 1)
                i = j - 4
                if 0 <= i < NT:
                    eng.wait_ge(wo_done, i + 1)
                    eng.bn_stats(s6[:, 1, :], bank[2 + 2 * (i % 2)][:, 0:D]).then_inc(st_a, 1)
                    nst += 1
                i = j - 6
                if 0 <= i < NT:
                    eng.wait_ge(up_done, i + 1)
                    if i == 0:
                        eng.wait_ge(h_in, 16)
                    eng.tensor_tensor(h2[:, i, :], bank[3][:, 0:D], h2[:, i, :], ALU.add).then_inc(h2_out, 1)
                i = j - 4
                if 0 <= i < NT:
                    eng.wait_ge(st_a, nst)
                    eng.bn_aggr(mvs[:, 1, i % 3, 0:2], s6[:, 1, :]).then_inc(st_t, 1)
                i = j - 6
                if 0 <= i < NT:
                    eng.wait_ge(h2_out, i + 1)
                    eng.bn_stats(s6[:, 2, :], h2[:, i, :]).then_inc(st_a, 1)
                    nst += 1
                i = j - 2
                if 0 <= i < NT:
                    eng.wait_ge(y_out, i + 1)
                    eng.bn_stats(s6[:, 0, :], ZS[i % 5][:, 0:D]).then_inc(st_a, 1)
                    nst += 1
                if nst:
                    eng.wait_ge(st_a, nst)
                i = j - 6
                if 0 <= i < NT:
                    eng.bn_aggr(mvs[:, 2, i % 3, 0:2], s6[:, 2, :]).then_inc(st_h, 1)
                i = j - 2
                if 0 <= i < NT:
                    eng.bn_aggr(mvs[:, 0, i % 3, 0:2], s6[:, 0, :]).then_inc(st_y, 1)

            def bc(t, n=E):
                return t.unsqueeze(2).broadcast_to([P, NT, n])

            w8b = w8.unsqueeze(1).broadcast_to([P, NT, E])
            eng.wait_ge(zq_done, NT)
            eng.wait_ge(lg_out, NT)
            eng.tensor_tensor(Lb, LG[:, :, 0:E], ebias[:, :].unsqueeze(1).broadcast_to([P, NT, E]), ALU.add).then_inc(rt_dve, 1)
            eng.wait_ge(rt_act, 1)
            eng.tensor_scalar(nrm[:, 2, :], nrm[:, 1, :], 1e-12, None, ALU.max).then_inc(rt_dve, 1)
            eng.wait_ge(rt_dve, RT["norm floor"])
            eng.reciprocal(nrm[:, 1, :], nrm[:, 2, :]).then_inc(rt_dve, 1)
            eng.wait_ge(rt_dve, RT["norm inverse"])
            eng.tensor_tensor(al8, LG[:, :, E:2 * E], bc(nrm[:, 1, :]), ALU.mult).then_inc(rt_dve, 1)
            eng.wait_ge(rt_dve, RT["align"])
            eng.scalar_tensor_tensor(Lg, al8, 0.02, Lb, ALU.mult, ALU.add).then_inc(rt_dve, 1)
            eng.wait_ge(rc_out, RC)
            eng.wait_ge(rt_dve, RT["logits"])
            eng.tensor_reduce(mx[:, 0, :], Lg, AX.X, ALU.max).then_inc(rt_dve, 1)
            eng.wait_ge(rt_dve, RT["max 1"])
            eng.tensor_tensor(eqt, Lg, bc(mx[:, 0, :]), ALU.is_equal).then_inc(rt_dve, 1)
            eng.wait_ge(rt_dve, RT["eq 1"])
            eng.tensor_tensor(sct, eqt, w8b, ALU.mult).then_inc(rt_dve, 1)
            eng.wait_ge(rt_dve, RT["tie 1"])
            eng.tensor_reduce(cs[:, 0, :], sct, AX.X, ALU.max).then_inc(rt_dve, 1)
            eng.wait_ge(rt_dve, RT["first 1"])
            eng.tensor_tensor(oh1, w8b, bc(cs[:, 0, :]), ALU.is_equal).then_inc(rt_dve, 1)
            eng.wait_ge(rt_dve, RT["onehot 1"])
            eng.scalar_tensor_tensor(L2t, oh1, -1e30, Lg, ALU.mult, ALU.add).then_inc(rt_dve, 1)
            eng.wait_ge(rt_dve, RT["rest"])
            eng.tensor_reduce(mx[:, 1, :], L2t, AX.X, ALU.max).then_inc(rt_dve, 1)
            eng.wait_ge(rt_dve, RT["max 2"])
            eng.tensor_tensor(eqt, L2t, bc(mx[:, 1, :]), ALU.is_equal).then_inc(rt_dve, 1)
            eng.tensor_tensor(gt[:, 3, :], mx[:, 1, :], mx[:, 0, :], ALU.subtract).then_inc(rt_dve, 1)
            eng.wait_ge(rt_dve, RT["eq 2"])
            eng.tensor_tensor(sct, eqt, w8b, ALU.mult).then_inc(rt_dve, 1)
            eng.wait_ge(rt_dve, RT["tie 2"])
            eng.tensor_reduce(cs[:, 1, :], sct, AX.X, ALU.max).then_inc(rt_dve, 1)
            eng.wait_ge(rt_dve, RT["first 2"])
            eng.tensor_tensor(oh2, w8b, bc(cs[:, 1, :]), ALU.is_equal).then_inc(rt_dve, 1)
            eng.wait_ge(rt_dve, RT["onehot 2"])
            eng.tensor_tensor(oha, oh1, oh2, ALU.add).then_inc(rt_dve, 1)
            eng.wait_ge(rt_dve, RT["both"])
            with nc.allow_low_precision("counts up to 16 are exact"):
                eng.tensor_reduce(cnt, oha.rearrange("p i e -> p e i"), AX.X, ALU.add).then_inc(rt_dve, 1)
            eng.wait_ge(rt_pe, 1)
            eng.tensor_tensor(tlm, bank[0][:, 0:E].unsqueeze(2).broadcast_to([P, E, NT]),
                              k128[:, 0:NT].unsqueeze(1).broadcast_to([P, E, NT]), ALU.is_gt).then_inc(rt_dve, 1)
            eng.wait_ge(rt_act, 2)
            eng.tensor_scalar(gt[:, 3, :], gt[:, 2, :], 1.0, None, ALU.add).then_inc(rt_dve, 1)
            eng.wait_ge(rt_dve, RT["slots of"])
            eng.tensor_reduce(tl, tlm, AX.X, ALU.add).then_inc(rt_dve, 1)
            eng.wait_ge(rt_dve, RT["gate sum"])
            eng.reciprocal(gt[:, 0, :], gt[:, 3, :]).then_inc(rt_dve, 1)
            eng.wait_ge(rt_dve, RT["slots"])
            eng.tensor_tensor(bmt, tl.unsqueeze(1).broadcast_to([P, E, E]), emask, ALU.mult).then_inc(rt_dve, 1)
            eng.wait_ge(rt_dve, RT["gate 1"])
            eng.tensor_tensor(gt[:, 1, :], gt[:, 2, :], gt[:, 0, :], ALU.mult).then_inc(rt_dve, 1)
            eng.wait_ge(rt_dve, RT["before"])
            eng.tensor_reduce(bs[:, 0:E], bmt, AX.X, ALU.add).then_inc(rt_dve, 1)
            eng.wait_ge(rt_dve, RT["gate 2"])
            g12 = gt[:, 0:2, :].rearrange("p c i -> p (c i)")
            eng.tensor_copy(gp[:, 0, :], g12).then_inc(rt_dve, 1)
            eng.wait_ge(rt_dve, RT["base"])
            eng.scalar_tensor_tensor(bs[:, E:2 * E], tl, float(P), bs[:, 0:E], ALU.mult, ALU.add).then_inc(rt_dve, 1)
            eng.wait_ge(rt_dve, RT["gate part 1"])
            eng.tensor_tensor(gr[:, 0, :], g12, gp[:, 0, :], ALU.subtract).then_inc(rt_dve, 1)
            eng.wait_ge(rt_pe, 2)
            eng.tensor_tensor(P8, bank[1][:, 0:NI].rearrange("p (i e) -> p i e", e=E),
                              bs[:, 0:E].unsqueeze(1).broadcast_to([P, NT, E]), ALU.add).then_inc(rt_dve, 1)
            eng.wait_ge(rt_dve, RT["gate rest 1"])
            eng.tensor_copy(gp[:, 1, :], gr[:, 0, :]).then_inc(rt_dve, 1)
            eng.wait_ge(rt_dve, RT["places"])
            eng.tensor_tensor(sct, oh1, P8, ALU.mult).then_inc(rt_dve, 1)
            eng.wait_ge(rt_dve, RT["of 1"])
            eng.tensor_reduce(pos[:, 0:NT], sct, AX.X, ALU.add).then_inc(rt_dve, 1)
            eng.tensor_tensor(scu, oh2, P8, ALU.mult).then_inc(rt_dve, 1)
            eng.tensor_tensor(gr[:, 1, :], gr[:, 0, :], gp[:, 1, :], ALU.subtract).then_inc(rt_dve, 1)
            eng.wait_ge(rt_dve, RT["of 2"])
            eng.tensor_reduce(pos[:, NT:2 * NT], scu, AX.X, ALU.add).then_inc(rt_dve, 1)
            eng.wait_ge(rt_dve, RT["gate rest 2"])
            eng.tensor_copy(gp[:, 2, :], gr[:, 1, :]).then_inc(rt_dve, 1)
            eng.wait_ge(rt_dve, RT["pos 2"])
            eng.tensor_scalar(slot_, pos, 1.0 / P, -(P - 1) / (2.0 * P), ALU.mult, ALU.add).then_inc(rt_dve, 1)
            eng.wait_ge(rt_dve, RT["slot scaled"])
            eng.tensor_scalar(slot_, slot_, 1.5 * 2 ** 23, 1.5 * 2 ** 23, ALU.add, ALU.subtract).then_inc(rt_dve, 1)
            eng.wait_ge(rt_dve, RT["slot"])
            eng.scalar_tensor_tensor(row_, slot_, -float(P), pos, ALU.mult, ALU.add).then_inc(rt_dve, 1)
            J2 = 2 * NT
            eng.tensor_tensor(Aoh, slot_.unsqueeze(2).broadcast_to([P, J2, SLOTS]),
                              ik.unsqueeze(1).broadcast_to([P, J2, SLOTS]), ALU.is_equal).then_inc(rt_dve, 1)
            eng.wait_ge(rt_dve, RT["slot onehot"])
            for v in range(2):
                eng.tensor_tensor(av[:, :, 2 + v, :], Aoh, gp[:, v, :].unsqueeze(2).broadcast_to([P, J2, SLOTS]),
                                  ALU.mult).then_inc(rt_dve, 1)
            for q in range(NQB):
                eng.tensor_tensor(Bh[:, 8 * q:8 * q + 8, :], irow.unsqueeze(1).broadcast_to([P, 8, P]),
                                  row_[:, 8 * q:8 * q + 8].unsqueeze(2).broadcast_to([P, 8, P]), ALU.is_equal).then_inc(rt_dve, 1)
            eng.tensor_tensor(exm, k128.unsqueeze(2).broadcast_to([P, SLOTS, E]),
                              bs[:, E:2 * E].unsqueeze(1).broadcast_to([P, SLOTS, E]), ALU.is_ge).then_inc(rt_dve, 1)
            eng.wait_ge(rt_dve, RT["ended"])
            eng.tensor_reduce(exf, exm, AX.X, ALU.add).then_inc(rt_dve, 1)
            eng.wait_ge(rt_dve, RT["expert"])
            eng.tensor_scalar(ex[:, :], exf, float(E - 1), None, ALU.min).then_inc(rt_dve, 1)
            eng.wait_ge(rt_pe, 3)
            eng.tensor_copy(lst, bank[2][:, 0:5 * SLOTS].rearrange("p (v k) -> p v k", k=SLOTS)).then_inc(rt_dve, 1)
            eng.wait_ge(rt_dve, RT["lists"])
            eng.tensor_tensor(tok1, lst[:, 0, :], lst[:, 1, :], ALU.add).then_inc(rt_dve, 1)
            eng.tensor_tensor(lst[:, 3, :], lst[:, 3, :], lst[:, 4, :], ALU.add).then_inc(rt_dve, 1)
            eng.wait_ge(rt_dve, RT["token"])
            eng.tensor_scalar(pad, tok1, 0.0, trash, ALU.is_equal, ALU.mult).then_inc(rt_dve, 1)
            eng.wait_ge(rt_dve, RT["gate low"])
            eng.tensor_tensor(gates[:, :], lst[:, 2, :], lst[:, 3, :], ALU.add).then_inc(rt_dve, 1)
            eng.wait_ge(rt_dve, RT["pad"])
            eng.scalar_tensor_tensor(idx[:, :], tok1, -1.0, pad, ALU.add, ALU.add).then_inc(idx_out, 1)
            eng.wait_ge(rt_dve, RT["gates"])

            def relu(s):
                for m in range(2):
                    eng.wait_ge(l1_done, 2 * s + m + 1)
                    if m == 0 and not (isinstance(s, int) and s == 0):
                        eng.wait_ge(hid_out, 2 * s)
                    eng.tensor_scalar(RL[:, HID // 2 * m:HID // 2 * (m + 1)], bank[m][:, 0:HID // 2], 0.0, None, ALU.max).then_inc(relu_out, 1)

            def w1_copy(s, k):
                e = eng.value_load(ex[0:1, ds(s, 1)], min_val=0, max_val=E - 1)
                eng.tensor_copy(W1S[k % 2], W1[:, :, ds(e * HID, HID)]).then_inc(w1_copied, 1)

            def y_evac(s, k, g):
                e = eng.value_load(ex[0:1, ds(s, 1)], min_val=0, max_val=E - 1)
                if not (isinstance(g, int) and g == 0):
                    eng.wait_ge(y_add, 64 * g)
                eng.wait_ge(l2_done, s + 1)
                eng.tensor_tensor(YO[k], bank[7][:, 0:D], b2r[:, ds(e * D, D)], ALU.add).then_inc(yb_out, 1)
                eng.wait_ge(yb_out, s + 1)
                eng.tensor_scalar(YO[k], YO[k], gates[:, ds(s, 1)], None, ALU.mult).then_inc(yo_out, 1)

            def results(g, last):
                for k in range(SLOTS - 4 * LASTG if last else 4):
                    s = 4 * g + k
                    if not (last and s == SLOTS - 1):
                        relu(s + 1)
                    if not (last and s + 3 >= SLOTS):
                        w1_copy(s + 3, k + 3)
                    y_evac(s, k, g)

            eng.wait_ge(idx_out, 1)
            eng.wait_ge(w_acc, 16 * 32)
            for k in range(3):
                eng.wait_ge(xn_st[k], 16 * len(range(k, NT, 3)))
            w1_copy(0, 0)
            w1_copy(1, 1)
            relu(0)
            w1_copy(2, 2)
            eng.wait_ge(b2_in, 16)
            results(0, False)
            with eng.Fori(1, LASTG) as g:
                results(g, False)
            results(LASTG, True)



def kernel(**inputs):
    import numpy as np
    import concourse.bacc as bacc
    from concourse.bass_utils import run_bass_kernel_spmd as run

    nc = bacc.Bacc("TRN2", target_bir_lowering=False, num_devices=1)
    arrays, io = {}, {}
    for name, a in inputs.items():
        a = np.ascontiguousarray(a)
        arrays["in_" + name] = a
        io[name] = nc.dram_tensor("in_" + name, a.shape, mybir.dt.from_np(a.dtype), kind="ExternalInput").ap()
    B, T, D = inputs["x"].shape
    out = nc.dram_tensor("out_0", (B, (T + 3) // 4 * 2, D), F32, kind="ExternalOutput").ap()
    audio_tower_kernel(nc, io, out)
    r = run(nc, [arrays], core_ids=[0])
    return r.results[0]["out_0"]
```
